# Optimizing a Trainium2 kernel written in Bass

```python
import numpy as np
import jax
import jax.numpy as jnp

def _softmax(x, axis=-1):
    return jax.nn.softmax(x, axis=axis)

def _gelu(x):
    return jax.nn.gelu(x, approximate=True)

def _silu(x):
    return jax.nn.silu(x)

def _sigmoid(x):
    return jax.nn.sigmoid(x)

def _layernorm(x, axis=-1, eps=1e-05):
    m = jnp.mean(x, axis=axis, keepdims=True)
    v = jnp.var(x, axis=axis, keepdims=True)
    return (x - m) / jnp.sqrt(v + eps)

def _scatter_add(tgt, idx, src, axis=0):
    return tgt.at[idx].add(src)

def _segment_sum(src, seg, n):
    return jax.ops.segment_sum(src, seg, n)
kernel_name = 'mk_xattn_ffn_d2_seqx_r4_788ec7'

def setup_inputs(seed: int=0):
    np.random.seed(seed)
    _w = jnp.asarray

    def _rec_inputs():
        import jax
        import jax.numpy as jnp
        _rk = jax.random.key(seed)
        x = 0.0001212 + 1 * jax.random.normal(jax.random.fold_in(_rk, 1), (32, 128, 512), jnp.float32)
        _lenS = 128 - jax.random.randint(jax.random.fold_in(_rk, 7), (32,), 0, max(1, 128 // 4) + 1, jnp.int32)
        _lenS2 = 128 - jax.random.randint(jax.random.fold_in(_rk, 8), (32,), 0, max(1, 128 // 4) + 1, jnp.int32)
        _ctx_2048P = jax.random.normal(jax.random.fold_in(_rk, 11), (32, 16, 512), jnp.float32)
        _ctx_2048c = jax.random.dirichlet(jax.random.fold_in(_rk, 511), 0.3 * jnp.ones((16,), jnp.float32), (32, 128))
        _ctx_2048t = jnp.einsum('bsk,bkd->bsd', _ctx_2048c, _ctx_2048P)
        _ctx_2048t = _ctx_2048t * jax.lax.rsqrt(jnp.mean(jnp.square(_ctx_2048t)) + 1e-12) * 0.953939
        ctx_2048 = 0.000173663 + 1.0001 * (_ctx_2048t + 0.3 * jax.random.normal(jax.random.fold_in(_rk, 611), (32, 128, 512), jnp.float32))
        return (x, ctx_2048)
    x, ctx_2048 = _rec_inputs()

    def _L0_xattn_setup():
        import jax, jax.numpy as jnp
        import numpy as np
        B_DIM, T_DIM, C_DIM = (16, 256, 512)

        def _wkv(w, u, k, v):
            Bn, Tn, Cn = k.shape
            NEG_INF = jnp.float32(-1e+38)

            def step(carry, kv_t):
                p, q, o = carry
                kt, vt = kv_t
                no = jnp.maximum(o, u + kt)
                A = jnp.exp(o - no)
                E = jnp.exp(u + kt - no)
                y = (A * p + E * vt) / (A * q + E)
                no2 = jnp.maximum(w + o, kt)
                A2 = jnp.exp(w + o - no2)
                E2 = jnp.exp(kt - no2)
                return ((A2 * p + E2 * vt, A2 * q + E2, no2), y)
            init = (jnp.zeros((Bn, Cn), k.dtype), jnp.zeros((Bn, Cn), k.dtype), jnp.full((Bn, Cn), NEG_INF, k.dtype))
            kT = jnp.moveaxis(k, 1, 0)
            vT = jnp.moveaxis(v, 1, 0)
            _, yT = jax.lax.scan(step, init, (kT, vT))
            return jnp.moveaxis(yT, 0, 1)
        key = jax.random.key(seed)
        k1, k2, k3, k4 = jax.random.split(key, 4)
        w = -jnp.exp(jax.random.normal(k1, (C_DIM,), jnp.float32))
        u = jax.random.normal(k2, (C_DIM,), jnp.float32)
        k = jax.random.normal(k3, (B_DIM, T_DIM, C_DIM), jnp.float32)
        v = jax.random.normal(k4, (B_DIM, T_DIM, C_DIM), jnp.float32)
        return {'B': B_DIM, 'T': T_DIM, 'C': C_DIM, 'w': w, 'u': u, 'k': k, 'v': v}
    _L0_xattn_all = _L0_xattn_setup()
    _L0_xattn_in = {k: v for k, v in _L0_xattn_all.items() if k in ('w', 'u')}
    del _L0_xattn_all

    def _L0_ffn_setup():
        import jax, jax.numpy as jnp
        import numpy as np
        N_HEAD = 16
        N_EMBD = 512
        R = 8
        HEAD_DIM = N_EMBD // N_HEAD
        D_STD = HEAD_DIM - R
        THRESHOLD = 0.1
        B, T = (4, 256)
        key = jax.random.key(seed)
        k1, k2, k3, k4, k5 = jax.random.split(key, 5)
        fused_dim = 2 * N_HEAD * D_STD + N_EMBD + 2 * N_HEAD * R
        x = jax.random.normal(k1, (B, T, N_EMBD), dtype=jnp.float32)
        Wa = jax.random.normal(k2, (N_EMBD, fused_dim), dtype=jnp.float32) * 0.02
        Wp = jax.random.normal(k3, (N_EMBD, N_EMBD), dtype=jnp.float32) * 0.02
        w_std = jax.random.uniform(k4, (N_HEAD,), dtype=jnp.float32, minval=0.3, maxval=0.7)
        w_rec = jax.random.uniform(k5, (N_HEAD,), dtype=jnp.float32)
        return {'x': x, 'Wa': Wa, 'Wp': Wp, 'w_std': w_std, 'w_rec': w_rec}
    _L0_ffn_all = _L0_ffn_setup()
    _L0_ffn_in = {k: v for k, v in _L0_ffn_all.items() if k in ('Wa', 'Wp', 'w_std', 'w_rec')}
    del _L0_ffn_all

    def _L1_xattn_setup():
        import jax, jax.numpy as jnp
        import numpy as np
        B, S, E, NH = (2, 256, 512, 16)
        DH = E // NH
        EPS = 1e-06

        def _mlstm_forward(q, k, v, Wi, bi, Wf, bf, ln_scale):
            b, s, e = q.shape
            nh = Wi.shape[1]
            dh = e // nh
            x = jnp.concatenate([q, k, v], axis=-1)
            ig = (x @ Wi + bi).transpose(0, 2, 1)[..., None]
            fg = (x @ Wf + bf).transpose(0, 2, 1)[..., None]
            split = lambda t: t.reshape(b, s, nh, dh).transpose(0, 2, 1, 3)
            qh, kh, vh = (split(q), split(k), split(v))
            log_f = jax.nn.log_sigmoid(fg)
            log_f_cum = jnp.concatenate([jnp.zeros((b, nh, 1, 1), q.dtype), jnp.cumsum(log_f, axis=2)], axis=2)
            fg_mat = log_f_cum - jnp.transpose(log_f_cum, (0, 1, 3, 2))
            ltr = jnp.tril(jnp.ones((s, s), dtype=bool))
            log_fg = jnp.where(ltr, fg_mat[:, :, 1:, 1:], -jnp.inf)
            log_D = log_fg + jnp.transpose(ig, (0, 1, 3, 2))
            max_log_D = jnp.max(log_D, axis=-1, keepdims=True)
            D = jnp.exp(log_D - max_log_D)
            qk = jnp.einsum('bhsd,bhtd->bhst', qh, kh) / jnp.sqrt(jnp.asarray(dh, q.dtype))
            C = qk * D
            normalizer = jnp.maximum(jnp.abs(C.sum(-1, keepdims=True)), jnp.exp(-max_log_D))
            Cn = C / (normalizer + EPS)
            h = jnp.einsum('bhst,bhtd->bhsd', Cn, vh)
            mu = h.mean(-1, keepdims=True)
            var = ((h - mu) ** 2).mean(-1, keepdims=True)
            hn = (h - mu) * jax.lax.rsqrt(var + EPS)
            hn = hn * ln_scale.reshape(1, nh, 1, dh)
            return hn.transpose(0, 2, 1, 3).reshape(b, s, e)
        key = jax.random.key(seed)
        ks = jax.random.split(key, 6)
        q = jax.random.normal(ks[0], (B, S, E), dtype=jnp.float32)
        k = jax.random.normal(ks[1], (B, S, E), dtype=jnp.float32)
        v = jax.random.normal(ks[2], (B, S, E), dtype=jnp.float32)
        Wi = jax.random.normal(ks[3], (3 * E, NH), dtype=jnp.float32) * 0.02
        bi = jax.random.normal(ks[4], (NH,), dtype=jnp.float32) * 0.1
        Wf = jax.random.normal(ks[5], (3 * E, NH), dtype=jnp.float32) * 0.02
        bf = jnp.linspace(3.0, 6.0, NH, dtype=jnp.float32)
        ln_scale = jnp.ones((E,), dtype=jnp.float32)
        return {'q': q, 'k': k, 'v': v, 'Wi': Wi, 'bi': bi, 'Wf': Wf, 'bf': bf, 'ln_scale': ln_scale}
    _L1_xattn_all = _L1_xattn_setup()
    _L1_xattn_in = {k: v for k, v in _L1_xattn_all.items() if k in ('Wi', 'bi', 'Wf', 'bf', 'ln_scale')}
    del _L1_xattn_all

    def _L1_ffn_setup():
        import jax, jax.numpy as jnp
        import numpy as np
        HIDDEN = 512
        INTER = 192
        N_EXPERTS = 32
        TOP_K = 8
        key = jax.random.key(seed)
        k = jax.random.split(key, 5)
        s = 1.0 / np.sqrt(HIDDEN)
        return {'hidden_states': jax.random.normal(k[0], (1, 256, HIDDEN), jnp.float32), 'gate_w': jax.random.normal(k[1], (HIDDEN, N_EXPERTS), jnp.float32) * s, 'w_gate': jax.random.normal(k[2], (N_EXPERTS, HIDDEN, INTER), jnp.float32) * s, 'w_up': jax.random.normal(k[3], (N_EXPERTS, HIDDEN, INTER), jnp.float32) * s, 'w_down': jax.random.normal(k[4], (N_EXPERTS, INTER, HIDDEN), jnp.float32) * (1.0 / np.sqrt(INTER))}
    _L1_ffn_all = _L1_ffn_setup()
    _L1_ffn_in = {k: v for k, v in _L1_ffn_all.items() if k in ('gate_w', 'w_gate', 'w_up', 'w_down')}
    del _L1_ffn_all
    return {'x': x, 'ctx_2048': ctx_2048, 'L0_xattn_w': _L0_xattn_in['w'], 'L0_xattn_u': _L0_xattn_in['u'], 'L0_ffn_Wa': _L0_ffn_in['Wa'], 'L0_ffn_Wp': _L0_ffn_in['Wp'], 'L0_ffn_w_std': _L0_ffn_in['w_std'], 'L0_ffn_w_rec': _L0_ffn_in['w_rec'], 'L1_xattn_Wi': _L1_xattn_in['Wi'], 'L1_xattn_bi': _L1_xattn_in['bi'], 'L1_xattn_Wf': _L1_xattn_in['Wf'], 'L1_xattn_bf': _L1_xattn_in['bf'], 'L1_xattn_ln_scale': _L1_xattn_in['ln_scale'], 'L1_ffn_gate_w': _L1_ffn_in['gate_w'], 'L1_ffn_w_gate': _L1_ffn_in['w_gate'], 'L1_ffn_w_up': _L1_ffn_in['w_up'], 'L1_ffn_w_down': _L1_ffn_in['w_down']}

def reference(x, ctx_2048, L0_xattn_w, L0_xattn_u, L0_ffn_Wa, L0_ffn_Wp, L0_ffn_w_std, L0_ffn_w_rec, L1_xattn_Wi, L1_xattn_bi, L1_xattn_Wf, L1_xattn_bf, L1_xattn_ln_scale, L1_ffn_gate_w, L1_ffn_w_gate, L1_ffn_w_up, L1_ffn_w_down):
    import jax
    import jax.numpy as jnp

    def _L0_xattn_ref(B, T, C, w, u, k, v):
        import jax, jax.numpy as jnp
        import numpy as np
        B_DIM, T_DIM, C_DIM = (16, 256, 512)

        def _wkv(w, u, k, v):
            Bn, Tn, Cn = k.shape
            NEG_INF = jnp.float32(-1e+38)

            def step(carry, kv_t):
                p, q, o = carry
                kt, vt = kv_t
                no = jnp.maximum(o, u + kt)
                A = jnp.exp(o - no)
                E = jnp.exp(u + kt - no)
                y = (A * p + E * vt) / (A * q + E)
                no2 = jnp.maximum(w + o, kt)
                A2 = jnp.exp(w + o - no2)
                E2 = jnp.exp(kt - no2)
                return ((A2 * p + E2 * vt, A2 * q + E2, no2), y)
            init = (jnp.zeros((Bn, Cn), k.dtype), jnp.zeros((Bn, Cn), k.dtype), jnp.full((Bn, Cn), NEG_INF, k.dtype))
            kT = jnp.moveaxis(k, 1, 0)
            vT = jnp.moveaxis(v, 1, 0)
            _, yT = jax.lax.scan(step, init, (kT, vT))
            return jnp.moveaxis(yT, 0, 1)
        return _wkv(w, u, k, v)

    def _L0_ffn_ref(x, Wa, Wp, w_std, w_rec):
        import jax, jax.numpy as jnp
        import numpy as np
        N_HEAD = 16
        N_EMBD = 512
        R = 8
        HEAD_DIM = N_EMBD // N_HEAD
        D_STD = HEAD_DIM - R
        THRESHOLD = 0.1
        B, T = (4, 256)
        Bx, Tx, C = x.shape
        H, D, Ds, r = (N_HEAD, HEAD_DIM, D_STD, R)
        s_std = jnp.sqrt(jnp.clip(w_std, 1e-08, None))
        s_rec = jnp.sqrt(jnp.clip(w_rec, 1e-08, None))
        col_scale = jnp.concatenate([jnp.repeat(s_std, Ds), jnp.repeat(s_std, Ds), jnp.ones((C,), dtype=x.dtype), jnp.repeat(s_rec, r), jnp.repeat(s_rec, r)])
        Wb = Wa * col_scale[None, :]
        fused = x @ Wb
        q_std_end = H * Ds
        k_std_end = q_std_end + H * Ds
        v_end = k_std_end + C
        q_low_end = v_end + H * r

        def heads(t, d):
            return t.reshape(Bx, Tx, H, d).transpose(0, 2, 1, 3)
        Q_std = heads(fused[..., :q_std_end], Ds)
        K_std = heads(fused[..., q_std_end:k_std_end], Ds)
        V = heads(fused[..., k_std_end:v_end], D)
        Q_low = heads(fused[..., v_end:q_low_end], r)
        K_low = heads(fused[..., q_low_end:], r)
        use_ra = (w_rec > THRESHOLD)[None, :, None, None]
        q_tail = jnp.where(use_ra, K_low, Q_low)
        k_tail = jnp.where(use_ra, Q_low, K_low)
        Qf = jnp.concatenate([Q_std, q_tail], axis=-1)
        Kf = jnp.concatenate([K_std, k_tail], axis=-1)
        scale = 1.0 / jnp.sqrt(jnp.asarray(D, dtype=x.dtype))
        scores = jnp.einsum('bhtd,bhsd->bhts', Qf, Kf) * scale
        causal = jnp.tril(jnp.ones((Tx, Tx), dtype=bool))
        scores = jnp.where(causal[None, None], scores, jnp.finfo(scores.dtype).min)
        attn = jax.nn.softmax(scores, axis=-1)
        out = jnp.einsum('bhts,bhsd->bhtd', attn, V)
        y = out.transpose(0, 2, 1, 3).reshape(Bx, Tx, C)
        return y @ Wp

    def _L1_xattn_ref(q, k, v, Wi, bi, Wf, bf, ln_scale):
        import jax, jax.numpy as jnp
        import numpy as np
        B, S, E, NH = (2, 256, 512, 16)
        DH = E // NH
        EPS = 1e-06

        def _mlstm_forward(q, k, v, Wi, bi, Wf, bf, ln_scale):
            b, s, e = q.shape
            nh = Wi.shape[1]
            dh = e // nh
            x = jnp.concatenate([q, k, v], axis=-1)
            ig = (x @ Wi + bi).transpose(0, 2, 1)[..., None]
            fg = (x @ Wf + bf).transpose(0, 2, 1)[..., None]
            split = lambda t: t.reshape(b, s, nh, dh).transpose(0, 2, 1, 3)
            qh, kh, vh = (split(q), split(k), split(v))
            log_f = jax.nn.log_sigmoid(fg)
            log_f_cum = jnp.concatenate([jnp.zeros((b, nh, 1, 1), q.dtype), jnp.cumsum(log_f, axis=2)], axis=2)
            fg_mat = log_f_cum - jnp.transpose(log_f_cum, (0, 1, 3, 2))
            ltr = jnp.tril(jnp.ones((s, s), dtype=bool))
            log_fg = jnp.where(ltr, fg_mat[:, :, 1:, 1:], -jnp.inf)
            log_D = log_fg + jnp.transpose(ig, (0, 1, 3, 2))
            max_log_D = jnp.max(log_D, axis=-1, keepdims=True)
            D = jnp.exp(log_D - max_log_D)
            qk = jnp.einsum('bhsd,bhtd->bhst', qh, kh) / jnp.sqrt(jnp.asarray(dh, q.dtype))
            C = qk * D
            normalizer = jnp.maximum(jnp.abs(C.sum(-1, keepdims=True)), jnp.exp(-max_log_D))
            Cn = C / (normalizer + EPS)
            h = jnp.einsum('bhst,bhtd->bhsd', Cn, vh)
            mu = h.mean(-1, keepdims=True)
            var = ((h - mu) ** 2).mean(-1, keepdims=True)
            hn = (h - mu) * jax.lax.rsqrt(var + EPS)
            hn = hn * ln_scale.reshape(1, nh, 1, dh)
            return hn.transpose(0, 2, 1, 3).reshape(b, s, e)
        return _mlstm_forward(q, k, v, Wi, bi, Wf, bf, ln_scale)

    def _L1_ffn_ref(hidden_states, gate_w, w_gate, w_up, w_down):
        import jax, jax.numpy as jnp
        import numpy as np
        HIDDEN = 512
        INTER = 192
        N_EXPERTS = 32
        TOP_K = 8
        B, S, H = hidden_states.shape
        E = gate_w.shape[1]
        x = hidden_states.reshape(-1, H)
        T = x.shape[0]
        K = TOP_K
        P = T * K
        C = 2 * (P // E)
        probs = jax.nn.softmax(x @ gate_w, axis=-1)
        w, sel = jax.lax.top_k(probs, K)
        w = w / jnp.sum(w, axis=-1, keepdims=True)
        flat_e = sel.reshape(-1)
        flat_t = jnp.repeat(jnp.arange(T), K)
        flat_w = w.reshape(-1)
        order = jnp.argsort(flat_e)
        se = flat_e[order]
        start = jnp.searchsorted(se, jnp.arange(E))
        pos = jnp.arange(P) - start[se]
        slot = jnp.where(pos < C, se * C + pos, E * C)
        slot_pair = jnp.full((E * C,), P, dtype=jnp.int32).at[slot].set(order.astype(jnp.int32), mode='drop')
        t_slot = jnp.concatenate([flat_t, jnp.array([T])])[slot_pair]
        w_slot = jnp.concatenate([flat_w, jnp.zeros((1,), flat_w.dtype)])[slot_pair]
        x_pad = jnp.concatenate([x, jnp.zeros((1, H), x.dtype)], axis=0)
        xg = x_pad[t_slot].reshape(E, C, H)
        g = jnp.einsum('ech,ehi->eci', xg, w_gate)
        u = jnp.einsum('ech,ehi->eci', xg, w_up)
        y = jnp.einsum('eci,eih->ech', jax.nn.silu(g) * u, w_down).reshape(E * C, H)
        out = jnp.zeros((T + 1, H), x.dtype).at[t_slot].add(w_slot[:, None] * y)
        return out[:T].reshape(B, S, H)
    x = x + _L0_xattn_ref(32, 128, 512, L0_xattn_w, L0_xattn_u, _layernorm(x, axis=-1), ctx_2048)
    x = x + _L0_ffn_ref(_layernorm(x, axis=-1), L0_ffn_Wa, L0_ffn_Wp, L0_ffn_w_std, L0_ffn_w_rec)
    x = x + _L1_xattn_ref(_layernorm(x, axis=-1), ctx_2048, ctx_2048, L1_xattn_Wi, L1_xattn_bi, L1_xattn_Wf, L1_xattn_bf, L1_xattn_ln_scale)
    x = x + _L1_ffn_ref(_layernorm(x, axis=-1), L1_ffn_gate_w, L1_ffn_w_gate, L1_ffn_w_up, L1_ffn_w_down)
    return x

_drawn_inputs = setup_inputs


def setup_inputs(seed=0):
    import zlib

    import numpy as np

    out = dict(_drawn_inputs(seed))
    spreads = {'L1_xattn_ln_scale': (1.0, 0.2)}
    factors = {'L0_ffn_w_std': 64.0, 'L0_ffn_w_rec': 64.0, 'L1_xattn_bi': 64.0}
    for name, (base, spread) in spreads.items():
        noise = np.random.default_rng([zlib.crc32(name.encode()), seed]).standard_normal(out[name].shape)
        drawn = base * np.exp(spread * noise) if base else spread * noise
        out[name] = jnp.asarray(drawn.astype(out[name].dtype))
    for name, factor in factors.items():
        out[name] = (out[name] * factor).astype(out[name].dtype)
    return out
```

```python
from contextlib import ExitStack

import concourse.bass as bass
from concourse import mybir

F32 = mybir.dt.float32
BF16 = mybir.dt.bfloat16
ALU = mybir.AluOpType
ACT = mybir.ActivationFunctionType
AX = mybir.AxisListType

P = 128
NEG = -1.0e30
K_SHIFT = 16.0
U_CAP = 70.0


def build(nc, x, ctx_in, w, u, Wa, Wp, w_std, w_rec, Wi, bi, Wf, bf, ln_scale, gate_w, w_gate, w_up,
          w_down, out, NB=None, NE=None):
    B, T, D = x.shape
    H = w_std.shape[0]
    R = 8
    DH = D // H
    DS = DH - R
    KC = D // P
    E = gate_w.shape[1]
    INTER = w_gate.shape[2]
    I2 = INTER - P
    CAP = 2 * (B * T * 8 // E)
    assert T == P and H == 16 and DH == 32 and KC == 4 and E == 32 and INTER == 192
    nb, ne = NB or B, NE or E
    THRESH = 0.1
    QSCALE = float(DH) ** -0.5

    x3_d = nc.dram_tensor("x3_scratch", [B, P, D], F32, kind="Internal").ap()
    xT_d = nc.dram_tensor("xT_scratch", [P, KC, B * T], F32, kind="Internal").ap()

    with ExitStack() as whole:
        def sem(name):
            return whole.enter_context(nc.semaphore(name))

        def sbw(name, shape, dt=F32):
            return whole.enter_context(nc.sbuf_tensor(name, shape, dt))

        ps = whole.enter_context(nc.psum_tensor("ps", [P, 8, 512], F32))
        wc = sbw("wc", [P, B, E])

        with ExitStack() as ctx:
            def sb(name, shape, dt=F32):
                return ctx.enter_context(nc.sbuf_tensor(name, shape, dt))

            ident = sb("ident", [P, P])
            identb = sb("identb", [P, P], BF16)
            onesf = sb("onesf", [P, P])
            onesb = sb("onesb", [P, P], BF16)
            ustrict = sb("ustrict", [P, P], BF16)
            mask_ts = sb("mask_ts", [P, 4, P], BF16)
            mask_st = sb("mask_st", [P, 4, P], BF16)
            zerob = sb("zerob", [P, 4, P], BF16)
            ind = sb("ind", [H, 4, 4])
            steps = sb("steps", [P, T])
            eps5 = sb("eps5", [P, 1])
            eps6 = sb("eps6", [P, 1])
            nshift = sb("nshift", [P, 1])
            wch = sb("wch", [P, KC])
            uch = sb("uch", [P, KC])
            wpos = sb("wpos", [P, KC])
            nwpos = sb("nwpos", [P, KC])
            wneg = sb("wneg", [P, KC])
            decay = sb("decay", [P, KC])
            uw = sb("uw", [P, KC])
            dtab = sb("dtab", [P, KC, T])
            gam = sb("gam", [P, KC, T])
            zc = sb("zc", [P, KC, T])
            hs_ = sb("hs_", [P, 3, H])
            sst = sb("sst", [P, H])
            srl = sb("srl", [P, 4, H])
            wqk = sb("wqk", [P, KC, 2, H, DH])
            wv = sb("wv", [P, KC, D])
            wp = sb("wp", [P, KC, D])
            wg = sb("wg", [P, 2, KC, 48])
            gbias = sb("gbias", [48, 1])
            lnsc = sb("lnsc", [P, D])
            gw = sb("gw", [P, KC, E])
            xt = sb("xt", [P, D])
            ct = sb("ct", [P, D])
            st = [sb(f"st{n}", [P, 6]) for n in range(4)]
            mv = [sb(f"mv{n}", [P, 2]) for n in range(4)]
            lnv = [sb(f"lnv{n}", [P, 1]) for n in range(4)]
            rstd = [sb(f"rstd{n}", [P, 1]) for n in range(4)]
            kn = sb("kn", [P, D])
            ex = sb("ex", [P, KC, T])
            vT = sb("vT", [P, KC, T])
            gg = sb("gg", [P, KC, T])
            cc = sb("cc", [P, KC, T])
            gv = sb("gv", [P, KC, T])
            cv = sb("cv", [P, KC, T])
            sq_ = sb("sq_", [P, KC, T])
            sp_ = sb("sp_", [P, KC, T])
            rden = sb("rden", [P, KC, T])
            yy = sb("yy", [P, KC, T])
            x1 = sb("x1", [P, D])
            xn = sb("xn", [P, D])
            xnT = sb("xnT", [P, KC, T])
            qs = sb("qs", [P, KC, T])
            ks = sb("ks", [P, KC, T])
            vs = sb("vs", [P, D])
            nm = sb("nm", [P, 4, 4])
            rsum = sb("rsum", [P, 4, 4])
            rinv = sb("rinv", [P, 4, 4])
            pr = sb("pr", [P, 4, 4, T])
            pT = sb("pT", [P, 4, 4, T])
            on = sb("on", [P, D])
            oT = sb("oT", [P, KC, T])
            x2 = sb("x2", [P, D])
            qn = sb("qn", [P, D])
            qT = sb("qT", [P, KC, T])
            kT2 = sb("kT2", [P, KC, T])
            vaug = sb("vaug", [P, H, DH + 1])
            ig = sb("ig", [H, T])
            fg = sb("fg", [H, T])
            fa = sb("fa", [H, T])
            fe = sb("fe", [H, T])
            fl = sb("fl", [H, T])
            lf = sb("lf", [H, T])
            cum = sb("cum", [H, T])
            cmx = sb("cmx", [H, T])
            ncmx = sb("ncmx", [H, T])
            fm = sb("fm", [H, T])
            efm = sb("efm", [H, T])
            ar = sb("ar", [48, T])
            bd = sb("bd", [48, 4, 4, T])
            dm = sb("dm", [P, 4, 4, T])
            cm = sb("cm", [P, 4, 4, T])
            enT = sb("enT", [P, H])
            nrm = sb("nrm", [P, H])
            nrm2 = sb("nrm2", [P, H])
            rn = sb("rn", [P, H])
            hh = sb("hh", [P, H, DH])
            hmu = sb("hmu", [P, H])
            hmu2 = sb("hmu2", [P, H])
            hc = sb("hc", [P, H, DH])
            hsq = sb("hsq", [P, H, DH])
            hvar = sb("hvar", [P, H])
            hlv = sb("hlv", [P, H])
            hrs = sb("hrs", [P, H])
            hn = sb("hn", [P, H, DH])
            hw = sb("hw", [P, D])
            x3 = sb("x3", [P, D])
            zn = sb("zn", [P, D])
            zT = sb("zT", [P, KC, T])
            nmx = sb("nmx", [P, 1])
            er = sb("er", [P, E])
            top = sb("top", [P, 8])
            er2 = sb("er2", [P, E])
            sel = sb("sel", [P, E])
            selb = sb("selb", [P, E], BF16)
            selacc = sb("selacc", [P, E], BF16)
            s8 = sb("s8", [P, 1])
            r8 = sb("r8", [P, 1])
            wsel = sb("wsel", [P, E])

            wa_loaded = sem("wa_loaded")
            wg_loaded = sem("wg_loaded")
            small_loaded = sem("small_loaded")
            const_ready = sem("const_ready")
            tabs_ready = sem("tabs_ready")
            act_step = sem("act_step")
            dve_step = sem("dve_step")
            pool_step = sem("pool_step")
            x_loaded = sem("x_loaded")
            ctx_loaded = sem("ctx_loaded")
            x_free = sem("x_free")
            ct_free = sem("ct_free")
            st0 = sem("st0")
            st1 = sem("st1")
            st2 = sem("st2")
            st3 = sem("st3")
            rs0 = sem("rs0")
            rs1 = sem("rs1")
            rs2 = sem("rs2")
            rs3 = sem("rs3")
            kn_ready = sem("kn_ready")
            kT_ps = sem("kT_ps")
            cT_ps = sem("cT_ps")
            e_ready = sem("e_ready")
            g_ready = sem("g_ready")
            c_ready = sem("c_ready")
            vT_ready = sem("vT_ready")
            ctx_used = sem("ctx_used")
            y_ready = sem("y_ready")
            yT_ps = sem("yT_ps")
            xn_ready = sem("xn_ready")
            xnT_ps = sem("xnT_ps")
            xnT_ready = sem("xnT_ready")
            q_ps = sem("q_ps")
            k_ps = sem("k_ps")
            v_ps = sem("v_ps")
            q_ready = sem("q_ready")
            k_ready = sem("k_ready")
            v_ready = sem("v_ready")
            s_ps = sem("s_ps")
            nm_ready = sem("nm_ready")
            p_ready = sem("p_ready")
            pT_ps_dve = sem("pT_ps_dve")
            pT_ps_act = sem("pT_ps_act")
            pT_ready_dve = sem("pT_ready_dve")
            pT_ready_act = sem("pT_ready_act")
            o_ps = sem("o_ps")
            on_ready = sem("on_ready")
            oT_ps = sem("oT_ps")
            oT_ready = sem("oT_ready")
            att_ps = sem("att_ps")
            cd_ctx_free = sem("cd_ctx_free")
            cd_ctx_ready = sem("cd_ctx_ready")
            qn_ready = sem("qn_ready")
            qT_ps = sem("qT_ps")
            qT_ready = sem("qT_ready")
            g_ps = sem("g_ps")
            lf_parts = sem("lf_parts")
            m_ready = sem("m_ready")
            fm_ready = sem("fm_ready")
            efm_ready = sem("efm_ready")
            nT_ps = sem("nT_ps")
            enT_done = sem("enT_done")
            bd_ready = sem("bd_ready")
            l_ps = sem("l_ps")
            d_ready = sem("d_ready")
            qk_ps = sem("qk_ps")
            cm_ready = sem("cm_ready")
            hu_ps = sem("hu_ps")
            hc_ready = sem("hc_ready")
            hsq_ready = sem("hsq_ready")
            hvar_ready = sem("hvar_ready")
            hrs_ready = sem("hrs_ready")
            hn_ready = sem("hn_ready")
            x3_ready = sem("x3_ready")
            x3_go = sem("x3_go")
            x3_stored = sem("x3_stored")
            zn_ready = sem("zn_ready")
            zT_ps = sem("zT_ps")
            zT_ready = sem("zT_ready")
            zT_stored = sem("zT_stored")
            rl_ps = sem("rl_ps")
            nmx_ready = sem("nmx_ready")
            er_ready = sem("er_ready")
            sel_ready = sem("sel_ready")
            pos_ps = sem("pos_ps")
            wts_scaled = sem("wts_scaled")
            masks_ready = sem("masks_ready")
            tab_parts = sem("tab_parts")
            scale_parts = sem("scale_parts")
            srs_ready = sem("srs_ready")

            wraw = dm[:, :, :, :].rearrange("p a b t -> p (a b t)")
            block = ctx.enter_context(nc.Block())

            @block.sync
            def _(sp):
                sp.dma_start(wch[:, :], w.rearrange("(k p) -> p k", p=P), allow_slow_non_contiguous=True).then_inc(small_loaded, 16)
                sp.dma_start(uch[:, :], u.rearrange("(k p) -> p k", p=P), allow_slow_non_contiguous=True).then_inc(small_loaded, 16)
                sp.dma_start(hs_[:, 0, :], w_std.partition_broadcast(P)).then_inc(small_loaded, 16)
                sp.dma_start(hs_[:, 1, :], w_rec.partition_broadcast(P)).then_inc(small_loaded, 16)
                sp.dma_start(xt[:, :], x[0]).then_inc(x_loaded, 16)
                sp.dma_start(ct[:, :], ctx_in[0]).then_inc(ctx_loaded, 16)
                wa_v = Wa.rearrange("(k p) n -> p k n", p=P)
                q_end, k_end, v_end, ql_end = H * DS, 2 * H * DS, 2 * H * DS + D, 2 * H * DS + D + H * R
                for k in range(KC):
                    for j, (c0, l0) in enumerate([(0, v_end), (q_end, ql_end)]):
                        sp.dma_start(wqk[:, k, j, :, 0:DS],
                                     wa_v[:, k, c0:c0 + H * DS].rearrange("p (h d) -> p h d", h=H)).then_inc(wa_loaded, 16)
                        sp.dma_start(wraw[:, (2 * k + j) * H * R:(2 * k + j + 1) * H * R],
                                     wa_v[:, k, l0:l0 + H * R]).then_inc(wa_loaded, 16)
                sp.dma_start(wv[:, :, :], wa_v[:, :, k_end:v_end]).then_inc(wa_loaded, 16)
                sp.dma_start(wp[:, :, :], Wp.rearrange("(k p) n -> p k n", p=P)).then_inc(wa_loaded, 16)
                sp.wait_ge(masks_ready, 1)
                sp.sem_inc(masks_ready, -1)
                for a, (W_, c0) in enumerate([(Wi, 0), (Wf, 32)]):
                    v_ = W_.rearrange("(j k p) n -> p j k n", j=3, p=P)
                    for k in range(KC):
                        sp.dma_start(wg[:, 0, k, c0:c0 + H], v_[:, 0, k, :]).then_inc(wg_loaded, 16)
                        sp.dma_start(wg[:, 1, k, c0:c0 + H], v_[:, 1, k, :]).then_inc(wg_loaded, 16)
                        sp.dma_start(cm[:, a, 0, k * H:(k + 1) * H], v_[:, 2, k, :]).then_inc(wg_loaded, 16)
                sp.dma_start(gbias[0:H, :], bi.rearrange("(h a) -> h a", a=1)).then_inc(wg_loaded, 16)
                sp.dma_start(gbias[32:32 + H, :], bf.rearrange("(h a) -> h a", a=1)).then_inc(wg_loaded, 16)
                sp.dma_start(lnsc[:, :], ln_scale.partition_broadcast(P)).then_inc(wg_loaded, 16)
                sp.dma_start(gw[:, :, :], gate_w.rearrange("(k p) e -> p k e", p=P)).then_inc(wg_loaded, 16)

                def load(i):
                    sp.wait_ge(x_free, 1)
                    sp.sem_inc(x_free, -1)
                    sp.dma_start(xt[:, :], x[bass.ds(i, 1)].rearrange("a p d -> p (a d)")).then_inc(x_loaded, 16)
                    sp.wait_ge(ct_free, 1)
                    sp.sem_inc(ct_free, -1)
                    sp.dma_start(ct[:, :], ctx_in[bass.ds(i, 1)].rearrange("a p d -> p (a d)")).then_inc(ctx_loaded, 16)

                def store(i):
                    sp.wait_ge(x3_go, 1)
                    sp.sem_inc(x3_go, -1)
                    sp.dma_start(x3_d[bass.ds(i, 1)].rearrange("a p d -> p (a d)"), x3[:, :]).then_inc(x3_stored, 16)

                with sp.Fori(1, nb) as i:
                    load(i)
                    store(i - 1)
                sp.wait_ge(x_free, 1)
                sp.sem_inc(x_free, -1)
                sp.wait_ge(ct_free, 1)
                sp.sem_inc(ct_free, -1)
                store(nb - 1)

            @block.gpsimd
            def _(pool):
                pool.memset(wg[:, :, :, :], 0.0).then_inc(masks_ready, 1)
                pool.memset(ident[:, :], 0.0)
                pool.memset(onesf[:, :], 1.0)
                pool.memset(onesb[:, :], 1.0)
                pool.memset(zerob[:, :, :], 0.0)
                pool.memset(eps5[:, :], 1e-5)
                pool.memset(eps6[:, :], 1e-6)
                pool.memset(nshift[:, :], -K_SHIFT)
                pool.memset(selacc[:, :], 0.0)
                pool.memset(ar[:, :], 0.0)
                pool.memset(ind[:, :, :], 0.0)
                pool.memset(bd[:, :, :, :], 0.0).then_inc(pool_step, 1)
                pool.wait_ge(pool_step, 1)
                pool.sem_inc(pool_step, -1)
                pool.memset(ar[0:H, :], 1.0)
                pool.affine_select(out=ident[:, :], in_=ident[:, :], compare_op=ALU.not_equal, fill=1.0, base=0,
                                   pattern=[[-1, P]], channel_multiplier=1)
                pool.affine_select(out=identb[:, :], in_=zerob[:, 0, :], compare_op=ALU.not_equal, fill=1.0, base=0,
                                   pattern=[[-1, P]], channel_multiplier=1)
                pool.affine_select(out=ustrict[:, :], in_=zerob[:, 0, :], compare_op=ALU.is_ge, fill=1.0, base=0,
                                   pattern=[[-1, P]], channel_multiplier=1)
                pool.affine_select(out=mask_ts[:, :, :], in_=zerob[:, :, :], compare_op=ALU.is_ge, fill=NEG, base=0,
                                   pattern=[[0, 4], [-1, P]], channel_multiplier=1)
                pool.affine_select(out=mask_st[:, :, :], in_=zerob[:, :, :], compare_op=ALU.is_ge, fill=NEG, base=0,
                                   pattern=[[0, 4], [1, P]], channel_multiplier=-1)
                pool.affine_select(out=ind[:, :, :], in_=ind[:, :, :], compare_op=ALU.not_equal, fill=1.0, base=0,
                                   pattern=[[-1, 4], [-4, 4]], channel_multiplier=1).then_inc(pool_step, 1)
                pool.wait_ge(pool_step, 1)
                pool.sem_inc(pool_step, -1)
                pool.affine_select(out=bd[32:32 + H, :, :, :], in_=bd[32:32 + H, :, :, :],
                                   compare_op=ALU.not_equal, fill=1.0, base=0,
                                   pattern=[[-1, 4], [-4, 4], [0, T]], channel_multiplier=1).then_inc(pool_step, 1)
                pool.wait_ge(pool_step, 1)
                pool.sem_inc(pool_step, -1)
                pool.iota(steps[:, :], pattern=[[1, T]], base=0, channel_multiplier=0,
                          allow_small_or_imprecise_dtypes=True).then_inc(pool_step, 1)
                pool.wait_ge(pool_step, 1)
                pool.sem_inc(pool_step, -1)
                pool.sem_inc(x3_stored, 16)
                pool.sem_inc(zT_stored, 16)
                pool.sem_inc(cd_ctx_free, 1)
                pool.sem_inc(const_ready, 3)

                def a3():
                    pool.wait_ge(e_ready, 1)
                    pool.sem_inc(e_ready, -1)
                    pool.tensor_tensor(gg[:, :, :], gam[:, :, :], ex[:, :, :], ALU.mult).then_inc(g_ready, 1)
                    pool.tensor_tensor(cc[:, :, :], zc[:, :, :], ex[:, :, :], ALU.mult).then_inc(c_ready, 1)

                def a7():
                    pool.wait_ge(ctx_used, 1)
                    pool.sem_inc(ctx_used, -1)
                    pool.wait_ge(cd_ctx_free, 1)
                    pool.sem_inc(cd_ctx_free, -1)
                    pool.tensor_copy(kT2[:, :, :], vT[:, :, :])
                    pool.tensor_copy(vaug[:, :, 0:DH], ct[:, :].rearrange("p (h d) -> p h d", h=H)).then_inc(ct_free, 1)
                    pool.memset(vaug[:, :, DH:DH + 1], 1.0).then_inc(cd_ctx_ready, 1)

                def c2():
                    pool.wait_ge(m_ready, 1)
                    pool.sem_inc(m_ready, -1)
                    pool.tensor_tensor(bd[0:H, :, :, :].rearrange("h r c t -> h (r c) t"),
                                       ind[:, :, :].rearrange("h r c -> h (r c)").unsqueeze(2).to_broadcast([H, 16, T]),
                                       ncmx[:, :].unsqueeze(1).to_broadcast([H, 16, T]), ALU.mult).then_inc(bd_ready, 1)

                def c5():
                    pool.wait_ge(hn_ready, 1)
                    pool.sem_inc(hn_ready, -1)
                    pool.tensor_tensor(hw[:, :], hn[:, :, :].rearrange("p h d -> p (h d)"), lnsc[:, :], ALU.mult).then_inc(pool_step, 1)
                    pool.wait_ge(pool_step, 1)
                    pool.sem_inc(pool_step, -1)
                    pool.wait_ge(x3_stored, 16)
                    pool.sem_inc(x3_stored, -16)
                    pool.tensor_tensor(x3[:, :], x2[:, :], hw[:, :], ALU.add).then_inc(x3_ready, 1)

                pool.wait_ge(tabs_ready, 1)
                pool.sem_inc(tabs_ready, -1)
                a3()
                a7()
                with pool.Fori(1, nb):
                    c2()
                    a3()
                    c5()
                    a7()
                c2()
                c5()
                pool.wait_ge(x3_stored, 16)
                pool.sem_inc(x3_stored, -16)

            @block.scalar
            def _(act):
                act.preload_act_table_set("natural_log_exp_and_others")
                act.wait_ge(const_ready, 1)
                act.sem_inc(const_ready, -1)
                act.wait_ge(tab_parts, 1)
                act.sem_inc(tab_parts, -1)
                act.activation(decay[:, :], wneg[:, :], ACT.Exp)
                for k in range(KC):
                    act.activation(gam[:, k, :], steps[:, :], ACT.Exp, scale=nwpos[:, k:k + 1])
                    a = act.activation(zc[:, k, :], zc[:, k, :], ACT.Exp)
                a.then_inc(scale_parts, 1)
                act.wait_ge(tab_parts, 1)
                act.sem_inc(tab_parts, -1)
                act.activation(srl[:, 0:2, :], hs_[:, 0:2, :], ACT.Ln).then_inc(act_step, 1)
                act.wait_ge(act_step, 1)
                act.sem_inc(act_step, -1)
                act.activation(srl[:, 2:4, :], srl[:, 0:2, :], ACT.Exp, scale=0.5).then_inc(srs_ready, 1)

                def rstd_of(n, eps):
                    act.wait_ge((st0, st1, st2, st3)[n], 1)
                    act.sem_inc((st0, st1, st2, st3)[n], -1)
                    act.activation(lnv[n][:, :], mv[n][:, 1:2], ACT.Ln, bias=eps[:, :]).then_inc(act_step, 1)
                    act.wait_ge(act_step, 1)
                    act.sem_inc(act_step, -1)
                    act.activation(rstd[n][:, :], lnv[n][:, :], ACT.Exp, scale=-0.5).then_inc((rs0, rs1, rs2, rs3)[n], 1)

                def a1():
                    rstd_of(0, eps5)

                def a2():
                    act.wait_ge(kT_ps, 1)
                    act.sem_inc(kT_ps, -1)
                    act.activation(ex[:, :, :].rearrange("p k t -> p (k t)"), ps[:, 0, :], ACT.Exp,
                                   bias=nshift[:, :]).then_inc(e_ready, 1)
                    act.wait_ge(cT_ps, 1)
                    act.sem_inc(cT_ps, -1)
                    act.activation(vT[:, :, :].rearrange("p k t -> p (k t)"), ps[:, 1, :], ACT.Copy).then_inc(vT_ready, 1)

                def a4():
                    rstd_of(1, eps5)

                def a5():
                    act.wait_ge(xnT_ps, 1)
                    act.sem_inc(xnT_ps, -1)
                    act.activation(xnT[:, :, :].rearrange("p k t -> p (k t)"), ps[:, 3, :], ACT.Copy).then_inc(xnT_ready, 1)
                    act.wait_ge(k_ps, 1)
                    act.sem_inc(k_ps, -1)
                    act.activation(ks[:, :, :].rearrange("p k t -> p (k t)"), ps[:, 1, :], ACT.Copy).then_inc(k_ready, 1)
                    act.wait_ge(v_ps, 1)
                    act.sem_inc(v_ps, -1)
                    act.activation(vs[:, :], ps[:, 2, :], ACT.Copy).then_inc(v_ready, 1)

                def exps(r):
                    act.wait_ge(nm_ready, 1)
                    act.sem_inc(nm_ready, -1)
                    bank = (3, 0, 1, 3)[r]
                    for c in range(4):
                        a = act.activation(pr[:, r, c, :], ps[:, bank, c * T:(c + 1) * T], ACT.Exp,
                                           bias=nm[:, r, c:c + 1], accum_out=rsum[:, r, c:c + 1])
                    a.then_inc(p_ready, 1)

                def pT_copy(r):
                    act.wait_ge(pT_ps_act, 1)
                    act.sem_inc(pT_ps_act, -1)
                    bank = (2, 0, 1, 3)[r]
                    act.activation(pT[:, r, :, :].rearrange("p c t -> p (c t)"), ps[:, bank, :], ACT.Copy)\
                       .then_inc(pT_ready_act, 1)

                def a6():
                    exps(0)
                    exps(1)
                    exps(2)
                    pT_copy(1)
                    exps(3)
                    pT_copy(3)

                def a7():
                    act.wait_ge(oT_ps, 1)
                    act.sem_inc(oT_ps, -1)
                    act.activation(oT[:, :, :].rearrange("p k t -> p (k t)"), ps[:, 0, :], ACT.Copy).then_inc(oT_ready, 1)

                def c1():
                    rstd_of(2, eps5)
                    act.wait_ge(qT_ps, 1)
                    act.sem_inc(qT_ps, -1)
                    act.activation(qT[:, :, :].rearrange("p k t -> p (k t)"), ps[:, 4, :], ACT.Copy).then_inc(qT_ready, 1)

                def c2():
                    act.wait_ge(g_ps, 1)
                    act.sem_inc(g_ps, -1)
                    act.activation(ig[:, :], ps[0:H, 5, 0:T], ACT.Identity, bias=gbias[0:H, :])
                    act.activation(fg[:, :], ps[32:32 + H, 5, 0:T], ACT.Identity, bias=gbias[32:32 + H, :]).then_inc(act_step, 1)
                    act.wait_ge(act_step, 1)
                    act.sem_inc(act_step, -1)
                    act.activation(fa[:, :], fg[:, :], ACT.Abs).then_inc(act_step, 1)
                    act.wait_ge(act_step, 1)
                    act.sem_inc(act_step, -1)
                    act.activation(fe[:, :], fa[:, :], ACT.Exp, scale=-1.0).then_inc(act_step, 1)
                    act.wait_ge(act_step, 1)
                    act.sem_inc(act_step, -1)
                    act.activation(fl[:, :], fe[:, :], ACT.Ln, bias=1.0).then_inc(lf_parts, 1)
                    act.wait_ge(fm_ready, 1)
                    act.sem_inc(fm_ready, -1)
                    act.activation(efm[:, :], fm[:, :], ACT.Exp, scale=-1.0).then_inc(efm_ready, 1)

                def c3():
                    for r in range(4):
                        act.wait_ge(l_ps, 1)
                        act.sem_inc(l_ps, -1)
                        act.activation(dm[:, r, :, :].rearrange("p c t -> p (c t)"), ps[:, (4, 6)[r % 2], :],
                                       ACT.Exp).then_inc(d_ready, 1)

                def c5():
                    act.wait_ge(hc_ready, 1)
                    act.sem_inc(hc_ready, -1)
                    act.activation(hsq[:, :, :], hc[:, :, :], ACT.Square).then_inc(hsq_ready, 1)
                    act.wait_ge(hvar_ready, 1)
                    act.sem_inc(hvar_ready, -1)
                    act.activation(hlv[:, :], hvar[:, :], ACT.Ln, scale=1.0 / DH, bias=eps6[:, :]).then_inc(act_step, 1)
                    act.wait_ge(act_step, 1)
                    act.sem_inc(act_step, -1)
                    act.activation(hrs[:, :], hlv[:, :], ACT.Exp, scale=-0.5).then_inc(hrs_ready, 1)

                def d1(i):
                    rstd_of(3, eps5)
                    act.wait_ge(zT_ps, 1)
                    act.sem_inc(zT_ps, -1)
                    act.wait_ge(zT_stored, 16)
                    act.sem_inc(zT_stored, -16)
                    act.activation(zT[:, :, :].rearrange("p k t -> p (k t)"), ps[:, 6, :], ACT.Copy).then_inc(act_step, 1)
                    act.wait_ge(act_step, 1)
                    act.sem_inc(act_step, -1)
                    act.sem_inc(zT_ready, 1)
                    act.dma_start(xT_d[:, :, bass.ds(i * T, T)], zT[:, :, :]).then_inc(zT_stored, 16)
                    act.wait_ge(nmx_ready, 1)
                    act.sem_inc(nmx_ready, -1)
                    act.activation(er[:, :], ps[:, 7, 0:E], ACT.Exp, bias=nmx[:, :]).then_inc(er_ready, 1)

                a1()
                a2()
                a4()
                a5()
                a6()
                a7()
                with act.Fori(1, nb) as i:
                    c1()
                    a1()
                    c2()
                    a2()
                    c3()
                    a4()
                    c5()
                    a5()
                    d1(i - 1)
                    a6()
                    a7()
                c1()
                c2()
                c3()
                c5()
                d1(nb - 1)
                act.wait_ge(zT_stored, 16)
                act.sem_inc(zT_stored, -16)

            @block.tensor
            def _(pe):
                pe.wait_ge(const_ready, 1)
                pe.sem_inc(const_ready, -1)

                def turn(bank, src, signal):
                    for c in range(4):
                        m = pe.transpose(ps[:, bank, c * P:(c + 1) * P], src(c), ident[:, :])
                    m.then_inc(signal, 1)

                def a2():
                    pe.wait_ge(kn_ready, 1)
                    pe.sem_inc(kn_ready, -1)
                    turn(0, lambda c: kn[:, c * P:(c + 1) * P], kT_ps)
                    pe.wait_ge(ctx_loaded, 16)
                    pe.sem_inc(ctx_loaded, -16)
                    turn(1, lambda c: ct[:, c * P:(c + 1) * P], cT_ps)

                def a4():
                    pe.wait_ge(y_ready, 1)
                    pe.sem_inc(y_ready, -1)
                    turn(2, lambda c: yy[:, c, :], yT_ps)

                def a5():
                    pe.wait_ge(xn_ready, 1)
                    pe.sem_inc(xn_ready, -1)
                    turn(3, lambda c: xn[:, c * P:(c + 1) * P], xnT_ps)
                    pe.wait_ge(xnT_ready, 1)
                    pe.sem_inc(xnT_ready, -1)
                    for j, signal in enumerate((q_ps, k_ps)):
                        for c in range(4):
                            for k in range(KC):
                                m = pe.matmul(ps[:, j, c * T:(c + 1) * T],
                                              wqk[:, k, j, 4 * c:4 * c + 4, :].rearrange("p h d -> p (h d)"),
                                              xnT[:, k, :], start=(k == 0), stop=(k == KC - 1))
                        m.then_inc(signal, 1)
                    for k in range(KC):
                        m = pe.matmul(ps[:, 2, :], xnT[:, k, :], wv[:, k, :], start=(k == 0), stop=(k == KC - 1))
                    m.then_inc(v_ps, 1)

                def scores(r):
                    bank = (3, 0, 1, 3)[r]
                    pe.matmul(ps[:, bank, :], identb[:, :], mask_ts[:, :, :].rearrange("p a t -> p (a t)"),
                              start=True, stop=False, skip_group_check=True)
                    for c in range(4):
                        m = pe.matmul(ps[:, bank, c * T:(c + 1) * T], qs[32 * r:32 * r + 32, c, :],
                                      ks[32 * r:32 * r + 32, c, :], start=False, stop=True, skip_group_check=True)
                    m.then_inc(s_ps, 1)

                def p_turn(r):
                    pe.wait_ge(p_ready, 1)
                    pe.sem_inc(p_ready, -1)
                    bank = (2, 0, 1, 3)[r]
                    turn(bank, lambda c: pr[:, r, c, :], (pT_ps_dve, pT_ps_act)[r % 2])

                def a6():
                    pe.wait_ge(q_ready, 1)
                    pe.sem_inc(q_ready, -1)
                    pe.wait_ge(k_ready, 1)
                    pe.sem_inc(k_ready, -1)
                    scores(0)
                    scores(1)
                    scores(2)
                    pe.wait_ge(v_ready, 1)
                    pe.sem_inc(v_ready, -1)
                    p_turn(0)
                    scores(3)
                    p_turn(1)
                    p_turn(2)
                    p_turn(3)

                def a7():
                    for r in range(4):
                        pe.wait_ge((pT_ready_dve, pT_ready_act)[r % 2], 1)
                        pe.sem_inc((pT_ready_dve, pT_ready_act)[r % 2], -1)
                        for c in range(4):
                            h = 4 * c + r
                            m = pe.matmul(ps[:, 2, h * DH:(h + 1) * DH], pT[:, r, c, :], vs[:, h * DH:(h + 1) * DH],
                                          start=True, stop=True)
                    m.then_inc(o_ps, 1)
                    pe.wait_ge(on_ready, 1)
                    pe.sem_inc(on_ready, -1)
                    turn(0, lambda c: on[:, c * P:(c + 1) * P], oT_ps)
                    pe.wait_ge(oT_ready, 1)
                    pe.sem_inc(oT_ready, -1)
                    for k in range(KC):
                        m = pe.matmul(ps[:, 1, :], oT[:, k, :], wp[:, k, :], start=(k == 0), stop=(k == KC - 1))
                    m.then_inc(att_ps, 1)

                def c1():
                    pe.wait_ge(qn_ready, 1)
                    pe.sem_inc(qn_ready, -1)
                    turn(4, lambda c: qn[:, c * P:(c + 1) * P], qT_ps)

                def c2():
                    pe.wait_ge(cd_ctx_ready, 1)
                    pe.sem_inc(cd_ctx_ready, -1)
                    pe.wait_ge(qT_ready, 1)
                    pe.sem_inc(qT_ready, -1)
                    for j in range(2):
                        for k in range(KC):
                            m = pe.matmul(ps[0:48, 5, 0:T], wg[:, j, k, :], (qT, kT2)[j][:, k, :],
                                          start=(j == 0 and k == 0), stop=(j == 1 and k == KC - 1))
                    m.then_inc(g_ps, 1)

                def c3():
                    pe.wait_ge(efm_ready, 1)
                    pe.sem_inc(efm_ready, -1)
                    pe.transpose(ps[:, 7, 0:H], efm[:, :], ident[0:H, 0:H]).then_inc(nT_ps, 1)
                    pe.wait_ge(bd_ready, 1)
                    pe.sem_inc(bd_ready, -1)
                    for r in range(4):
                        if r == 1:
                            pe.wait_ge(enT_done, 1)
                            pe.sem_inc(enT_done, -1)
                        if r >= 2:
                            pe.wait_ge(cm_ready, 1)
                            pe.sem_inc(cm_ready, -1)
                        lb, qb = ((4, 5), (6, 7))[r % 2]
                        pe.matmul(ps[:, lb, :], identb[:, :], mask_st[:, :, :].rearrange("p a t -> p (a t)"),
                                  start=True, stop=False, skip_group_check=True)
                        pe.matmul(ps[:, lb, :], ar[:, :], bd[:, r, :, :].rearrange("h c t -> h (c t)"),
                                  start=False, stop=True, skip_group_check=True).then_inc(l_ps, 1)
                        for c in range(4):
                            m = pe.matmul(ps[:, qb, c * T:(c + 1) * T], kT2[32 * r:32 * r + 32, c, :],
                                          qT[32 * r:32 * r + 32, c, :], start=True, stop=True)
                        m.then_inc(qk_ps, 1)

                def c4():
                    for n in range(2):
                        pe.wait_ge(cm_ready, 1)
                        pe.sem_inc(cm_ready, -1)
                    for h in range(H):
                        r, c = h % 4, h // 4
                        o = (h % 8) * (DH + 1)
                        m = pe.matmul(ps[:, 4 + h // 8, o:o + DH + 1], cm[:, r, c, :], vaug[:, h, :],
                                      start=True, stop=True)
                    m.then_inc(hu_ps, 1)

                def d1():
                    pe.wait_ge(zn_ready, 1)
                    pe.sem_inc(zn_ready, -1)
                    turn(6, lambda c: zn[:, c * P:(c + 1) * P], zT_ps)
                    pe.wait_ge(zT_ready, 1)
                    pe.sem_inc(zT_ready, -1)
                    for k in range(KC):
                        m = pe.matmul(ps[:, 7, 0:E], zT[:, k, :], gw[:, k, :], start=(k == 0), stop=(k == KC - 1))
                    m.then_inc(rl_ps, 1)
                    pe.wait_ge(sel_ready, 1)
                    pe.sem_inc(sel_ready, -1)
                    pe.matmul(ps[:, 7, 64:64 + E], ustrict[:, :], selb[:, :], start=True, stop=False)
                    pe.matmul(ps[:, 7, 64:64 + E], onesb[:, :], selacc[:, :], start=False, stop=True).then_inc(pos_ps, 1)

                pe.wait_ge(wts_scaled, 1)
                pe.sem_inc(wts_scaled, -1)
                a2()
                a4()
                a5()
                a6()
                a7()
                with pe.Fori(1, nb):
                    c1()
                    c2()
                    a2()
                    c3()
                    a4()
                    c4()
                    a5()
                    d1()
                    a6()
                    a7()
                c1()
                c2()
                c3()
                c4()
                d1()

            @block.vector
            def _(dve):
                dve.wait_ge(const_ready, 1)
                dve.sem_inc(const_ready, -1)
                dve.wait_ge(small_loaded, 64)
                dve.sem_inc(small_loaded, -64)
                dve.tensor_scalar(wpos[:, :], wch[:, :], 0.0, None, ALU.max).then_inc(dve_step, 1)
                dve.wait_ge(dve_step, 1)
                dve.sem_inc(dve_step, -1)
                dve.tensor_scalar(nwpos[:, :], wch[:, :], 0.0, -1.0, ALU.max, ALU.mult)
                dve.tensor_scalar(wneg[:, :], wch[:, :], 0.0, None, ALU.min).then_inc(dve_step, 1)
                dve.wait_ge(dve_step, 1)
                dve.sem_inc(dve_step, -1)
                dve.tensor_tensor(uw[:, :], uch[:, :], wpos[:, :], ALU.add).then_inc(dve_step, 1)
                dve.wait_ge(dve_step, 1)
                dve.sem_inc(dve_step, -1)
                for k in range(KC):
                    dve.tensor_scalar(zc[:, k, :], steps[:, :], nwpos[:, k:k + 1], uw[:, k:k + 1], ALU.mult, ALU.add).then_inc(dve_step, 1)
                    dve.wait_ge(dve_step, 1)
                    dve.sem_inc(dve_step, -1)
                dve.tensor_scalar(zc[:, :, :], zc[:, :, :], U_CAP, None, ALU.min).then_inc(dve_step, 1)
                dve.wait_ge(dve_step, 1)
                dve.sem_inc(dve_step, -1)
                dve.sem_inc(tab_parts, 1)
                dve.tensor_scalar(hs_[:, 2, :], hs_[:, 1, :], THRESH, None, ALU.is_gt).then_inc(dve_step, 1)
                dve.wait_ge(dve_step, 1)
                dve.sem_inc(dve_step, -1)
                dve.tensor_scalar(hs_[:, 0:2, :], hs_[:, 0:2, :], 1e-8, None, ALU.max).then_inc(dve_step, 1)
                dve.wait_ge(dve_step, 1)
                dve.sem_inc(dve_step, -1)
                dve.sem_inc(tab_parts, 1)
                dve.wait_ge(scale_parts, 1)
                dve.sem_inc(scale_parts, -1)
                for k in range(KC):
                    dve.tensor_scalar(dtab[:, k, :], onesf[:, :], decay[:, k:k + 1], None, ALU.mult).then_inc(dve_step, 1)
                    dve.wait_ge(dve_step, 1)
                    dve.sem_inc(dve_step, -1)
                dve.memset(zc[:, :, 0:1], 1.0).then_inc(dve_step, 1)
                dve.wait_ge(dve_step, 1)
                dve.sem_inc(dve_step, -1)
                dve.memset(dtab[:, :, 0:1], 0.0).then_inc(dve_step, 1)
                dve.wait_ge(dve_step, 1)
                dve.sem_inc(dve_step, -1)
                dve.sem_inc(tabs_ready, 1)
                dve.wait_ge(srs_ready, 1)
                dve.sem_inc(srs_ready, -1)
                dve.tensor_copy(sst[:, :], srl[:, 2, :]).then_inc(dve_step, 1)
                dve.wait_ge(dve_step, 1)
                dve.sem_inc(dve_step, -1)
                dve.tensor_copy(srl[:, 0, :], srl[:, 3, :]).then_inc(dve_step, 1)
                dve.wait_ge(dve_step, 1)
                dve.sem_inc(dve_step, -1)
                dve.tensor_tensor(srl[:, 1, :], srl[:, 3, :], hs_[:, 2, :], ALU.mult).then_inc(dve_step, 1)
                dve.wait_ge(dve_step, 1)
                dve.sem_inc(dve_step, -1)
                dve.tensor_tensor(srl[:, 0, :], srl[:, 0, :], srl[:, 1, :], ALU.subtract).then_inc(dve_step, 1)
                dve.wait_ge(dve_step, 1)
                dve.sem_inc(dve_step, -1)
                dve.wait_ge(wa_loaded, 16 * (4 * KC + 2))
                dve.sem_inc(wa_loaded, -(16 * (4 * KC + 2)))
                for k in range(KC):
                    low = [wraw[:, (2 * k + j) * H * R:(2 * k + j + 1) * H * R].rearrange("p (h d) -> p h d", h=H)
                           for j in range(2)]
                    m_ = srl[:, 1, :].unsqueeze(2).to_broadcast([P, H, R])
                    n_ = srl[:, 0, :].unsqueeze(2).to_broadcast([P, H, R])
                    for j in range(2):
                        dve.tensor_tensor(wqk[:, k, j, :, 0:DS], wqk[:, k, j, :, 0:DS],
                                          sst[:, :].unsqueeze(2).to_broadcast([P, H, DS]), ALU.mult).then_inc(dve_step, 1)
                        dve.wait_ge(dve_step, 1)
                        dve.sem_inc(dve_step, -1)
                        dve.tensor_tensor(cm[:, j, 2, :].rearrange("p (h d) -> p h d", h=H), low[1 - j], m_, ALU.mult).then_inc(dve_step, 1)
                        dve.wait_ge(dve_step, 1)
                        dve.sem_inc(dve_step, -1)
                        dve.tensor_tensor(cm[:, j, 3, :].rearrange("p (h d) -> p h d", h=H), low[j], n_, ALU.mult).then_inc(dve_step, 1)
                        dve.wait_ge(dve_step, 1)
                        dve.sem_inc(dve_step, -1)
                        dve.tensor_tensor(wqk[:, k, j, :, DS:DH], cm[:, j, 2, :].rearrange("p (h d) -> p h d", h=H),
                                          cm[:, j, 3, :].rearrange("p (h d) -> p h d", h=H), ALU.add).then_inc(dve_step, 1)
                        dve.wait_ge(dve_step, 1)
                        dve.sem_inc(dve_step, -1)
                    dve.tensor_scalar(wqk[:, k, 0, :, :], wqk[:, k, 0, :, :], QSCALE, None, ALU.mult).then_inc(dve_step, 1)
                    dve.wait_ge(dve_step, 1)
                    dve.sem_inc(dve_step, -1)
                dve.wait_ge(wg_loaded, 16 * (6 * KC + 4))
                dve.sem_inc(wg_loaded, -(16 * (6 * KC + 4)))
                for a, c0 in enumerate((0, 32)):
                    dve.tensor_tensor(wg[:, 1, :, c0:c0 + H], wg[:, 1, :, c0:c0 + H],
                                      cm[:, a, 0, 0:KC * H].rearrange("p (k n) -> p k n", k=KC), ALU.add).then_inc(dve_step, 1)
                    dve.wait_ge(dve_step, 1)
                    dve.sem_inc(dve_step, -1)
                dve.sem_inc(wts_scaled, 1)

                def norm(n, src, dst, signal):
                    dve.bn_stats(st[n][:, :], src).then_inc(dve_step, 1)
                    dve.wait_ge(dve_step, 1)
                    dve.sem_inc(dve_step, -1)
                    dve.bn_aggr(mv[n][:, :], st[n][:, :]).then_inc((st0, st1, st2, st3)[n], 1)
                    dve.wait_ge((rs0, rs1, rs2, rs3)[n], 1)
                    dve.sem_inc((rs0, rs1, rs2, rs3)[n], -1)
                    dve.tensor_scalar(dst, src, mv[n][:, 0:1], rstd[n][:, 0:1], ALU.subtract, ALU.mult).then_inc(signal, 1)

                def flat(t):
                    return t[:, :, :].rearrange("p k t -> p (k t)")

                def a1():
                    dve.wait_ge(x_loaded, 16)
                    dve.sem_inc(x_loaded, -16)
                    norm(0, xt[:, :], kn[:, :], kn_ready)

                def a3():
                    dve.wait_ge(vT_ready, 1)
                    dve.sem_inc(vT_ready, -1)
                    dve.wait_ge(g_ready, 1)
                    dve.sem_inc(g_ready, -1)
                    dve.tensor_tensor(gv[:, :, :], gg[:, :, :], vT[:, :, :], ALU.mult).then_inc(dve_step, 1)
                    dve.wait_ge(dve_step, 1)
                    dve.sem_inc(dve_step, -1)
                    dve.wait_ge(c_ready, 1)
                    dve.sem_inc(c_ready, -1)
                    dve.tensor_tensor(cv[:, :, :], cc[:, :, :], vT[:, :, :], ALU.mult).then_inc(ctx_used, 1)
                    dve.tensor_tensor_scan(flat(sq_), flat(dtab), flat(gg), 0.0, ALU.mult, ALU.add)
                    dve.tensor_tensor_scan(flat(sp_), flat(dtab), flat(gv), 0.0, ALU.mult, ALU.add).then_inc(dve_step, 1)
                    dve.wait_ge(dve_step, 1)
                    dve.sem_inc(dve_step, -1)
                    dve.tensor_tensor(cc[:, :, 1:T], cc[:, :, 1:T], sq_[:, :, 0:T - 1], ALU.add)
                    dve.tensor_tensor(cv[:, :, 1:T], cv[:, :, 1:T], sp_[:, :, 0:T - 1], ALU.add).then_inc(dve_step, 1)
                    dve.wait_ge(dve_step, 1)
                    dve.sem_inc(dve_step, -1)
                    dve.reciprocal(rden[:, :, :], cc[:, :, :]).then_inc(dve_step, 1)
                    dve.wait_ge(dve_step, 1)
                    dve.sem_inc(dve_step, -1)
                    dve.tensor_tensor(yy[:, :, :], cv[:, :, :], rden[:, :, :], ALU.mult).then_inc(y_ready, 1)

                def a4():
                    dve.wait_ge(yT_ps, 1)
                    dve.sem_inc(yT_ps, -1)
                    dve.tensor_tensor(x1[:, :], xt[:, :], ps[:, 2, :], ALU.add).then_inc(dve_step, 1)
                    dve.wait_ge(dve_step, 1)
                    dve.sem_inc(dve_step, -1)
                    dve.sem_inc(x_free, 1)
                    norm(1, x1[:, :], xn[:, :], xn_ready)

                def a5():
                    dve.wait_ge(q_ps, 1)
                    dve.sem_inc(q_ps, -1)
                    dve.tensor_copy(flat(qs), ps[:, 0, :]).then_inc(q_ready, 1)

                def row_max(r):
                    dve.wait_ge(s_ps, 1)
                    dve.sem_inc(s_ps, -1)
                    bank = (3, 0, 1, 3)[r]
                    dve.tensor_reduce(nm[:, r, :], ps[:, bank, :].rearrange("p (c t) -> p c t", c=4), AX.X, ALU.max,
                                      negate=True).then_inc(nm_ready, 1)

                def pT_copy(r):
                    dve.wait_ge(pT_ps_dve, 1)
                    dve.sem_inc(pT_ps_dve, -1)
                    bank = (2, 0, 1, 3)[r]
                    dve.tensor_copy(pT[:, r, :, :].rearrange("p c t -> p (c t)"), ps[:, bank, :]).then_inc(pT_ready_dve, 1)

                def a6():
                    row_max(0)
                    row_max(1)
                    row_max(2)
                    pT_copy(0)
                    row_max(3)
                    pT_copy(2)

                def a7():
                    dve.wait_ge(o_ps, 1)
                    dve.sem_inc(o_ps, -1)
                    dve.reciprocal(rinv[:, :, :], rsum[:, :, :]).then_inc(dve_step, 1)
                    dve.wait_ge(dve_step, 1)
                    dve.sem_inc(dve_step, -1)
                    dve.tensor_tensor(on[:, :].rearrange("p (c r d) -> p r c d", c=4, r=4),
                                      ps[:, 2, :].rearrange("p (c r d) -> p r c d", c=4, r=4),
                                      rinv[:, :, :].unsqueeze(3).to_broadcast([P, 4, 4, DH]), ALU.mult).then_inc(on_ready, 1)
                    dve.wait_ge(att_ps, 1)
                    dve.sem_inc(att_ps, -1)
                    dve.tensor_tensor(x2[:, :], x1[:, :], ps[:, 1, :], ALU.add).then_inc(dve_step, 1)
                    dve.wait_ge(dve_step, 1)
                    dve.sem_inc(dve_step, -1)

                def c1():
                    norm(2, x2[:, :], qn[:, :], qn_ready)

                def c2():
                    dve.wait_ge(lf_parts, 1)
                    dve.sem_inc(lf_parts, -1)
                    dve.scalar_tensor_tensor(lf[:, :], fg[:, :], 0.0, fl[:, :], ALU.min, ALU.subtract).then_inc(dve_step, 1)
                    dve.wait_ge(dve_step, 1)
                    dve.sem_inc(dve_step, -1)
                    dve.tensor_tensor_scan(cum[:, :], onesf[0:H, :], lf[:, :], 0.0, ALU.mult, ALU.add).then_inc(dve_step, 1)
                    dve.wait_ge(dve_step, 1)
                    dve.sem_inc(dve_step, -1)
                    dve.tensor_tensor(ar[32:32 + H, :], ig[:, :], cum[:, :], ALU.subtract).then_inc(dve_step, 1)
                    dve.wait_ge(dve_step, 1)
                    dve.sem_inc(dve_step, -1)
                    dve.tensor_tensor_scan(cmx[:, :], onesf[32:32 + H, :], ar[32:32 + H, :], -3.0e38, ALU.mult, ALU.max).then_inc(dve_step, 1)
                    dve.wait_ge(dve_step, 1)
                    dve.sem_inc(dve_step, -1)
                    dve.tensor_scalar(ncmx[:, :], cmx[:, :], -1.0, None, ALU.mult).then_inc(m_ready, 1)
                    dve.tensor_tensor(fm[:, :], cum[:, :], cmx[:, :], ALU.add).then_inc(dve_step, 1)
                    dve.wait_ge(dve_step, 1)
                    dve.sem_inc(dve_step, -1)
                    dve.tensor_scalar(fm[:, :], fm[:, :], -86.0, None, ALU.max).then_inc(fm_ready, 1)

                def c3():
                    dve.wait_ge(nT_ps, 1)
                    dve.sem_inc(nT_ps, -1)
                    dve.tensor_copy(enT[:, :], ps[:, 7, 0:H]).then_inc(enT_done, 1)
                    for r in range(4):
                        dve.wait_ge(d_ready, 1)
                        dve.sem_inc(d_ready, -1)
                        dve.wait_ge(qk_ps, 1)
                        dve.sem_inc(qk_ps, -1)
                        dve.scalar_tensor_tensor(cm[:, r, :, :].rearrange("p c t -> p (c t)"), ps[:, (5, 7)[r % 2], :], QSCALE,
                                                 dm[:, r, :, :].rearrange("p c t -> p (c t)"), ALU.mult, ALU.mult)\
                           .then_inc(cm_ready, 1)

                def wide(t, n):
                    return t[:, :].unsqueeze(2).to_broadcast([P, H, n])

                def c5():
                    dve.wait_ge(hu_ps, 1)
                    dve.sem_inc(hu_ps, -1)
                    dve.sem_inc(cd_ctx_free, 1)
                    raw = ps[:, 4:6, 0:8 * (DH + 1)].rearrange("p b (h e) -> p b h e", e=DH + 1)
                    half = [t[:, :].rearrange("p (b h) -> p b h", b=2) for t in (nrm, nrm2, enT)]
                    dve.scalar_tensor_tensor(half[0], raw[:, :, :, DH], -1.0, half[2], ALU.mult, ALU.max).then_inc(dve_step, 1)
                    dve.wait_ge(dve_step, 1)
                    dve.sem_inc(dve_step, -1)
                    dve.tensor_tensor(half[1], half[0], raw[:, :, :, DH], ALU.max).then_inc(dve_step, 1)
                    dve.wait_ge(dve_step, 1)
                    dve.sem_inc(dve_step, -1)
                    dve.tensor_scalar(nrm[:, :], nrm2[:, :], 1e-6, None, ALU.add).then_inc(dve_step, 1)
                    dve.wait_ge(dve_step, 1)
                    dve.sem_inc(dve_step, -1)
                    dve.reciprocal(rn[:, :], nrm[:, :]).then_inc(dve_step, 1)
                    dve.wait_ge(dve_step, 1)
                    dve.sem_inc(dve_step, -1)
                    dve.tensor_tensor(hh[:, :, :].rearrange("p (b h) d -> p b h d", b=2), raw[:, :, :, 0:DH],
                                      rn[:, :].rearrange("p (b h) -> p b h", b=2).unsqueeze(3).to_broadcast([P, 2, 8, DH]),
                                      ALU.mult).then_inc(dve_step, 1)
                    dve.wait_ge(dve_step, 1)
                    dve.sem_inc(dve_step, -1)
                    dve.tensor_reduce(hmu[:, :], hh[:, :, :], AX.X, ALU.add).then_inc(dve_step, 1)
                    dve.wait_ge(dve_step, 1)
                    dve.sem_inc(dve_step, -1)
                    dve.tensor_scalar(hmu2[:, :], hmu[:, :], 1.0 / DH, None, ALU.mult).then_inc(dve_step, 1)
                    dve.wait_ge(dve_step, 1)
                    dve.sem_inc(dve_step, -1)
                    dve.tensor_tensor(hc[:, :, :], hh[:, :, :], wide(hmu2, DH), ALU.subtract).then_inc(hc_ready, 1)
                    dve.wait_ge(hsq_ready, 1)
                    dve.sem_inc(hsq_ready, -1)
                    dve.tensor_reduce(hvar[:, :], hsq[:, :, :], AX.X, ALU.add).then_inc(hvar_ready, 1)
                    dve.wait_ge(hrs_ready, 1)
                    dve.sem_inc(hrs_ready, -1)
                    dve.tensor_tensor(hn[:, :, :], hc[:, :, :], wide(hrs, DH), ALU.mult).then_inc(hn_ready, 1)

                def d1(i):
                    dve.wait_ge(x3_ready, 1)
                    dve.sem_inc(x3_ready, -1)
                    dve.sem_inc(x3_go, 1)
                    norm(3, x3[:, :], zn[:, :], zn_ready)
                    dve.wait_ge(rl_ps, 1)
                    dve.sem_inc(rl_ps, -1)
                    dve.tensor_reduce(nmx[:, :], ps[:, 7, 0:E], AX.X, ALU.max, negate=True).then_inc(nmx_ready, 1)
                    dve.wait_ge(er_ready, 1)
                    dve.sem_inc(er_ready, -1)
                    dve.max(top[:, :], er[:, :]).then_inc(dve_step, 1)
                    dve.wait_ge(dve_step, 1)
                    dve.sem_inc(dve_step, -1)
                    dve.match_replace(er2[:, :], top[:, :], er[:, :], -1.0).then_inc(dve_step, 1)
                    dve.wait_ge(dve_step, 1)
                    dve.sem_inc(dve_step, -1)
                    dve.tensor_scalar(sel[:, :], er2[:, :], 0.0, None, ALU.is_lt)
                    dve.tensor_scalar(selb[:, :], er2[:, :], 0.0, None, ALU.is_lt).then_inc(sel_ready, 1)
                    dve.tensor_reduce(s8[:, :], top[:, :], AX.X, ALU.add).then_inc(dve_step, 1)
                    dve.wait_ge(dve_step, 1)
                    dve.sem_inc(dve_step, -1)
                    dve.reciprocal(r8[:, :], s8[:, :]).then_inc(dve_step, 1)
                    dve.wait_ge(dve_step, 1)
                    dve.sem_inc(dve_step, -1)
                    dve.scalar_tensor_tensor(wsel[:, :], er[:, :], r8[:, :], sel[:, :], ALU.mult, ALU.mult).then_inc(dve_step, 1)
                    dve.wait_ge(dve_step, 1)
                    dve.sem_inc(dve_step, -1)
                    dve.wait_ge(pos_ps, 1)
                    dve.sem_inc(pos_ps, -1)
                    dve.scalar_tensor_tensor(wc[:, bass.ds(i, 1), :].rearrange("p a e -> p (a e)"), ps[:, 7, 64:64 + E],
                                             float(CAP), wsel[:, :], ALU.is_lt, ALU.mult)
                    dve.tensor_tensor(selacc[:, :], selacc[:, :], selb[:, :], ALU.add).then_inc(dve_step, 1)
                    dve.wait_ge(dve_step, 1)
                    dve.sem_inc(dve_step, -1)

                a1()
                a3()
                a4()
                a5()
                a6()
                a7()
                with dve.Fori(1, nb) as i:
                    c1()
                    a1()
                    c2()
                    c3()
                    a3()
                    a4()
                    c5()
                    a5()
                    d1(i - 1)
                    a6()
                    a7()
                c1()
                c2()
                c3()
                c5()
                d1(nb - 1)

        with ExitStack() as ctx:
            def sb(name, shape, dt=F32):
                return ctx.enter_context(nc.sbuf_tensor(name, shape, dt))

            TOK = nb * T
            NG = TOK // 512
            xT = sb("xT", [P, KC, TOK])
            acc = sb("acc", [P, nb, D])
            wgu = sb("wgu", [P, 2, KC, 2 * INTER])
            wd1 = sb("wd1", [P, 2, D])
            wd2 = sb("wd2", [I2, 2, D])
            s1 = sb("s1", [P, 2, 512])
            s2 = sb("s2", [I2, 2, 512])
            h1 = sb("h1", [P, 2, 512])
            h2 = sb("h2", [I2, 2, 512])
            wcol = sb("wcol", [P, 2, nb])
            xT_loaded = sem("xT_loaded")
            acc_loaded = sem("acc_loaded")
            w_loaded0 = sem("w_loaded0")
            w_loaded1 = sem("w_loaded1")
            w_free0 = sem("w_free0")
            w_free1 = sem("w_free1")
            gu_ps = sem("gu_ps")
            s_ready = sem("s_ready")
            h_ready = sem("h_ready")
            o_ps2 = sem("o_ps2")
            o_free0 = sem("o_free0")
            o_free1 = sem("o_free1")
            wcol_step = sem("wcol_step")
            experts_done = sem("experts_done")
            stored = sem("stored")
            w_loaded = (w_loaded0, w_loaded1)
            w_free = (w_free0, w_free1)
            o_free = (o_free0, o_free1)
            block2 = ctx.enter_context(nc.Block())

            @block2.sync
            def _(sp):
                def load(e, j):
                    for src, c1_, c2_ in ((w_gate, 0, 2 * P), (w_up, P, 2 * P + I2)):
                        v_ = src[bass.ds(e, 1)].rearrange("a (k p) n -> p (a k) n", p=P)
                        sp.dma_start(wgu[:, j, :, c1_:c1_ + P], v_[:, :, 0:P]).then_inc(w_loaded[j], 16)
                        sp.dma_start(wgu[:, j, :, c2_:c2_ + I2], v_[:, :, P:INTER]).then_inc(w_loaded[j], 16)
                    v_ = w_down[bass.ds(e, 1)].rearrange("a i d -> (a i) d")
                    sp.dma_start(wd1[:, j, :], v_[0:P, :]).then_inc(w_loaded[j], 16)
                    sp.dma_start(wd2[:, j, :], v_[P:INTER, :]).then_inc(w_loaded[j], 16)

                load(0, 0)
                for k in range(KC):
                    sp.dma_start(xT[:, k, :], xT_d[:, k, 0:TOK]).then_inc(xT_loaded, 16)
                sp.dma_start(acc[:, :, :], x3_d[0:nb].rearrange("b p d -> p b d")).then_inc(acc_loaded, 16)
                load(1, 1)
                with sp.Fori(1, ne // 2) as i:
                    for j in range(2):
                        sp.wait_ge(w_free[j], 1)
                        sp.sem_inc(w_free[j], -1)
                        load(2 * i + j, j)
                for j in range(2):
                    sp.wait_ge(w_free[j], 1)
                    sp.sem_inc(w_free[j], -1)
                sp.wait_ge(experts_done, 1)
                sp.sem_inc(experts_done, -1)
                for g in range(8):
                    n = nb // 8
                    sp.dma_start(out[g * n:(g + 1) * n].rearrange("b p d -> p b d"), acc[:, g * n:(g + 1) * n, :])\
                      .then_inc(stored, 16)
                sp.wait_ge(stored, 16 * 8)

            @block2.gpsimd
            def _(pool):
                pass

            @block2.tensor
            def _(pe):
                def gate_up(g):
                    j, n, q = g // NG, g % NG, g % 2
                    for m_ in range(3):
                        for k in range(KC):
                            m = pe.matmul(ps[:, 3 * q + m_, :], wgu[:, j, k, m_ * P:(m_ + 1) * P],
                                          xT[:, k, n * 512:(n + 1) * 512], start=(k == 0), stop=(k == KC - 1))
                    m.then_inc(gu_ps, 1)

                def down(g):
                    j, q = g // NG, g % 2
                    pe.wait_ge(h_ready, 1)
                    pe.sem_inc(h_ready, -1)
                    for t in range(4):
                        pe.wait_ge(o_free[t % 2], 1)
                        pe.sem_inc(o_free[t % 2], -1)
                        pe.matmul(ps[:, 6 + t % 2, :], h1[:, q, t * P:(t + 1) * P], wd1[:, j, :], start=True, stop=False)
                        pe.matmul(ps[:, 6 + t % 2, :], h2[:, q, t * P:(t + 1) * P], wd2[:, j, :], start=False, stop=True)\
                          .then_inc(o_ps2, 1)

                pe.sem_inc(o_free[0], 1)
                pe.sem_inc(o_free[1], 1)
                pe.wait_ge(xT_loaded, 16 * KC)
                pe.sem_inc(xT_loaded, -(16 * KC))
                with pe.Fori(0, ne // 2):
                    pe.wait_ge(w_loaded[0], 96)
                    pe.sem_inc(w_loaded[0], -96)
                    gate_up(0)
                    for g in range(2 * NG):
                        if g == NG - 1:
                            pe.wait_ge(w_loaded[1], 96)
                            pe.sem_inc(w_loaded[1], -96)
                        if g < 2 * NG - 1:
                            gate_up(g + 1)
                        down(g)

            @block2.scalar
            def _(act):
                with act.Fori(0, ne // 2):
                    for g in range(2 * NG):
                        q = g % 2
                        act.wait_ge(gu_ps, 1)
                        act.sem_inc(gu_ps, -1)
                        act.activation(s1[:, q, :], ps[:, 3 * q, :], ACT.Silu)
                        act.activation(s2[:, q, :], ps[0:I2, 3 * q + 2, :], ACT.Silu).then_inc(s_ready, 1)

            @block2.vector
            def _(dve):
                def hidden(g):
                    q = g % 2
                    dve.wait_ge(s_ready, 1)
                    dve.sem_inc(s_ready, -1)
                    dve.tensor_tensor(h1[:, q, :], s1[:, q, :], ps[:, 3 * q + 1, :], ALU.mult)
                    dve.tensor_tensor(h2[:, q, :], s2[:, q, :], ps[I2:2 * I2, 3 * q + 2, :], ALU.mult).then_inc(h_ready, 1)

                def combine(g):
                    j, n = g // NG, g % NG
                    for t in range(4):
                        b = 4 * n + t
                        dve.wait_ge(o_ps2, 1)
                        dve.sem_inc(o_ps2, -1)
                        a = dve.scalar_tensor_tensor(acc[:, b, :], ps[:, 6 + t % 2, :], wcol[:, j, b:b + 1], acc[:, b, :],
                                                     ALU.mult, ALU.add)
                        a.then_inc(o_free[t % 2], 1)
                    if g % NG == NG - 1:
                        dve.sem_inc(w_free[j], 1)

                dve.wait_ge(acc_loaded, 16)
                dve.sem_inc(acc_loaded, -16)
                with dve.Fori(0, ne // 2) as i:
                    for j in range(2):
                        a = dve.tensor_copy(wcol[:, j, :], wc[:, 0:nb, bass.ds(2 * i + j, 1)].rearrange("p b e -> p (b e)"))
                    a.then_inc(wcol_step, 1)
                    dve.wait_ge(wcol_step, 1)
                    dve.sem_inc(wcol_step, -1)
                    hidden(0)
                    for g in range(2 * NG):
                        if g < 2 * NG - 1:
                            hidden(g + 1)
                        combine(g)
                    dve.drain().then_inc(wcol_step, 1)
                    dve.wait_ge(wcol_step, 1)
                    dve.sem_inc(wcol_step, -1)
                dve.drain().then_inc(experts_done, 1)


_INS = ['x', 'ctx_2048', 'L0_xattn_w', 'L0_xattn_u', 'L0_ffn_Wa', 'L0_ffn_Wp', 'L0_ffn_w_std', 'L0_ffn_w_rec',
        'L1_xattn_Wi', 'L1_xattn_bi', 'L1_xattn_Wf', 'L1_xattn_bf', 'L1_xattn_ln_scale', 'L1_ffn_gate_w',
        'L1_ffn_w_gate', 'L1_ffn_w_up', 'L1_ffn_w_down']


def kernel(**inputs):
    import numpy as _np
    import concourse.bacc as _bacc
    from concourse import mybir as _mybir
    from concourse.bass_utils import run_bass_kernel_spmd as _run

    nc = _bacc.Bacc("TRN2", target_bir_lowering=False, num_devices=1)
    arrays, args = {}, []
    for name in _INS:
        a = _np.ascontiguousarray(inputs[name])
        arrays[f"in_{name}_dram"] = a
        args.append(nc.dram_tensor(f"in_{name}_dram", a.shape, _mybir.dt.from_np(a.dtype), kind="ExternalInput").ap())
    out = nc.dram_tensor("out_0_dram", (32, 128, 512), _mybir.dt.float32, kind="ExternalOutput").ap()
    build(nc, *args, out)
    r = _run(nc, [arrays], core_ids=[0])
    return r.results[0]["out_0_dram"]
```

```python
from contextlib import ExitStack

import concourse.bass as bass
from concourse import mybir

F32 = mybir.dt.float32
BF16 = mybir.dt.bfloat16
F16 = mybir.dt.float16
U32 = mybir.dt.uint32
ALU = mybir.AluOpType
ACT = mybir.ActivationFunctionType
AX = mybir.AxisListType

P = 128
NEG = -1.0e30
K_SHIFT = 16.0
ROUND = 1.5 * 2.0 ** 23
U_CAP = 70.0


def build(nc, x, ctx_in, w, u, Wa, Wp, w_std, w_rec, Wi, bi, Wf, bf, ln_scale, gate_w, w_gate, w_up,
          w_down, out, NB=None, NE=None):
    B, T, D = x.shape
    H = w_std.shape[0]
    R = 8
    DH = D // H
    DS = DH - R
    KC = D // P
    E = gate_w.shape[1]
    INTER = w_gate.shape[2]
    I2 = INTER - P
    CAP = 2 * (B * T * 8 // E)
    assert T == P and H == 16 and DH == 32 and KC == 4 and E == 32 and INTER == 192
    nb, ne = NB or B, NE or E
    THRESH = 0.1
    QSCALE = float(DH) ** -0.5

    TOK = B * T
    GROUP = 2 * P
    SLOTS = E * CAP
    COLS = SLOTS // P
    WSC = 256.0
    acc_d = nc.dram_tensor("acc_scratch", [TOK + GROUP, D], F32, kind="Internal").ap()
    z_d = nc.dram_tensor("z_scratch", [TOK + GROUP, D], F32, kind="Internal").ap()
    slot_d = nc.dram_tensor("slot_scratch", [SLOTS + P, 2], U32, kind="Internal").ap()

    with ExitStack() as whole:
        def sem(name):
            return whole.enter_context(nc.semaphore(name))

        def sbw(name, shape, dt=F32):
            return whole.enter_context(nc.sbuf_tensor(name, shape, dt))

        ps = whole.enter_context(nc.psum_tensor("ps", [P, 8, 512], F32))
        counts = sbw("counts", [P, E], U32)

        with ExitStack() as ctx:
            def sb(name, shape, dt=F32):
                return ctx.enter_context(nc.sbuf_tensor(name, shape, dt))

            ident = sb("ident", [P, P])
            identb = sb("identb", [P, P], BF16)
            onesf = sb("onesf", [P, P])
            onesb = sb("onesb", [P, P], BF16)
            ustrict = sb("ustrict", [P, P], BF16)
            mask_ts = sb("mask_ts", [P, 4, P], BF16)
            mask_st = sb("mask_st", [P, 4, P], BF16)
            zerob = sb("zerob", [P, 4, P], BF16)
            ind = sb("ind", [H, 4, 4])
            steps = sb("steps", [P, T])
            eps5 = sb("eps5", [P, 1])
            eps6 = sb("eps6", [P, 1])
            nshift = sb("nshift", [P, 1])
            wch = sb("wch", [P, KC])
            uch = sb("uch", [P, KC])
            wpos = sb("wpos", [P, KC])
            nwpos = sb("nwpos", [P, KC])
            wneg = sb("wneg", [P, KC])
            decay = sb("decay", [P, KC])
            uw = sb("uw", [P, KC])
            dtab = sb("dtab", [P, KC, T])
            gam = sb("gam", [P, KC, T])
            zc = sb("zc", [P, KC, T])
            hs_ = sb("hs_", [P, 3, H])
            sst = sb("sst", [P, H])
            srl = sb("srl", [P, 4, H])
            wqk = sb("wqk", [P, KC, 2, H, DH])
            wv = sb("wv", [P, KC, D])
            wp = sb("wp", [P, KC, D])
            wg = sb("wg", [P, 2, KC, 48])
            gbias = sb("gbias", [48, 1])
            lnsc = sb("lnsc", [P, D])
            gw = sb("gw", [P, KC, E])
            xt = sb("xt", [P, D])
            ct = sb("ct", [P, D])
            st = [sb(f"st{n}", [P, 6]) for n in range(4)]
            mv = [sb(f"mv{n}", [P, 2]) for n in range(4)]
            lnv = [sb(f"lnv{n}", [P, 1]) for n in range(4)]
            rstd = [sb(f"rstd{n}", [P, 1]) for n in range(4)]
            kn = sb("kn", [P, D])
            ex = sb("ex", [P, KC, T])
            vT = sb("vT", [P, KC, T])
            gg = sb("gg", [P, KC, T])
            cc = sb("cc", [P, KC, T])
            gv = sb("gv", [P, KC, T])
            cv = sb("cv", [P, KC, T])
            sq_ = sb("sq_", [P, KC, T])
            sp_ = sb("sp_", [P, KC, T])
            rden = sb("rden", [P, KC, T])
            yy = sb("yy", [P, KC, T])
            x1 = sb("x1", [P, D])
            xn = sb("xn", [P, D])
            xnT = sb("xnT", [P, KC, T])
            qs = sb("qs", [P, KC, T])
            ks = sb("ks", [P, KC, T])
            vs = sb("vs", [P, D])
            nm = sb("nm", [P, 4, 4])
            rsum = sb("rsum", [P, 4, 4])
            rinv = sb("rinv", [P, 4, 4])
            pr = sb("pr", [P, 4, 4, T])
            pT = sb("pT", [P, 4, 4, T])
            on = sb("on", [P, D])
            oT = sb("oT", [P, KC, T])
            x2 = sb("x2", [P, D])
            qn = sb("qn", [P, D])
            qT = sb("qT", [P, KC, T])
            kT2 = sb("kT2", [P, KC, T])
            vaug = sb("vaug", [P, H, DH + 1])
            ig = sb("ig", [H, T])
            fg = sb("fg", [H, T])
            fa = sb("fa", [H, T])
            fe = sb("fe", [H, T])
            fl = sb("fl", [H, T])
            lf = sb("lf", [H, T])
            cum = sb("cum", [H, T])
            cmx = sb("cmx", [H, T])
            ncmx = sb("ncmx", [H, T])
            fm = sb("fm", [H, T])
            efm = sb("efm", [H, T])
            ar = sb("ar", [48, T])
            bd = sb("bd", [48, 4, 4, T])
            dm = sb("dm", [P, 4, 4, T])
            cm = sb("cm", [P, 4, 4, T])
            enT = sb("enT", [P, H])
            nrm = sb("nrm", [P, H])
            nrm2 = sb("nrm2", [P, H])
            rn = sb("rn", [P, H])
            hh = sb("hh", [P, H, DH])
            hmu = sb("hmu", [P, H])
            hmu2 = sb("hmu2", [P, H])
            hc = sb("hc", [P, H, DH])
            hsq = sb("hsq", [P, H, DH])
            hvar = sb("hvar", [P, H])
            hlv = sb("hlv", [P, H])
            hrs = sb("hrs", [P, H])
            hn = sb("hn", [P, H, DH])
            hw = sb("hw", [P, D])
            x3 = sb("x3", [P, D])
            zn = sb("zn", [P, D])
            zT = sb("zT", [P, KC, T])
            nmx = sb("nmx", [P, 1])
            er = sb("er", [P, E])
            top = sb("top", [P, 8])
            er2 = sb("er2", [P, E])
            sel = sb("sel", [P, E])
            selb = sb("selb", [P, E], BF16)
            selacc = sb("selacc", [P, E], BF16)
            s8 = sb("s8", [P, 1])
            r8 = sb("r8", [P, 1])
            wsel = sb("wsel", [P, E])
            slot1 = sb("slot1", [P, E])
            trash = sb("trash", [P, 1])
            tok_f = sb("tok_f", [P, 1])
            kept = sb("kept", [P, E])
            key = sb("key", [P, E])
            key2 = sb("key2", [P, E])
            key3 = sb("key3", [P, E])
            keys = sb("keys", [P, 8])
            miss = sb("miss", [P, 8])
            slots = sb("slots", [P, 8], U32)
            junk = sb("junk", [P, E])
            pair = sb("pair", [P, 8, 2], U32)
            cntf = sb("cntf", [P, E])
            zero = sb("zero", [P, 2 * D])

            wa_loaded = sem("wa_loaded")
            wg_loaded = sem("wg_loaded")
            small_loaded = sem("small_loaded")
            const_ready = sem("const_ready")
            tabs_ready = sem("tabs_ready")
            act_step = sem("act_step")
            dve_step = sem("dve_step")
            pool_step = sem("pool_step")
            x_loaded = sem("x_loaded")
            ctx_loaded = sem("ctx_loaded")
            x_free = sem("x_free")
            ct_free = sem("ct_free")
            st0 = sem("st0")
            st1 = sem("st1")
            st2 = sem("st2")
            st3 = sem("st3")
            rs0 = sem("rs0")
            rs1 = sem("rs1")
            rs2 = sem("rs2")
            rs3 = sem("rs3")
            kn_ready = sem("kn_ready")
            kT_ps = sem("kT_ps")
            cT_ps = sem("cT_ps")
            e_ready = sem("e_ready")
            g_ready = sem("g_ready")
            c_ready = sem("c_ready")
            vT_ready = sem("vT_ready")
            ctx_used = sem("ctx_used")
            y_ready = sem("y_ready")
            yT_ps = sem("yT_ps")
            xn_ready = sem("xn_ready")
            xnT_ps = sem("xnT_ps")
            xnT_ready = sem("xnT_ready")
            q_ps = sem("q_ps")
            k_ps = sem("k_ps")
            v_ps = sem("v_ps")
            q_ready = sem("q_ready")
            k_ready = sem("k_ready")
            v_ready = sem("v_ready")
            s_ps = sem("s_ps")
            nm_ready = sem("nm_ready")
            p_ready = sem("p_ready")
            pT_ps_dve = sem("pT_ps_dve")
            pT_ps_act = sem("pT_ps_act")
            pT_ready_dve = sem("pT_ready_dve")
            pT_ready_act = sem("pT_ready_act")
            o_ps = sem("o_ps")
            on_ready = sem("on_ready")
            oT_ps = sem("oT_ps")
            oT_ready = sem("oT_ready")
            att_ps = sem("att_ps")
            cd_ctx_free = sem("cd_ctx_free")
            cd_ctx_ready = sem("cd_ctx_ready")
            qn_ready = sem("qn_ready")
            qT_ps = sem("qT_ps")
            qT_ready = sem("qT_ready")
            g_ps = sem("g_ps")
            lf_parts = sem("lf_parts")
            m_ready = sem("m_ready")
            fm_ready = sem("fm_ready")
            efm_ready = sem("efm_ready")
            nT_ps = sem("nT_ps")
            enT_done = sem("enT_done")
            bd_ready = sem("bd_ready")
            l_ps = sem("l_ps")
            d_ready = sem("d_ready")
            qk_ps = sem("qk_ps")
            cm_ready = sem("cm_ready")
            hu_ps = sem("hu_ps")
            hc_ready = sem("hc_ready")
            hsq_ready = sem("hsq_ready")
            hvar_ready = sem("hvar_ready")
            hrs_ready = sem("hrs_ready")
            hn_ready = sem("hn_ready")
            x3_ready = sem("x3_ready")
            x3_go = sem("x3_go")
            x3_stored = sem("x3_stored")
            zn_ready = sem("zn_ready")
            zT_ps = sem("zT_ps")
            zT_ready = sem("zT_ready")
            zn_stored = sem("zn_stored")
            scratch_set = sem("scratch_set")
            pairs_ready = sem("pairs_ready")
            pairs_stored = sem("pairs_stored")
            pairs_free = sem("pairs_free")
            cnt_ps = sem("cnt_ps")
            rl_ps = sem("rl_ps")
            nmx_ready = sem("nmx_ready")
            er_ready = sem("er_ready")
            sel_ready = sem("sel_ready")
            pos_ps = sem("pos_ps")
            wts_scaled = sem("wts_scaled")
            masks_ready = sem("masks_ready")
            zeros_ready = sem("zeros_ready")
            tab_parts = sem("tab_parts")
            scale_parts = sem("scale_parts")
            srs_ready = sem("srs_ready")

            blank = pr[:, :, :, :].rearrange("p a b t -> p (a b t)")[:, 0:2 * SLOTS // P].bitcast(U32)
            wraw = dm[:, :, :, :].rearrange("p a b t -> p (a b t)")
            block = ctx.enter_context(nc.Block())

            @block.sync
            def _(sp):
                sp.dma_start(wch[:, :], w.rearrange("(k p) -> p k", p=P), allow_slow_non_contiguous=True).then_inc(small_loaded, 16)
                sp.dma_start(uch[:, :], u.rearrange("(k p) -> p k", p=P), allow_slow_non_contiguous=True).then_inc(small_loaded, 16)
                sp.dma_start(hs_[:, 0, :], w_std.partition_broadcast(P)).then_inc(small_loaded, 16)
                sp.dma_start(hs_[:, 1, :], w_rec.partition_broadcast(P)).then_inc(small_loaded, 16)
                sp.dma_start(xt[:, :], x[0]).then_inc(x_loaded, 16)
                sp.dma_start(ct[:, :], ctx_in[0]).then_inc(ctx_loaded, 16)
                wa_v = Wa.rearrange("(k p) n -> p k n", p=P)
                q_end, k_end, v_end, ql_end = H * DS, 2 * H * DS, 2 * H * DS + D, 2 * H * DS + D + H * R
                for k in range(KC):
                    for j, (c0, l0) in enumerate([(0, v_end), (q_end, ql_end)]):
                        sp.dma_start(wqk[:, k, j, :, 0:DS],
                                     wa_v[:, k, c0:c0 + H * DS].rearrange("p (h d) -> p h d", h=H)).then_inc(wa_loaded, 16)
                        sp.dma_start(wraw[:, (2 * k + j) * H * R:(2 * k + j + 1) * H * R],
                                     wa_v[:, k, l0:l0 + H * R]).then_inc(wa_loaded, 16)
                sp.dma_start(wv[:, :, :], wa_v[:, :, k_end:v_end]).then_inc(wa_loaded, 16)
                sp.dma_start(wp[:, :, :], Wp.rearrange("(k p) n -> p k n", p=P)).then_inc(wa_loaded, 16)
                sp.wait_ge(zeros_ready, 1)
                sp.sem_inc(zeros_ready, -1)
                for t_ in (acc_d, z_d):
                    sp.dma_start(t_[TOK:TOK + GROUP, :].rearrange("(p a) d -> p (a d)", p=P), zero[:, :])\
                      .then_inc(scratch_set, 16)
                sp.dma_start(slot_d[0:SLOTS, :].rearrange("(p s) c -> p (s c)", p=P), blank)\
                  .then_inc(scratch_set, 16)
                sp.wait_ge(masks_ready, 1)
                sp.sem_inc(masks_ready, -1)
                for a, (W_, c0) in enumerate([(Wi, 0), (Wf, 32)]):
                    v_ = W_.rearrange("(j k p) n -> p j k n", j=3, p=P)
                    for k in range(KC):
                        sp.dma_start(wg[:, 0, k, c0:c0 + H], v_[:, 0, k, :]).then_inc(wg_loaded, 16)
                        sp.dma_start(wg[:, 1, k, c0:c0 + H], v_[:, 1, k, :]).then_inc(wg_loaded, 16)
                        sp.dma_start(cm[:, a, 0, k * H:(k + 1) * H], v_[:, 2, k, :]).then_inc(wg_loaded, 16)
                sp.dma_start(gbias[0:H, :], bi.rearrange("(h a) -> h a", a=1)).then_inc(wg_loaded, 16)
                sp.dma_start(gbias[32:32 + H, :], bf.rearrange("(h a) -> h a", a=1)).then_inc(wg_loaded, 16)
                sp.dma_start(lnsc[:, :], ln_scale.partition_broadcast(P)).then_inc(wg_loaded, 16)
                sp.dma_start(gw[:, :, :], gate_w.rearrange("(k p) e -> p k e", p=P)).then_inc(wg_loaded, 16)

                def load(i):
                    sp.wait_ge(x_free, 1)
                    sp.sem_inc(x_free, -1)
                    sp.dma_start(xt[:, :], x[bass.ds(i, 1)].rearrange("a p d -> p (a d)")).then_inc(x_loaded, 16)
                    sp.wait_ge(ct_free, 1)
                    sp.sem_inc(ct_free, -1)
                    sp.dma_start(ct[:, :], ctx_in[bass.ds(i, 1)].rearrange("a p d -> p (a d)")).then_inc(ctx_loaded, 16)

                def store(i):
                    sp.wait_ge(x3_go, 1)
                    sp.sem_inc(x3_go, -1)
                    sp.dma_start(acc_d[bass.ds(i * P, P), :], x3[:, :]).then_inc(x3_stored, 16)

                with sp.Fori(1, nb) as i:
                    load(i)
                    store(i - 1)
                sp.wait_ge(x_free, 1)
                sp.sem_inc(x_free, -1)
                sp.wait_ge(ct_free, 1)
                sp.sem_inc(ct_free, -1)
                store(nb - 1)

            @block.gpsimd
            def _(pool):
                pool.memset(wg[:, :, :, :], 0.0).then_inc(masks_ready, 1)
                pool.memset(ident[:, :], 0.0)
                pool.memset(onesf[:, :], 1.0)
                pool.memset(onesb[:, :], 1.0)
                pool.memset(zerob[:, :, :], 0.0)
                pool.memset(eps5[:, :], 1e-5)
                pool.memset(eps6[:, :], 1e-6)
                pool.memset(nshift[:, :], -K_SHIFT)
                pool.memset(selacc[:, :], 0.0)
                pool.memset(ar[:, :], 0.0)
                pool.memset(ind[:, :, :], 0.0)
                pool.memset(bd[:, :, :, :], 0.0).then_inc(pool_step, 1)
                pool.wait_ge(pool_step, 1)
                pool.sem_inc(pool_step, -1)
                pool.memset(ar[0:H, :], 1.0)
                pool.affine_select(out=ident[:, :], in_=ident[:, :], compare_op=ALU.not_equal, fill=1.0, base=0,
                                   pattern=[[-1, P]], channel_multiplier=1)
                pool.affine_select(out=identb[:, :], in_=zerob[:, 0, :], compare_op=ALU.not_equal, fill=1.0, base=0,
                                   pattern=[[-1, P]], channel_multiplier=1)
                pool.affine_select(out=ustrict[:, :], in_=zerob[:, 0, :], compare_op=ALU.is_ge, fill=1.0, base=0,
                                   pattern=[[-1, P]], channel_multiplier=1)
                pool.affine_select(out=mask_ts[:, :, :], in_=zerob[:, :, :], compare_op=ALU.is_ge, fill=NEG, base=0,
                                   pattern=[[0, 4], [-1, P]], channel_multiplier=1)
                pool.affine_select(out=mask_st[:, :, :], in_=zerob[:, :, :], compare_op=ALU.is_ge, fill=NEG, base=0,
                                   pattern=[[0, 4], [1, P]], channel_multiplier=-1)
                pool.affine_select(out=ind[:, :, :], in_=ind[:, :, :], compare_op=ALU.not_equal, fill=1.0, base=0,
                                   pattern=[[-1, 4], [-4, 4]], channel_multiplier=1).then_inc(pool_step, 1)
                pool.wait_ge(pool_step, 1)
                pool.sem_inc(pool_step, -1)
                pool.affine_select(out=bd[32:32 + H, :, :, :], in_=bd[32:32 + H, :, :, :],
                                   compare_op=ALU.not_equal, fill=1.0, base=0,
                                   pattern=[[-1, 4], [-4, 4], [0, T]], channel_multiplier=1).then_inc(pool_step, 1)
                pool.wait_ge(pool_step, 1)
                pool.sem_inc(pool_step, -1)
                pool.iota(steps[:, :], pattern=[[1, T]], base=0, channel_multiplier=0,
                          allow_small_or_imprecise_dtypes=True).then_inc(pool_step, 1)
                pool.wait_ge(pool_step, 1)
                pool.sem_inc(pool_step, -1)
                pool.memset(zero[:, :], 0.0)
                pool.memset(blank, 0).then_inc(pool_step, 1)
                pool.wait_ge(pool_step, 1)
                pool.sem_inc(pool_step, -1)
                pool.iota(slot1[:, :], pattern=[[CAP // P, E]], base=1, channel_multiplier=0,
                          allow_small_or_imprecise_dtypes=True)
                pool.iota(trash[:, :], pattern=[[1, 1]], base=SLOTS + 1, channel_multiplier=1,
                          allow_small_or_imprecise_dtypes=True)
                pool.iota(tok_f[:, :], pattern=[[1, 1]], base=0, channel_multiplier=1,
                          allow_small_or_imprecise_dtypes=True)
                pool.iota(blank.bitcast(mybir.dt.int32).rearrange("p (a s c) -> p a s c", s=2, c=2)[:, :, :, 0],
                          pattern=[[0, COLS // 2], [P, 2]], base=TOK, channel_multiplier=1).then_inc(pool_step, 1)
                pool.wait_ge(pool_step, 1)
                pool.sem_inc(pool_step, -1)
                pool.sem_inc(zeros_ready, 1)
                pool.sem_inc(x3_stored, 16)
                pool.sem_inc(zn_stored, 16)
                pool.sem_inc(pairs_free, 1)
                pool.sem_inc(cd_ctx_free, 1)
                pool.sem_inc(const_ready, 3)

                def a3():
                    pool.wait_ge(e_ready, 1)
                    pool.sem_inc(e_ready, -1)
                    pool.tensor_tensor(gg[:, :, :], gam[:, :, :], ex[:, :, :], ALU.mult).then_inc(g_ready, 1)
                    pool.tensor_tensor(cc[:, :, :], zc[:, :, :], ex[:, :, :], ALU.mult).then_inc(c_ready, 1)

                def a7():
                    pool.wait_ge(ctx_used, 1)
                    pool.sem_inc(ctx_used, -1)
                    pool.wait_ge(cd_ctx_free, 1)
                    pool.sem_inc(cd_ctx_free, -1)
                    pool.tensor_copy(kT2[:, :, :], vT[:, :, :])
                    pool.tensor_copy(vaug[:, :, 0:DH], ct[:, :].rearrange("p (h d) -> p h d", h=H)).then_inc(ct_free, 1)
                    pool.memset(vaug[:, :, DH:DH + 1], 1.0).then_inc(cd_ctx_ready, 1)

                def c2():
                    pool.wait_ge(m_ready, 1)
                    pool.sem_inc(m_ready, -1)
                    pool.tensor_tensor(bd[0:H, :, :, :].rearrange("h r c t -> h (r c) t"),
                                       ind[:, :, :].rearrange("h r c -> h (r c)").unsqueeze(2).to_broadcast([H, 16, T]),
                                       ncmx[:, :].unsqueeze(1).to_broadcast([H, 16, T]), ALU.mult).then_inc(bd_ready, 1)

                def c5():
                    pool.wait_ge(hn_ready, 1)
                    pool.sem_inc(hn_ready, -1)
                    pool.tensor_tensor(hw[:, :], hn[:, :, :].rearrange("p h d -> p (h d)"), lnsc[:, :], ALU.mult).then_inc(pool_step, 1)
                    pool.wait_ge(pool_step, 1)
                    pool.sem_inc(pool_step, -1)
                    pool.wait_ge(x3_stored, 16)
                    pool.sem_inc(x3_stored, -16)
                    pool.tensor_tensor(x3[:, :], x2[:, :], hw[:, :], ALU.add).then_inc(x3_ready, 1)

                def d1():
                    pool.wait_ge(pairs_ready, 1)
                    pool.sem_inc(pairs_ready, -1)
                    for k in range(8):
                        pool.indirect_dma_start(out=slot_d[:, :], out_offset=bass.IndirectOffsetOnAxis(ap=slots[:, k:k + 1], axis=0),
                                                in_=pair[:, k, :], in_offset=None).then_inc(pairs_stored, 16)

                pool.wait_ge(tabs_ready, 1)
                pool.sem_inc(tabs_ready, -1)
                def pairs_done(n):
                    pool.wait_ge(pairs_stored, n * (16 * 8))
                    pool.sem_inc(pairs_free, 1)

                pool.wait_ge(scratch_set, 48)
                pool.sem_inc(scratch_set, -48)
                a3()
                a7()
                with pool.Fori(1, nb) as i:
                    c2()
                    a3()
                    c5()
                    d1()
                    a7()
                    pairs_done(i)
                c2()
                c5()
                d1()
                pairs_done(nb)
                pool.wait_ge(x3_stored, 16)
                pool.sem_inc(x3_stored, -16)

            @block.scalar
            def _(act):
                act.preload_act_table_set("natural_log_exp_and_others")
                act.wait_ge(const_ready, 1)
                act.sem_inc(const_ready, -1)
                act.wait_ge(tab_parts, 1)
                act.sem_inc(tab_parts, -1)
                act.activation(decay[:, :], wneg[:, :], ACT.Exp)
                for k in range(KC):
                    act.activation(gam[:, k, :], steps[:, :], ACT.Exp, scale=nwpos[:, k:k + 1])
                    a = act.activation(zc[:, k, :], zc[:, k, :], ACT.Exp)
                a.then_inc(scale_parts, 1)
                act.wait_ge(tab_parts, 1)
                act.sem_inc(tab_parts, -1)
                act.activation(srl[:, 0:2, :], hs_[:, 0:2, :], ACT.Ln).then_inc(act_step, 1)
                act.wait_ge(act_step, 1)
                act.sem_inc(act_step, -1)
                act.activation(srl[:, 2:4, :], srl[:, 0:2, :], ACT.Exp, scale=0.5).then_inc(srs_ready, 1)

                def rstd_of(n, eps):
                    act.wait_ge((st0, st1, st2, st3)[n], 1)
                    act.sem_inc((st0, st1, st2, st3)[n], -1)
                    act.activation(lnv[n][:, :], mv[n][:, 1:2], ACT.Ln, bias=eps[:, :]).then_inc(act_step, 1)
                    act.wait_ge(act_step, 1)
                    act.sem_inc(act_step, -1)
                    act.activation(rstd[n][:, :], lnv[n][:, :], ACT.Exp, scale=-0.5).then_inc((rs0, rs1, rs2, rs3)[n], 1)

                def a1():
                    rstd_of(0, eps5)

                def a2():
                    act.wait_ge(kT_ps, 1)
                    act.sem_inc(kT_ps, -1)
                    act.activation(ex[:, :, :].rearrange("p k t -> p (k t)"), ps[:, 0, :], ACT.Exp,
                                   bias=nshift[:, :]).then_inc(e_ready, 1)
                    act.wait_ge(cT_ps, 1)
                    act.sem_inc(cT_ps, -1)
                    act.activation(vT[:, :, :].rearrange("p k t -> p (k t)"), ps[:, 1, :], ACT.Copy).then_inc(vT_ready, 1)

                def a4():
                    rstd_of(1, eps5)

                def a5():
                    act.wait_ge(xnT_ps, 1)
                    act.sem_inc(xnT_ps, -1)
                    act.activation(xnT[:, :, :].rearrange("p k t -> p (k t)"), ps[:, 3, :], ACT.Copy).then_inc(xnT_ready, 1)
                    act.wait_ge(k_ps, 1)
                    act.sem_inc(k_ps, -1)
                    act.activation(ks[:, :, :].rearrange("p k t -> p (k t)"), ps[:, 1, :], ACT.Copy).then_inc(k_ready, 1)
                    act.wait_ge(v_ps, 1)
                    act.sem_inc(v_ps, -1)
                    act.activation(vs[:, :], ps[:, 2, :], ACT.Copy).then_inc(v_ready, 1)

                def exps(r):
                    act.wait_ge(nm_ready, 1)
                    act.sem_inc(nm_ready, -1)
                    bank = (3, 0, 1, 3)[r]
                    for c in range(4):
                        a = act.activation(pr[:, r, c, :], ps[:, bank, c * T:(c + 1) * T], ACT.Exp,
                                           bias=nm[:, r, c:c + 1], accum_out=rsum[:, r, c:c + 1])
                    a.then_inc(p_ready, 1)

                def pT_copy(r):
                    act.wait_ge(pT_ps_act, 1)
                    act.sem_inc(pT_ps_act, -1)
                    bank = (2, 0, 1, 3)[r]
                    act.activation(pT[:, r, :, :].rearrange("p c t -> p (c t)"), ps[:, bank, :], ACT.Copy)\
                       .then_inc(pT_ready_act, 1)

                def a6():
                    exps(0)
                    exps(1)
                    exps(2)
                    pT_copy(1)
                    exps(3)
                    pT_copy(3)

                def a7():
                    act.wait_ge(oT_ps, 1)
                    act.sem_inc(oT_ps, -1)
                    act.activation(oT[:, :, :].rearrange("p k t -> p (k t)"), ps[:, 0, :], ACT.Copy).then_inc(oT_ready, 1)

                def c1():
                    rstd_of(2, eps5)
                    act.wait_ge(qT_ps, 1)
                    act.sem_inc(qT_ps, -1)
                    act.activation(qT[:, :, :].rearrange("p k t -> p (k t)"), ps[:, 4, :], ACT.Copy).then_inc(qT_ready, 1)

                def c2():
                    act.wait_ge(g_ps, 1)
                    act.sem_inc(g_ps, -1)
                    act.activation(ig[:, :], ps[0:H, 5, 0:T], ACT.Identity, bias=gbias[0:H, :])
                    act.activation(fg[:, :], ps[32:32 + H, 5, 0:T], ACT.Identity, bias=gbias[32:32 + H, :]).then_inc(act_step, 1)
                    act.wait_ge(act_step, 1)
                    act.sem_inc(act_step, -1)
                    act.activation(fa[:, :], fg[:, :], ACT.Abs).then_inc(act_step, 1)
                    act.wait_ge(act_step, 1)
                    act.sem_inc(act_step, -1)
                    act.activation(fe[:, :], fa[:, :], ACT.Exp, scale=-1.0).then_inc(act_step, 1)
                    act.wait_ge(act_step, 1)
                    act.sem_inc(act_step, -1)
                    act.activation(fl[:, :], fe[:, :], ACT.Ln, bias=1.0).then_inc(lf_parts, 1)
                    act.wait_ge(fm_ready, 1)
                    act.sem_inc(fm_ready, -1)
                    act.activation(efm[:, :], fm[:, :], ACT.Exp, scale=-1.0).then_inc(efm_ready, 1)

                def c3():
                    for r in range(4):
                        act.wait_ge(l_ps, 1)
                        act.sem_inc(l_ps, -1)
                        act.activation(dm[:, r, :, :].rearrange("p c t -> p (c t)"), ps[:, (4, 6)[r % 2], :],
                                       ACT.Exp).then_inc(d_ready, 1)

                def c5():
                    act.wait_ge(hc_ready, 1)
                    act.sem_inc(hc_ready, -1)
                    act.activation(hsq[:, :, :], hc[:, :, :], ACT.Square).then_inc(hsq_ready, 1)
                    act.wait_ge(hvar_ready, 1)
                    act.sem_inc(hvar_ready, -1)
                    act.activation(hlv[:, :], hvar[:, :], ACT.Ln, scale=1.0 / DH, bias=eps6[:, :]).then_inc(act_step, 1)
                    act.wait_ge(act_step, 1)
                    act.sem_inc(act_step, -1)
                    act.activation(hrs[:, :], hlv[:, :], ACT.Exp, scale=-0.5).then_inc(hrs_ready, 1)

                def d1(i):
                    rstd_of(3, eps5)
                    act.wait_ge(zT_ps, 1)
                    act.sem_inc(zT_ps, -1)
                    act.activation(zT[:, :, :].rearrange("p k t -> p (k t)"), ps[:, 6, :], ACT.Copy).then_inc(zT_ready, 1)
                    act.dma_start(z_d[bass.ds(i * P, P), :], zn[:, :]).then_inc(zn_stored, 16)
                    act.wait_ge(nmx_ready, 1)
                    act.sem_inc(nmx_ready, -1)
                    act.activation(er[:, :], ps[:, 7, 0:E], ACT.Exp, bias=nmx[:, :]).then_inc(er_ready, 1)

                a1()
                a2()
                a4()
                a5()
                a6()
                a7()
                with act.Fori(1, nb) as i:
                    c1()
                    a1()
                    c2()
                    a2()
                    c3()
                    a4()
                    c5()
                    a5()
                    d1(i - 1)
                    a6()
                    a7()
                c1()
                c2()
                c3()
                c5()
                d1(nb - 1)

            @block.tensor
            def _(pe):
                pe.wait_ge(const_ready, 1)
                pe.sem_inc(const_ready, -1)

                def turn(bank, src, signal):
                    for c in range(4):
                        m = pe.transpose(ps[:, bank, c * P:(c + 1) * P], src(c), ident[:, :])
                    m.then_inc(signal, 1)

                def a2():
                    pe.wait_ge(kn_ready, 1)
                    pe.sem_inc(kn_ready, -1)
                    turn(0, lambda c: kn[:, c * P:(c + 1) * P], kT_ps)
                    pe.wait_ge(ctx_loaded, 16)
                    pe.sem_inc(ctx_loaded, -16)
                    turn(1, lambda c: ct[:, c * P:(c + 1) * P], cT_ps)

                def a4():
                    pe.wait_ge(y_ready, 1)
                    pe.sem_inc(y_ready, -1)
                    turn(2, lambda c: yy[:, c, :], yT_ps)

                def a5():
                    pe.wait_ge(xn_ready, 1)
                    pe.sem_inc(xn_ready, -1)
                    turn(3, lambda c: xn[:, c * P:(c + 1) * P], xnT_ps)
                    pe.wait_ge(xnT_ready, 1)
                    pe.sem_inc(xnT_ready, -1)
                    for j, signal in enumerate((q_ps, k_ps)):
                        for c in range(4):
                            for k in range(KC):
                                m = pe.matmul(ps[:, j, c * T:(c + 1) * T],
                                              wqk[:, k, j, 4 * c:4 * c + 4, :].rearrange("p h d -> p (h d)"),
                                              xnT[:, k, :], start=(k == 0), stop=(k == KC - 1))
                        m.then_inc(signal, 1)
                    for k in range(KC):
                        m = pe.matmul(ps[:, 2, :], xnT[:, k, :], wv[:, k, :], start=(k == 0), stop=(k == KC - 1))
                    m.then_inc(v_ps, 1)

                def scores(r):
                    bank = (3, 0, 1, 3)[r]
                    pe.matmul(ps[:, bank, :], identb[:, :], mask_ts[:, :, :].rearrange("p a t -> p (a t)"),
                              start=True, stop=False, skip_group_check=True)
                    for c in range(4):
                        m = pe.matmul(ps[:, bank, c * T:(c + 1) * T], qs[32 * r:32 * r + 32, c, :],
                                      ks[32 * r:32 * r + 32, c, :], start=False, stop=True, skip_group_check=True)
                    m.then_inc(s_ps, 1)

                def p_turn(r):
                    pe.wait_ge(p_ready, 1)
                    pe.sem_inc(p_ready, -1)
                    bank = (2, 0, 1, 3)[r]
                    turn(bank, lambda c: pr[:, r, c, :], (pT_ps_dve, pT_ps_act)[r % 2])

                def a6():
                    pe.wait_ge(q_ready, 1)
                    pe.sem_inc(q_ready, -1)
                    pe.wait_ge(k_ready, 1)
                    pe.sem_inc(k_ready, -1)
                    scores(0)
                    scores(1)
                    scores(2)
                    pe.wait_ge(v_ready, 1)
                    pe.sem_inc(v_ready, -1)
                    p_turn(0)
                    scores(3)
                    p_turn(1)
                    p_turn(2)
                    p_turn(3)

                def a7():
                    for r in range(4):
                        pe.wait_ge((pT_ready_dve, pT_ready_act)[r % 2], 1)
                        pe.sem_inc((pT_ready_dve, pT_ready_act)[r % 2], -1)
                        for c in range(4):
                            h = 4 * c + r
                            m = pe.matmul(ps[:, 2, h * DH:(h + 1) * DH], pT[:, r, c, :], vs[:, h * DH:(h + 1) * DH],
                                          start=True, stop=True)
                    m.then_inc(o_ps, 1)
                    pe.wait_ge(on_ready, 1)
                    pe.sem_inc(on_ready, -1)
                    turn(0, lambda c: on[:, c * P:(c + 1) * P], oT_ps)
                    pe.wait_ge(oT_ready, 1)
                    pe.sem_inc(oT_ready, -1)
                    for k in range(KC):
                        m = pe.matmul(ps[:, 1, :], oT[:, k, :], wp[:, k, :], start=(k == 0), stop=(k == KC - 1))
                    m.then_inc(att_ps, 1)

                def c1():
                    pe.wait_ge(qn_ready, 1)
                    pe.sem_inc(qn_ready, -1)
                    turn(4, lambda c: qn[:, c * P:(c + 1) * P], qT_ps)

                def c2():
                    pe.wait_ge(cd_ctx_ready, 1)
                    pe.sem_inc(cd_ctx_ready, -1)
                    pe.wait_ge(qT_ready, 1)
                    pe.sem_inc(qT_ready, -1)
                    for j in range(2):
                        for k in range(KC):
                            m = pe.matmul(ps[0:48, 5, 0:T], wg[:, j, k, :], (qT, kT2)[j][:, k, :],
                                          start=(j == 0 and k == 0), stop=(j == 1 and k == KC - 1))
                    m.then_inc(g_ps, 1)

                def c3():
                    pe.wait_ge(efm_ready, 1)
                    pe.sem_inc(efm_ready, -1)
                    pe.transpose(ps[:, 7, 0:H], efm[:, :], ident[0:H, 0:H]).then_inc(nT_ps, 1)
                    pe.wait_ge(bd_ready, 1)
                    pe.sem_inc(bd_ready, -1)
                    for r in range(4):
                        if r == 1:
                            pe.wait_ge(enT_done, 1)
                            pe.sem_inc(enT_done, -1)
                        if r >= 2:
                            pe.wait_ge(cm_ready, 1)
                            pe.sem_inc(cm_ready, -1)
                        lb, qb = ((4, 5), (6, 7))[r % 2]
                        pe.matmul(ps[:, lb, :], identb[:, :], mask_st[:, :, :].rearrange("p a t -> p (a t)"),
                                  start=True, stop=False, skip_group_check=True)
                        pe.matmul(ps[:, lb, :], ar[:, :], bd[:, r, :, :].rearrange("h c t -> h (c t)"),
                                  start=False, stop=True, skip_group_check=True).then_inc(l_ps, 1)
                        for c in range(4):
                            m = pe.matmul(ps[:, qb, c * T:(c + 1) * T], kT2[32 * r:32 * r + 32, c, :],
                                          qT[32 * r:32 * r + 32, c, :], start=True, stop=True)
                        m.then_inc(qk_ps, 1)

                def c4():
                    for n in range(2):
                        pe.wait_ge(cm_ready, 1)
                        pe.sem_inc(cm_ready, -1)
                    for h in range(H):
                        r, c = h % 4, h // 4
                        o = (h % 8) * (DH + 1)
                        m = pe.matmul(ps[:, 4 + h // 8, o:o + DH + 1], cm[:, r, c, :], vaug[:, h, :],
                                      start=True, stop=True)
                    m.then_inc(hu_ps, 1)

                def d1():
                    pe.wait_ge(zn_ready, 1)
                    pe.sem_inc(zn_ready, -1)
                    turn(6, lambda c: zn[:, c * P:(c + 1) * P], zT_ps)
                    pe.wait_ge(zT_ready, 1)
                    pe.sem_inc(zT_ready, -1)
                    for k in range(KC):
                        m = pe.matmul(ps[:, 7, 0:E], zT[:, k, :], gw[:, k, :], start=(k == 0), stop=(k == KC - 1))
                    m.then_inc(rl_ps, 1)
                    pe.wait_ge(sel_ready, 1)
                    pe.sem_inc(sel_ready, -1)
                    pe.matmul(ps[:, 7, 64:64 + E], ustrict[:, :], selb[:, :], start=True, stop=False)
                    pe.matmul(ps[:, 7, 64:64 + E], onesb[:, :], selacc[:, :], start=False, stop=True).then_inc(pos_ps, 1)

                pe.wait_ge(wts_scaled, 1)
                pe.sem_inc(wts_scaled, -1)
                a2()
                a4()
                a5()
                a6()
                a7()
                with pe.Fori(1, nb):
                    c1()
                    c2()
                    a2()
                    c3()
                    a4()
                    c4()
                    a5()
                    d1()
                    a6()
                    a7()
                c1()
                c2()
                c3()
                c4()
                d1()
                pe.wait_ge(sel_ready, 1)
                pe.sem_inc(sel_ready, -1)
                pe.matmul(ps[:, 7, 0:E], onesb[:, :], selacc[:, :], start=True, stop=True).then_inc(cnt_ps, 1)

            @block.vector
            def _(dve):
                dve.wait_ge(const_ready, 1)
                dve.sem_inc(const_ready, -1)
                dve.wait_ge(small_loaded, 64)
                dve.sem_inc(small_loaded, -64)
                dve.tensor_scalar(wpos[:, :], wch[:, :], 0.0, None, ALU.max).then_inc(dve_step, 1)
                dve.wait_ge(dve_step, 1)
                dve.sem_inc(dve_step, -1)
                dve.tensor_scalar(nwpos[:, :], wch[:, :], 0.0, -1.0, ALU.max, ALU.mult)
                dve.tensor_scalar(wneg[:, :], wch[:, :], 0.0, None, ALU.min).then_inc(dve_step, 1)
                dve.wait_ge(dve_step, 1)
                dve.sem_inc(dve_step, -1)
                dve.tensor_tensor(uw[:, :], uch[:, :], wpos[:, :], ALU.add).then_inc(dve_step, 1)
                dve.wait_ge(dve_step, 1)
                dve.sem_inc(dve_step, -1)
                for k in range(KC):
                    dve.tensor_scalar(zc[:, k, :], steps[:, :], nwpos[:, k:k + 1], uw[:, k:k + 1], ALU.mult, ALU.add).then_inc(dve_step, 1)
                    dve.wait_ge(dve_step, 1)
                    dve.sem_inc(dve_step, -1)
                dve.tensor_scalar(zc[:, :, :], zc[:, :, :], U_CAP, None, ALU.min).then_inc(dve_step, 1)
                dve.wait_ge(dve_step, 1)
                dve.sem_inc(dve_step, -1)
                dve.sem_inc(tab_parts, 1)
                dve.tensor_scalar(hs_[:, 2, :], hs_[:, 1, :], THRESH, None, ALU.is_gt).then_inc(dve_step, 1)
                dve.wait_ge(dve_step, 1)
                dve.sem_inc(dve_step, -1)
                dve.tensor_scalar(hs_[:, 0:2, :], hs_[:, 0:2, :], 1e-8, None, ALU.max).then_inc(dve_step, 1)
                dve.wait_ge(dve_step, 1)
                dve.sem_inc(dve_step, -1)
                dve.sem_inc(tab_parts, 1)
                dve.wait_ge(scale_parts, 1)
                dve.sem_inc(scale_parts, -1)
                for k in range(KC):
                    dve.tensor_scalar(dtab[:, k, :], onesf[:, :], decay[:, k:k + 1], None, ALU.mult).then_inc(dve_step, 1)
                    dve.wait_ge(dve_step, 1)
                    dve.sem_inc(dve_step, -1)
                dve.memset(zc[:, :, 0:1], 1.0).then_inc(dve_step, 1)
                dve.wait_ge(dve_step, 1)
                dve.sem_inc(dve_step, -1)
                dve.memset(dtab[:, :, 0:1], 0.0).then_inc(dve_step, 1)
                dve.wait_ge(dve_step, 1)
                dve.sem_inc(dve_step, -1)
                dve.sem_inc(tabs_ready, 1)
                dve.wait_ge(srs_ready, 1)
                dve.sem_inc(srs_ready, -1)
                dve.tensor_copy(sst[:, :], srl[:, 2, :]).then_inc(dve_step, 1)
                dve.wait_ge(dve_step, 1)
                dve.sem_inc(dve_step, -1)
                dve.tensor_copy(srl[:, 0, :], srl[:, 3, :]).then_inc(dve_step, 1)
                dve.wait_ge(dve_step, 1)
                dve.sem_inc(dve_step, -1)
                dve.tensor_tensor(srl[:, 1, :], srl[:, 3, :], hs_[:, 2, :], ALU.mult).then_inc(dve_step, 1)
                dve.wait_ge(dve_step, 1)
                dve.sem_inc(dve_step, -1)
                dve.tensor_tensor(srl[:, 0, :], srl[:, 0, :], srl[:, 1, :], ALU.subtract).then_inc(dve_step, 1)
                dve.wait_ge(dve_step, 1)
                dve.sem_inc(dve_step, -1)
                dve.wait_ge(wa_loaded, 16 * (4 * KC + 2))
                dve.sem_inc(wa_loaded, -(16 * (4 * KC + 2)))
                for k in range(KC):
                    low = [wraw[:, (2 * k + j) * H * R:(2 * k + j + 1) * H * R].rearrange("p (h d) -> p h d", h=H)
                           for j in range(2)]
                    m_ = srl[:, 1, :].unsqueeze(2).to_broadcast([P, H, R])
                    n_ = srl[:, 0, :].unsqueeze(2).to_broadcast([P, H, R])
                    for j in range(2):
                        dve.tensor_tensor(wqk[:, k, j, :, 0:DS], wqk[:, k, j, :, 0:DS],
                                          sst[:, :].unsqueeze(2).to_broadcast([P, H, DS]), ALU.mult).then_inc(dve_step, 1)
                        dve.wait_ge(dve_step, 1)
                        dve.sem_inc(dve_step, -1)
                        dve.tensor_tensor(cm[:, j, 2, :].rearrange("p (h d) -> p h d", h=H), low[1 - j], m_, ALU.mult).then_inc(dve_step, 1)
                        dve.wait_ge(dve_step, 1)
                        dve.sem_inc(dve_step, -1)
                        dve.tensor_tensor(cm[:, j, 3, :].rearrange("p (h d) -> p h d", h=H), low[j], n_, ALU.mult).then_inc(dve_step, 1)
                        dve.wait_ge(dve_step, 1)
                        dve.sem_inc(dve_step, -1)
                        dve.tensor_tensor(wqk[:, k, j, :, DS:DH], cm[:, j, 2, :].rearrange("p (h d) -> p h d", h=H),
                                          cm[:, j, 3, :].rearrange("p (h d) -> p h d", h=H), ALU.add).then_inc(dve_step, 1)
                        dve.wait_ge(dve_step, 1)
                        dve.sem_inc(dve_step, -1)
                    dve.tensor_scalar(wqk[:, k, 0, :, :], wqk[:, k, 0, :, :], QSCALE, None, ALU.mult).then_inc(dve_step, 1)
                    dve.wait_ge(dve_step, 1)
                    dve.sem_inc(dve_step, -1)
                dve.wait_ge(wg_loaded, 16 * (6 * KC + 4))
                dve.sem_inc(wg_loaded, -(16 * (6 * KC + 4)))
                for a, c0 in enumerate((0, 32)):
                    dve.tensor_tensor(wg[:, 1, :, c0:c0 + H], wg[:, 1, :, c0:c0 + H],
                                      cm[:, a, 0, 0:KC * H].rearrange("p (k n) -> p k n", k=KC), ALU.add).then_inc(dve_step, 1)
                    dve.wait_ge(dve_step, 1)
                    dve.sem_inc(dve_step, -1)
                dve.sem_inc(wts_scaled, 1)

                def norm(n, src, dst, signal):
                    dve.bn_stats(st[n][:, :], src).then_inc(dve_step, 1)
                    dve.wait_ge(dve_step, 1)
                    dve.sem_inc(dve_step, -1)
                    dve.bn_aggr(mv[n][:, :], st[n][:, :]).then_inc((st0, st1, st2, st3)[n], 1)
                    dve.wait_ge((rs0, rs1, rs2, rs3)[n], 1)
                    dve.sem_inc((rs0, rs1, rs2, rs3)[n], -1)
                    dve.tensor_scalar(dst, src, mv[n][:, 0:1], rstd[n][:, 0:1], ALU.subtract, ALU.mult).then_inc(signal, 1)

                def flat(t):
                    return t[:, :, :].rearrange("p k t -> p (k t)")

                def a1():
                    dve.wait_ge(x_loaded, 16)
                    dve.sem_inc(x_loaded, -16)
                    norm(0, xt[:, :], kn[:, :], kn_ready)

                def a3():
                    dve.wait_ge(vT_ready, 1)
                    dve.sem_inc(vT_ready, -1)
                    dve.wait_ge(g_ready, 1)
                    dve.sem_inc(g_ready, -1)
                    dve.tensor_tensor(gv[:, :, :], gg[:, :, :], vT[:, :, :], ALU.mult).then_inc(dve_step, 1)
                    dve.wait_ge(dve_step, 1)
                    dve.sem_inc(dve_step, -1)
                    dve.wait_ge(c_ready, 1)
                    dve.sem_inc(c_ready, -1)
                    dve.tensor_tensor(cv[:, :, :], cc[:, :, :], vT[:, :, :], ALU.mult).then_inc(ctx_used, 1)
                    dve.tensor_tensor_scan(flat(sq_), flat(dtab), flat(gg), 0.0, ALU.mult, ALU.add)
                    dve.tensor_tensor_scan(flat(sp_), flat(dtab), flat(gv), 0.0, ALU.mult, ALU.add).then_inc(dve_step, 1)
                    dve.wait_ge(dve_step, 1)
                    dve.sem_inc(dve_step, -1)
                    dve.tensor_tensor(cc[:, :, 1:T], cc[:, :, 1:T], sq_[:, :, 0:T - 1], ALU.add)
                    dve.tensor_tensor(cv[:, :, 1:T], cv[:, :, 1:T], sp_[:, :, 0:T - 1], ALU.add).then_inc(dve_step, 1)
                    dve.wait_ge(dve_step, 1)
                    dve.sem_inc(dve_step, -1)
                    dve.reciprocal(rden[:, :, :], cc[:, :, :]).then_inc(dve_step, 1)
                    dve.wait_ge(dve_step, 1)
                    dve.sem_inc(dve_step, -1)
                    dve.tensor_tensor(yy[:, :, :], cv[:, :, :], rden[:, :, :], ALU.mult).then_inc(y_ready, 1)

                def a4():
                    dve.wait_ge(yT_ps, 1)
                    dve.sem_inc(yT_ps, -1)
                    dve.tensor_tensor(x1[:, :], xt[:, :], ps[:, 2, :], ALU.add).then_inc(dve_step, 1)
                    dve.wait_ge(dve_step, 1)
                    dve.sem_inc(dve_step, -1)
                    dve.sem_inc(x_free, 1)
                    norm(1, x1[:, :], xn[:, :], xn_ready)

                def a5():
                    dve.wait_ge(q_ps, 1)
                    dve.sem_inc(q_ps, -1)
                    dve.tensor_copy(flat(qs), ps[:, 0, :]).then_inc(q_ready, 1)

                def row_max(r):
                    dve.wait_ge(s_ps, 1)
                    dve.sem_inc(s_ps, -1)
                    bank = (3, 0, 1, 3)[r]
                    dve.tensor_reduce(nm[:, r, :], ps[:, bank, :].rearrange("p (c t) -> p c t", c=4), AX.X, ALU.max,
                                      negate=True).then_inc(nm_ready, 1)

                def pT_copy(r):
                    dve.wait_ge(pT_ps_dve, 1)
                    dve.sem_inc(pT_ps_dve, -1)
                    bank = (2, 0, 1, 3)[r]
                    dve.tensor_copy(pT[:, r, :, :].rearrange("p c t -> p (c t)"), ps[:, bank, :]).then_inc(pT_ready_dve, 1)

                def a6():
                    row_max(0)
                    row_max(1)
                    row_max(2)
                    pT_copy(0)
                    row_max(3)
                    pT_copy(2)

                def a7():
                    dve.wait_ge(o_ps, 1)
                    dve.sem_inc(o_ps, -1)
                    dve.reciprocal(rinv[:, :, :], rsum[:, :, :]).then_inc(dve_step, 1)
                    dve.wait_ge(dve_step, 1)
                    dve.sem_inc(dve_step, -1)
                    dve.tensor_tensor(on[:, :].rearrange("p (c r d) -> p r c d", c=4, r=4),
                                      ps[:, 2, :].rearrange("p (c r d) -> p r c d", c=4, r=4),
                                      rinv[:, :, :].unsqueeze(3).to_broadcast([P, 4, 4, DH]), ALU.mult).then_inc(on_ready, 1)
                    dve.wait_ge(att_ps, 1)
                    dve.sem_inc(att_ps, -1)
                    dve.tensor_tensor(x2[:, :], x1[:, :], ps[:, 1, :], ALU.add).then_inc(dve_step, 1)
                    dve.wait_ge(dve_step, 1)
                    dve.sem_inc(dve_step, -1)

                def c1():
                    norm(2, x2[:, :], qn[:, :], qn_ready)

                def c2():
                    dve.wait_ge(lf_parts, 1)
                    dve.sem_inc(lf_parts, -1)
                    dve.scalar_tensor_tensor(lf[:, :], fg[:, :], 0.0, fl[:, :], ALU.min, ALU.subtract).then_inc(dve_step, 1)
                    dve.wait_ge(dve_step, 1)
                    dve.sem_inc(dve_step, -1)
                    dve.tensor_tensor_scan(cum[:, :], onesf[0:H, :], lf[:, :], 0.0, ALU.mult, ALU.add).then_inc(dve_step, 1)
                    dve.wait_ge(dve_step, 1)
                    dve.sem_inc(dve_step, -1)
                    dve.tensor_tensor(ar[32:32 + H, :], ig[:, :], cum[:, :], ALU.subtract).then_inc(dve_step, 1)
                    dve.wait_ge(dve_step, 1)
                    dve.sem_inc(dve_step, -1)
                    dve.tensor_tensor_scan(cmx[:, :], onesf[32:32 + H, :], ar[32:32 + H, :], -3.0e38, ALU.mult, ALU.max).then_inc(dve_step, 1)
                    dve.wait_ge(dve_step, 1)
                    dve.sem_inc(dve_step, -1)
                    dve.tensor_scalar(ncmx[:, :], cmx[:, :], -1.0, None, ALU.mult).then_inc(m_ready, 1)
                    dve.tensor_tensor(fm[:, :], cum[:, :], cmx[:, :], ALU.add).then_inc(dve_step, 1)
                    dve.wait_ge(dve_step, 1)
                    dve.sem_inc(dve_step, -1)
                    dve.tensor_scalar(fm[:, :], fm[:, :], -86.0, None, ALU.max).then_inc(fm_ready, 1)

                def c3():
                    dve.wait_ge(nT_ps, 1)
                    dve.sem_inc(nT_ps, -1)
                    dve.tensor_copy(enT[:, :], ps[:, 7, 0:H]).then_inc(enT_done, 1)
                    for r in range(4):
                        dve.wait_ge(d_ready, 1)
                        dve.sem_inc(d_ready, -1)
                        dve.wait_ge(qk_ps, 1)
                        dve.sem_inc(qk_ps, -1)
                        dve.scalar_tensor_tensor(cm[:, r, :, :].rearrange("p c t -> p (c t)"), ps[:, (5, 7)[r % 2], :], QSCALE,
                                                 dm[:, r, :, :].rearrange("p c t -> p (c t)"), ALU.mult, ALU.mult)\
                           .then_inc(cm_ready, 1)

                def wide(t, n):
                    return t[:, :].unsqueeze(2).to_broadcast([P, H, n])

                def c5():
                    dve.wait_ge(hu_ps, 1)
                    dve.sem_inc(hu_ps, -1)
                    dve.sem_inc(cd_ctx_free, 1)
                    raw = ps[:, 4:6, 0:8 * (DH + 1)].rearrange("p b (h e) -> p b h e", e=DH + 1)
                    half = [t[:, :].rearrange("p (b h) -> p b h", b=2) for t in (nrm, nrm2, enT)]
                    dve.scalar_tensor_tensor(half[0], raw[:, :, :, DH], -1.0, half[2], ALU.mult, ALU.max).then_inc(dve_step, 1)
                    dve.wait_ge(dve_step, 1)
                    dve.sem_inc(dve_step, -1)
                    dve.tensor_tensor(half[1], half[0], raw[:, :, :, DH], ALU.max).then_inc(dve_step, 1)
                    dve.wait_ge(dve_step, 1)
                    dve.sem_inc(dve_step, -1)
                    dve.tensor_scalar(nrm[:, :], nrm2[:, :], 1e-6, None, ALU.add).then_inc(dve_step, 1)
                    dve.wait_ge(dve_step, 1)
                    dve.sem_inc(dve_step, -1)
                    dve.reciprocal(rn[:, :], nrm[:, :]).then_inc(dve_step, 1)
                    dve.wait_ge(dve_step, 1)
                    dve.sem_inc(dve_step, -1)
                    dve.tensor_tensor(hh[:, :, :].rearrange("p (b h) d -> p b h d", b=2), raw[:, :, :, 0:DH],
                                      rn[:, :].rearrange("p (b h) -> p b h", b=2).unsqueeze(3).to_broadcast([P, 2, 8, DH]),
                                      ALU.mult).then_inc(dve_step, 1)
                    dve.wait_ge(dve_step, 1)
                    dve.sem_inc(dve_step, -1)
                    dve.tensor_reduce(hmu[:, :], hh[:, :, :], AX.X, ALU.add).then_inc(dve_step, 1)
                    dve.wait_ge(dve_step, 1)
                    dve.sem_inc(dve_step, -1)
                    dve.tensor_scalar(hmu2[:, :], hmu[:, :], 1.0 / DH, None, ALU.mult).then_inc(dve_step, 1)
                    dve.wait_ge(dve_step, 1)
                    dve.sem_inc(dve_step, -1)
                    dve.tensor_tensor(hc[:, :, :], hh[:, :, :], wide(hmu2, DH), ALU.subtract).then_inc(hc_ready, 1)
                    dve.wait_ge(hsq_ready, 1)
                    dve.sem_inc(hsq_ready, -1)
                    dve.tensor_reduce(hvar[:, :], hsq[:, :, :], AX.X, ALU.add).then_inc(hvar_ready, 1)
                    dve.wait_ge(hrs_ready, 1)
                    dve.sem_inc(hrs_ready, -1)
                    dve.tensor_tensor(hn[:, :, :], hc[:, :, :], wide(hrs, DH), ALU.mult).then_inc(hn_ready, 1)

                def d1():
                    dve.wait_ge(x3_ready, 1)
                    dve.sem_inc(x3_ready, -1)
                    dve.sem_inc(x3_go, 1)
                    dve.wait_ge(zn_stored, 16)
                    dve.sem_inc(zn_stored, -16)
                    norm(3, x3[:, :], zn[:, :], zn_ready)
                    dve.wait_ge(rl_ps, 1)
                    dve.sem_inc(rl_ps, -1)
                    dve.tensor_reduce(nmx[:, :], ps[:, 7, 0:E], AX.X, ALU.max, negate=True).then_inc(nmx_ready, 1)
                    dve.wait_ge(er_ready, 1)
                    dve.sem_inc(er_ready, -1)
                    dve.max(top[:, :], er[:, :]).then_inc(dve_step, 1)
                    dve.wait_ge(dve_step, 1)
                    dve.sem_inc(dve_step, -1)
                    dve.match_replace(er2[:, :], top[:, :], er[:, :], -1.0).then_inc(dve_step, 1)
                    dve.wait_ge(dve_step, 1)
                    dve.sem_inc(dve_step, -1)
                    dve.tensor_scalar(sel[:, :], er2[:, :], 0.0, None, ALU.is_lt)
                    dve.tensor_scalar(selb[:, :], er2[:, :], 0.0, None, ALU.is_lt).then_inc(sel_ready, 1)
                    dve.tensor_reduce(s8[:, :], top[:, :], AX.X, ALU.add).then_inc(dve_step, 1)
                    dve.wait_ge(dve_step, 1)
                    dve.sem_inc(dve_step, -1)
                    dve.reciprocal(r8[:, :], s8[:, :]).then_inc(dve_step, 1)
                    dve.wait_ge(dve_step, 1)
                    dve.sem_inc(dve_step, -1)
                    dve.tensor_scalar(wsel[:, :], er[:, :], r8[:, :], 1.0 / WSC, ALU.mult, ALU.mult).then_inc(dve_step, 1)
                    dve.wait_ge(dve_step, 1)
                    dve.sem_inc(dve_step, -1)
                    dve.wait_ge(pos_ps, 1)
                    dve.sem_inc(pos_ps, -1)
                    dve.scalar_tensor_tensor(kept[:, :], ps[:, 7, 64:64 + E], float(CAP), sel[:, :], ALU.is_lt, ALU.mult)
                    dve.tensor_scalar(key3[:, :], ps[:, 7, 64:64 + E], 0.5 - P / 2, 1.0 / P, ALU.add, ALU.mult).then_inc(dve_step, 1)
                    dve.wait_ge(dve_step, 1)
                    dve.sem_inc(dve_step, -1)
                    dve.scalar_tensor_tensor(key2[:, :], ps[:, 7, 64:64 + E], float(COLS), slot1[:, :], ALU.mult, ALU.add)
                    dve.tensor_scalar(key3[:, :], key3[:, :], ROUND, None, ALU.add).then_inc(dve_step, 1)
                    dve.wait_ge(dve_step, 1)
                    dve.sem_inc(dve_step, -1)
                    dve.tensor_scalar(key3[:, :], key3[:, :], ROUND, 1.0 - P * COLS, ALU.subtract, ALU.mult).then_inc(dve_step, 1)
                    dve.wait_ge(dve_step, 1)
                    dve.sem_inc(dve_step, -1)
                    dve.tensor_tensor(key[:, :], key2[:, :], key3[:, :], ALU.add).then_inc(dve_step, 1)
                    dve.wait_ge(dve_step, 1)
                    dve.sem_inc(dve_step, -1)
                    dve.tensor_tensor(key2[:, :], key[:, :], kept[:, :], ALU.mult).then_inc(dve_step, 1)
                    dve.wait_ge(dve_step, 1)
                    dve.sem_inc(dve_step, -1)
                    dve.tensor_tensor(selacc[:, :], selacc[:, :], selb[:, :], ALU.add)
                    dve.max(keys[:, :], key2[:, :]).then_inc(dve_step, 1)
                    dve.wait_ge(dve_step, 1)
                    dve.sem_inc(dve_step, -1)
                    dve.tensor_scalar(miss[:, :], keys[:, :], 0.0, trash[:, :], ALU.is_equal, ALU.mult).then_inc(dve_step, 1)
                    dve.wait_ge(dve_step, 1)
                    dve.sem_inc(dve_step, -1)
                    dve.wait_ge(pairs_free, 1)
                    dve.sem_inc(pairs_free, -1)
                    dve.scalar_tensor_tensor(slots[:, :], miss[:, :], -1.0, keys[:, :], ALU.add, ALU.add)
                    dve.tensor_copy(pair[:, :, 0], tok_f[:, :].to_broadcast([P, 8]))
                    for k in range(8):
                        dve.scalar_tensor_tensor(junk[:, :], key2[:, :], keys[:, k:k + 1], wsel[:, :], ALU.is_equal,
                                                 ALU.mult, accum_out=pair[:, k, 1:2].bitcast(F32)).then_inc(dve_step, 1)
                        dve.wait_ge(dve_step, 1)
                        dve.sem_inc(dve_step, -1)
                    dve.tensor_scalar(tok_f[:, :], tok_f[:, :], float(T), None, ALU.add).then_inc(pairs_ready, 1)

                a1()
                a3()
                a4()
                a5()
                a6()
                a7()
                with dve.Fori(1, nb):
                    c1()
                    a1()
                    c2()
                    c3()
                    a3()
                    a4()
                    c5()
                    a5()
                    d1()
                    a6()
                    a7()
                c1()
                c2()
                c3()
                c5()
                d1()
                dve.sem_inc(sel_ready, 1)
                dve.wait_ge(cnt_ps, 1)
                dve.sem_inc(cnt_ps, -1)
                dve.tensor_scalar(cntf[:, :], ps[:, 7, 0:E], float(CAP), 1.0, ALU.min, ALU.max).then_inc(dve_step, 1)
                dve.wait_ge(dve_step, 1)
                dve.sem_inc(dve_step, -1)
                dve.tensor_copy(counts[:, :], cntf[:, :]).then_inc(dve_step, 1)
                dve.wait_ge(dve_step, 1)
                dve.sem_inc(dve_step, -1)
                dve.wait_ge(zn_stored, 16)
                dve.sem_inc(zn_stored, -16)
                dve.wait_ge(pairs_free, 1)
                dve.sem_inc(pairs_free, -1)

        with ExitStack() as ctx:
            def sb(name, shape, dt=F32):
                return ctx.enter_context(nc.sbuf_tensor(name, shape, dt))

            NGRP = CAP // GROUP
            ident = sb("ident2", [P, P])
            zero_i = sb("zero_i", [P, P])
            wst = sb("wst", [P, KC, 2 * INTER])
            wdst = sb("wdst", [P, 2, D])
            wh = sb("wh", [P, 2, KC, 2 * INTER], F16)
            wl = sb("wl", [P, 2, KC, 2 * INTER], F16)
            dh = sb("dh", [P, 2, 2, D], F16)
            dl = sb("dl", [P, 2, 2, D], F16)
            slot_t = sb("slot_t", [P, COLS, 2], U32)
            m_in = sb("m_in", [P, 2, 2], U32)
            m_a = sb("m_a", [P, 2, 2], U32)
            m_b = sb("m_b", [P, 2, 2], U32)
            m_add = sb("m_add", [P, 2, 2], U32)
            xg = sb("xg", [P, 2, D])
            xh = sb("xh", [P, KC, GROUP], F16)
            xl = sb("xl", [P, KC, GROUP], F16)
            s1 = sb("s1", [P, GROUP])
            s2 = sb("s2", [I2, GROUP])
            h1 = sb("h1", [P, GROUP])
            h2 = sb("h2", [I2, GROUP])
            hh1 = sb("hh1", [P, GROUP], F16)
            hh2 = sb("hh2", [I2, GROUP], F16)
            hl1 = sb("hl1", [P, GROUP], F16)
            hl2 = sb("hl2", [I2, GROUP], F16)
            y = sb("y", [P, 2, D])
            w_loaded = sem("w_loaded")
            w_staged = sem("w_staged")
            hi_ready = sem("hi_ready")
            slots_loaded = sem("slots_loaded")
            wh_ready0 = sem("wh_ready0")
            wh_ready1 = sem("wh_ready1")
            w_free0 = sem("w_free0")
            w_free1 = sem("w_free1")
            meta_ready = sem("meta_ready")
            rows_landed = sem("rows_landed")
            rows_ready = sem("rows_ready")
            rows_free = sem("rows_free")
            rows_ps = sem("rows_ps")
            xh_ready = sem("xh_ready")
            xl_ready = sem("xl_ready")
            gate2_ps = sem("gate2_ps")
            gate_ps = sem("gate_ps")
            up_ps = sem("up_ps")
            s_ready = sem("s_ready")
            hh_ready = sem("hh_ready")
            hl_ready = sem("hl_ready")
            y_ps = sem("y_ps")
            wy_ready = sem("wy_ready")
            added = sem("added")
            copied = sem("copied")
            m_free = sem("m_free")
            set_step = sem("set_step")
            moe_step = sem("moe_step")
            id_ready = sem("id_ready")
            all_added = sem("all_added")
            v_step = sem("v_step")
            wh_ready = (wh_ready0, wh_ready1)
            w_free = (w_free0, w_free1)
            block2 = ctx.enter_context(nc.Block())

            def pairs_of_experts(eng, expert):
                with eng.Fori(0, ne // 2 - 1) as i:
                    for j in range(2):
                        expert(2 * i + j, j, True)
                for j in range(2):
                    expert(ne - 2 + j, j, j == 0)

            def other_groups(eng, e, group):
                n = eng.value_load(counts[0:1, bass.ds(e, 1)], min_val=1, max_val=CAP)
                with eng.Fori(1, NGRP) as g:
                    with eng.If(n > g * GROUP):
                        group(g)

            @block2.sync
            def _(sp):
                def load(e):
                    for src, c1_, c2_ in ((w_gate, 0, 2 * P), (w_up, P, 2 * P + I2)):
                        v_ = src[bass.ds(e, 1)].rearrange("a (k p) n -> p (a k) n", p=P)
                        sp.dma_start(wst[:, :, c1_:c1_ + P], v_[:, :, 0:P]).then_inc(w_loaded, 16)
                        sp.dma_start(wst[:, :, c2_:c2_ + I2], v_[:, :, P:INTER]).then_inc(w_loaded, 16)
                    v_ = w_down[bass.ds(e, 1)].rearrange("a i d -> (a i) d")
                    sp.dma_start(wdst[:, 0, :], v_[0:P, :]).then_inc(w_loaded, 16)
                    sp.dma_start(wdst[0:I2, 1, :], v_[P:INTER, :]).then_inc(w_loaded, 16)

                sp.dma_start(slot_t[:, :, :], slot_d[0:SLOTS, :].rearrange("(p s) c -> p s c", p=P)).then_inc(slots_loaded, 16)
                load(0)
                with sp.Fori(1, ne) as e:
                    sp.wait_ge(w_staged, 1)
                    sp.sem_inc(w_staged, -1)
                    load(e)
                sp.wait_ge(w_staged, 1)
                sp.sem_inc(w_staged, -1)
                sp.wait_ge(all_added, 1)
                sp.sem_inc(all_added, -1)
                sp.dma_start(out.rearrange("b t d -> (b t) d"), acc_d[0:TOK, :]).then_inc(copied, 16)
                sp.wait_ge(copied, 16)

            @block2.gpsimd
            def _(pool):
                n_added = pool.alloc_register("n_added")
                n_rows = pool.alloc_register("n_rows")
                pool.reg_mov(n_added, 0)
                pool.reg_mov(n_rows, 0)

                def shift():
                    pool.tensor_copy(m_add[:, :, :], m_b[:, :, :]).then_inc(pool_step, 1)
                    pool.wait_ge(pool_step, 1)
                    pool.sem_inc(pool_step, -1)
                    pool.sem_inc(meta_ready, 1)
                    pool.tensor_copy(m_b[:, :, :], m_a[:, :, :]).then_inc(pool_step, 1)
                    pool.wait_ge(pool_step, 1)
                    pool.sem_inc(pool_step, -1)

                def add_rows():
                    pool.wait_ge(wy_ready, 1)
                    pool.sem_inc(wy_ready, -1)
                    pool.reg_add(n_added, n_added, 32)
                    for h in range(2):
                        pool.indirect_dma_start(out=acc_d[:, :], out_offset=bass.IndirectOffsetOnAxis(ap=m_add[:, h, 0:1], axis=0),
                                                in_=y[:, h, :], in_offset=None, compute_op=ALU.add).then_inc(added, 16)

                def group(col):
                    pool.wait_ge(rows_free, 1)
                    pool.sem_inc(rows_free, -1)
                    pool.tensor_copy(m_in[:, :, :], slot_t[:, bass.ds(col, 2), :]).then_inc(pool_step, 1)
                    pool.wait_ge(pool_step, 1)
                    pool.sem_inc(pool_step, -1)
                    added_ = pool.snap(n_added, min_val=32, max_val=32 * (E * NGRP + 3))
                    pool.reg_add(n_rows, n_rows, 32)
                    landed = pool.snap(n_rows, min_val=32, max_val=32 * E * NGRP)
                    for h in range(2):
                        pool.indirect_dma_start(out=xg[:, h, :], out_offset=None, in_=z_d[:, :],
                                                in_offset=bass.IndirectOffsetOnAxis(ap=m_in[:, h, 0:1], axis=0)).then_inc(rows_landed, 16)
                    pool.wait_ge(added, added_)
                    pool.sem_inc(m_free, 1)
                    pool.wait_ge(m_free, 1)
                    pool.sem_inc(m_free, -1)
                    shift()
                    pool.tensor_copy(m_a[:, :, :], m_in[:, :, :]).then_inc(pool_step, 1)
                    pool.wait_ge(pool_step, 1)
                    pool.sem_inc(pool_step, -1)
                    pool.wait_ge(rows_landed, landed)
                    pool.sem_inc(rows_ready, 1)
                    add_rows()

                def expert(e, j, more):
                    group(e * (CAP // P))
                    other_groups(pool, e, lambda g: group(e * (CAP // P) + g * 2))

                pool.memset(zero_i[:, :], 0.0)
                for t_ in (hh1, hh2, hl1, hl2):
                    pool.memset(t_[:, :], 0.0)
                pool.memset(dh[:, 1, :, :], 0.0)
                pool.memset(dl[:, 1, :, :], 0.0)
                pool.memset(y[:, :, :], 0.0)
                for t_ in (m_a, m_b, m_add):
                    pool.memset(t_[:, :, :], 0).then_inc(pool_step, 1)
                    pool.wait_ge(pool_step, 1)
                    pool.sem_inc(pool_step, -1)
                    pool.iota(t_[:, :, 0].bitcast(mybir.dt.int32), pattern=[[P, 2]], base=TOK, channel_multiplier=1).then_inc(pool_step, 1)
                    pool.wait_ge(pool_step, 1)
                    pool.sem_inc(pool_step, -1)
                pool.affine_select(out=ident[:, :], in_=zero_i[:, :], compare_op=ALU.not_equal, fill=1.0, base=0,
                                   pattern=[[-1, P]], channel_multiplier=1).then_inc(pool_step, 1)
                pool.wait_ge(pool_step, 1)
                pool.sem_inc(pool_step, -1)
                pool.sem_inc(id_ready, 1)
                pool.sem_inc(rows_free, 1)
                pool.sem_inc(wy_ready, 1)
                pool.wait_ge(slots_loaded, 16)
                pool.sem_inc(slots_loaded, -16)
                add_rows()
                pool.sem_inc(wy_ready, 1)
                pairs_of_experts(pool, expert)
                for last in range(2):
                    added_ = pool.snap(n_added, min_val=32, max_val=32 * (E * NGRP + 3))
                    pool.wait_ge(added, added_)
                    pool.sem_inc(m_free, 1)
                    pool.wait_ge(m_free, 1)
                    pool.sem_inc(m_free, -1)
                    shift()
                    add_rows()
                added_ = pool.snap(n_added, min_val=32, max_val=32 * (E * NGRP + 3))
                pool.wait_ge(added, added_)
                pool.sem_inc(all_added, 1)

            @block2.tensor
            def _(pe):
                def turn():
                    pe.wait_ge(rows_ready, 1)
                    pe.sem_inc(rows_ready, -1)
                    for h in range(2):
                        for k in range(KC):
                            m = pe.transpose(ps[:, h, k * P:(k + 1) * P], xg[:, h, k * P:(k + 1) * P], ident[:, :])
                    m.then_inc(rows_ps, 1)

                def down(j):
                    pe.wait_ge(hh_ready, 1)
                    pe.sem_inc(hh_ready, -1)
                    for h in range(2):
                        o, t = ps[:, 5 + h, :], slice(h * P, h * P + P)
                        pe.matmul(o, hh1[:, t], dh[:, j, 0, :], start=True, stop=False)
                        pe.matmul(o, hh1[:, t], dl[:, j, 0, :], start=False, stop=False)
                        pe.matmul(o, hh2[:, t], dh[0:I2, j, 1, :], start=False, stop=False)
                        pe.matmul(o, hh2[:, t], dl[0:I2, j, 1, :], start=False, stop=False)
                    pe.wait_ge(hl_ready, 1)
                    pe.sem_inc(hl_ready, -1)
                    for h in range(2):
                        o, t = ps[:, 5 + h, :], slice(h * P, h * P + P)
                        pe.matmul(o, hl1[:, t], dh[:, j, 0, :], start=False, stop=False)
                        pe.matmul(o, hl2[:, t], dh[0:I2, j, 1, :], start=False, stop=True).then_inc(y_ps, 1)

                def gate_up(j):
                    pe.wait_ge(xl_ready, 1)
                    pe.sem_inc(xl_ready, -1)
                    for c0, dst, signal in ((2 * P, 3, gate2_ps), (0, 2, gate_ps), (P, 4, up_ps)):
                        for k in range(KC):
                            w_hi, w_lo = wh[:, j, k, c0:c0 + P], wl[:, j, k, c0:c0 + P]
                            pe.matmul(ps[:, dst, 0:GROUP], w_hi, xh[:, k, :], start=(k == 0), stop=False)
                            pe.matmul(ps[:, dst, 0:GROUP], w_hi, xl[:, k, :], start=False, stop=False)
                            m = pe.matmul(ps[:, dst, 0:GROUP], w_lo, xh[:, k, :], start=False, stop=(k == KC - 1))
                        m.then_inc(signal, 1)

                def expert(e, j, more):
                    turn()
                    down(1 - j)
                    pe.drain().then_inc(w_free[1 - j], 1)
                    pe.wait_ge(wh_ready[j], 1)
                    pe.sem_inc(wh_ready[j], -1)
                    gate_up(j)

                    def group(g):
                        turn()
                        down(j)
                        gate_up(j)
                    other_groups(pe, e, group)

                pe.wait_ge(id_ready, 1)
                pe.sem_inc(id_ready, -1)
                pe.sem_inc(hh_ready, 1)
                pe.sem_inc(hl_ready, 1)
                pairs_of_experts(pe, expert)
                down(1)

            @block2.scalar
            def _(act):
                def split_high(j):
                    act.wait_ge(w_loaded, 96)
                    act.sem_inc(w_loaded, -96)
                    act.activation(wh[:, j, :, :], wst[:, :, :], ACT.Copy, scale=WSC)
                    act.activation(dh[:, j, 0, :], wdst[:, 0, :], ACT.Copy, scale=WSC)
                    act.activation(dh[0:I2, j, 1, :], wdst[0:I2, 1, :], ACT.Copy, scale=WSC).then_inc(hi_ready, 1)

                def weigh():
                    act.wait_ge(meta_ready, 1)
                    act.sem_inc(meta_ready, -1)
                    for h in range(2):
                        act.wait_ge(y_ps, 1)
                        act.sem_inc(y_ps, -1)
                        a = act.activation(y[:, h, :], ps[:, 5 + h, :], ACT.Copy, scale=m_add[:, h, 1:2].bitcast(F32))
                    a.then_inc(wy_ready, 1)

                def group(g=0):
                    act.wait_ge(rows_ps, 1)
                    act.sem_inc(rows_ps, -1)
                    act.sem_inc(rows_free, 1)
                    for h in range(2):
                        a = act.activation(xh[:, :, h * P:(h + 1) * P], ps[:, h, :].rearrange("p (k t) -> p k t", k=KC), ACT.Copy)
                    a.then_inc(xh_ready, 1)
                    weigh()
                    act.wait_ge(gate2_ps, 1)
                    act.sem_inc(gate2_ps, -1)
                    act.activation(s2[:, :], ps[0:I2, 3, 0:GROUP], ACT.Silu, scale=1.0 / WSC)
                    act.wait_ge(gate_ps, 1)
                    act.sem_inc(gate_ps, -1)
                    act.activation(s1[:, :], ps[:, 2, 0:GROUP], ACT.Silu, scale=1.0 / WSC).then_inc(s_ready, 1)

                def expert(e, j, more):
                    group()
                    act.wait_ge(w_free[1 - j], 1)
                    act.sem_inc(w_free[1 - j], -1)
                    if more:
                        split_high(1 - j)
                    other_groups(act, e, group)

                split_high(0)
                act.wait_ge(meta_ready, 1)
                act.sem_inc(meta_ready, -1)
                pairs_of_experts(act, expert)
                weigh()

            @block2.vector
            def _(dve):

                def split_low(j):
                    dve.wait_ge(hi_ready, 1)
                    dve.sem_inc(hi_ready, -1)
                    dve.scalar_tensor_tensor(wl[:, j, :, :], wst[:, :, :], WSC, wh[:, j, :, :], ALU.mult, ALU.subtract)
                    dve.scalar_tensor_tensor(dl[:, j, 0, :], wdst[:, 0, :], WSC, dh[:, j, 0, :], ALU.mult, ALU.subtract)
                    dve.scalar_tensor_tensor(dl[0:I2, j, 1, :], wdst[0:I2, 1, :], WSC, dh[0:I2, j, 1, :],
                                             ALU.mult, ALU.subtract).then_inc(dve_step, 1)
                    dve.wait_ge(dve_step, 1)
                    dve.sem_inc(dve_step, -1)
                    dve.sem_inc(wh_ready[j], 1)
                    dve.sem_inc(w_staged, 1)

                def group(g=0):
                    dve.wait_ge(xh_ready, 1)
                    dve.sem_inc(xh_ready, -1)
                    for h in range(2):
                        a = dve.tensor_tensor(xl[:, :, h * P:(h + 1) * P], ps[:, h, :].rearrange("p (k t) -> p k t", k=KC),
                                              xh[:, :, h * P:(h + 1) * P], ALU.subtract)
                    a.then_inc(xl_ready, 1)
                    dve.wait_ge(s_ready, 1)
                    dve.sem_inc(s_ready, -1)
                    dve.wait_ge(up_ps, 1)
                    dve.sem_inc(up_ps, -1)
                    up1, up2 = ps[:, 4, 0:GROUP], ps[I2:2 * I2, 3, 0:GROUP]
                    dve.scalar_tensor_tensor(hh1[:, :], up1, 1.0 / WSC, s1[:, :], ALU.mult, ALU.mult)
                    dve.scalar_tensor_tensor(hh2[:, :], up2, 1.0 / WSC, s2[:, :], ALU.mult, ALU.mult).then_inc(hh_ready, 1)
                    dve.scalar_tensor_tensor(h1[:, :], up1, 1.0 / WSC, s1[:, :], ALU.mult, ALU.mult)
                    dve.scalar_tensor_tensor(h2[:, :], up2, 1.0 / WSC, s2[:, :], ALU.mult, ALU.mult).then_inc(dve_step, 1)
                    dve.wait_ge(dve_step, 1)
                    dve.sem_inc(dve_step, -1)
                    dve.tensor_tensor(hl1[:, :], h1[:, :], hh1[:, :], ALU.subtract)
                    dve.tensor_tensor(hl2[:, :], h2[:, :], hh2[:, :], ALU.subtract).then_inc(hl_ready, 1)

                def expert(e, j, more):
                    group()
                    if more:
                        split_low(1 - j)
                    other_groups(dve, e, group)

                split_low(0)
                pairs_of_experts(dve, expert)


_INS = ['x', 'ctx_2048', 'L0_xattn_w', 'L0_xattn_u', 'L0_ffn_Wa', 'L0_ffn_Wp', 'L0_ffn_w_std', 'L0_ffn_w_rec',
        'L1_xattn_Wi', 'L1_xattn_bi', 'L1_xattn_Wf', 'L1_xattn_bf', 'L1_xattn_ln_scale', 'L1_ffn_gate_w',
        'L1_ffn_w_gate', 'L1_ffn_w_up', 'L1_ffn_w_down']


def kernel(**inputs):
    import numpy as _np
    import concourse.bacc as _bacc
    from concourse import mybir as _mybir
    from concourse.bass_utils import run_bass_kernel_spmd as _run

    nc = _bacc.Bacc("TRN2", target_bir_lowering=False, num_devices=1)
    arrays, args = {}, []
    for name in _INS:
        a = _np.ascontiguousarray(inputs[name])
        arrays[f"in_{name}_dram"] = a
        args.append(nc.dram_tensor(f"in_{name}_dram", a.shape, _mybir.dt.from_np(a.dtype), kind="ExternalInput").ap())
    out = nc.dram_tensor("out_0_dram", (32, 128, 512), _mybir.dt.float32, kind="ExternalOutput").ap()
    build(nc, *args, out)
    r = _run(nc, [arrays], core_ids=[0])
    return r.results[0]["out_0_dram"]
```

```python
from contextlib import ExitStack

import concourse.bass as bass
from concourse import mybir

F32 = mybir.dt.float32
BF16 = mybir.dt.bfloat16
F16 = mybir.dt.float16
U32 = mybir.dt.uint32
ALU = mybir.AluOpType
ACT = mybir.ActivationFunctionType
AX = mybir.AxisListType

P = 128
NEG = -1.0e30
K_SHIFT = 16.0
ROUND = 1.5 * 2.0 ** 23
U_CAP = 70.0


def build(nc, x, ctx_in, w, u, Wa, Wp, w_std, w_rec, Wi, bi, Wf, bf, ln_scale, gate_w, w_gate, w_up,
          w_down, out, NB=None, NE=None):
    B, T, D = x.shape
    H = w_std.shape[0]
    R = 8
    DH = D // H
    DS = DH - R
    KC = D // P
    E = gate_w.shape[1]
    INTER = w_gate.shape[2]
    I2 = INTER - P
    CAP = 2 * (B * T * 8 // E)
    assert T == P and H == 16 and DH == 32 and KC == 4 and E == 32 and INTER == 192
    nb, ne = NB or B, NE or E
    THRESH = 0.1
    QSCALE = float(DH) ** -0.5

    TOK = B * T
    GROUP = 2 * P
    SLOTS = E * CAP
    COLS = SLOTS // P
    WSC = 256.0
    acc_d = nc.dram_tensor("acc_scratch", [TOK + GROUP, D], F32, kind="Internal").ap()
    z_d = nc.dram_tensor("z_scratch", [TOK + GROUP, D], F32, kind="Internal").ap()
    slot_d = nc.dram_tensor("slot_scratch", [SLOTS + P, 2], U32, kind="Internal").ap()

    with ExitStack() as whole:
        def sem(name):
            return whole.enter_context(nc.semaphore(name))

        def sbw(name, shape, dt=F32):
            return whole.enter_context(nc.sbuf_tensor(name, shape, dt))

        ps = whole.enter_context(nc.psum_tensor("ps", [P, 8, 512], F32))
        counts = sbw("counts", [P, E], U32)

        with ExitStack() as ctx:
            def sb(name, shape, dt=F32):
                return ctx.enter_context(nc.sbuf_tensor(name, shape, dt))

            ident = sb("ident", [P, P])
            identb = sb("identb", [P, P], BF16)
            onesf = sb("onesf", [P, P])
            onesb = sb("onesb", [P, P], BF16)
            ustrict = sb("ustrict", [P, P], BF16)
            mask_ts = sb("mask_ts", [P, 4, P], BF16)
            mask_st = sb("mask_st", [P, 4, P], BF16)
            zerob = sb("zerob", [P, 4, P], BF16)
            ind = sb("ind", [H, 4, 4])
            steps = sb("steps", [P, T])
            eps5 = sb("eps5", [P, 1])
            eps6 = sb("eps6", [P, 1])
            nshift = sb("nshift", [P, 1])
            wch = sb("wch", [P, KC])
            uch = sb("uch", [P, KC])
            wpos = sb("wpos", [P, KC])
            nwpos = sb("nwpos", [P, KC])
            wneg = sb("wneg", [P, KC])
            decay = sb("decay", [P, KC])
            uw = sb("uw", [P, KC])
            dtab = sb("dtab", [P, KC, T])
            gam = sb("gam", [P, KC, T])
            zc = sb("zc", [P, KC, T])
            hs_ = sb("hs_", [P, 3, H])
            sst = sb("sst", [P, H])
            srl = sb("srl", [P, 4, H])
            wqk = sb("wqk", [P, KC, 2, H, DH])
            wv = sb("wv", [P, KC, D])
            wp = sb("wp", [P, KC, D])
            wg = sb("wg", [P, 2, KC, 48])
            gbias = sb("gbias", [48, 1])
            lnsc = sb("lnsc", [P, D])
            gw = sb("gw", [P, KC, E])
            xt = sb("xt", [P, D])
            ct = sb("ct", [P, D])
            st = [sb(f"st{n}", [P, 6]) for n in range(4)]
            mv = [sb(f"mv{n}", [P, 2]) for n in range(4)]
            lnv = [sb(f"lnv{n}", [P, 1]) for n in range(4)]
            rstd = [sb(f"rstd{n}", [P, 1]) for n in range(4)]
            kn = sb("kn", [P, D])
            ex = sb("ex", [P, KC, T])
            vT = sb("vT", [P, KC, T])
            gg = sb("gg", [P, KC, T])
            cc = sb("cc", [P, KC, T])
            gv = sb("gv", [P, KC, T])
            cv = sb("cv", [P, KC, T])
            sq_ = sb("sq_", [P, KC, T])
            sp_ = sb("sp_", [P, KC, T])
            rden = sb("rden", [P, KC, T])
            yy = sb("yy", [P, KC, T])
            x1 = sb("x1", [P, D])
            x1n = sb("x1n", [P, D])
            ctk = sb("ctk", [P, D])
            vTk = sb("vTk", [P, KC, T])
            xn = sb("xn", [P, D])
            xnT = sb("xnT", [P, KC, T])
            qs = sb("qs", [P, KC, T])
            ks = sb("ks", [P, KC, T])
            vs = sb("vs", [P, D])
            nm = sb("nm", [P, 4, 4])
            rsum = sb("rsum", [P, 4, 4])
            rinv = sb("rinv", [P, 4, 4])
            pr = sb("pr", [P, 4, 4, T])
            pT = sb("pT", [P, 4, 4, T])
            on = sb("on", [P, D])
            oT = sb("oT", [P, KC, T])
            x2 = sb("x2", [P, D])
            qn = sb("qn", [P, D])
            qT = sb("qT", [P, KC, T])
            kT2 = sb("kT2", [P, KC, T])
            vaug = sb("vaug", [P, H, DH + 1])
            ig = sb("ig", [H, T])
            fg = sb("fg", [H, T])
            fa = sb("fa", [H, T])
            fe = sb("fe", [H, T])
            fl = sb("fl", [H, T])
            lf = sb("lf", [H, T])
            cum = sb("cum", [H, T])
            cmx = sb("cmx", [H, T])
            ncmx = sb("ncmx", [H, T])
            fm = sb("fm", [H, T])
            efm = sb("efm", [H, T])
            ar = sb("ar", [48, T])
            bd = sb("bd", [48, 4, 4, T])
            dm = sb("dm", [P, 4, 4, T])
            cm = sb("cm", [P, 4, 4, T])
            enT = sb("enT", [P, H])
            nrm = sb("nrm", [P, H])
            nrm2 = sb("nrm2", [P, H])
            rn = sb("rn", [P, H])
            hh = sb("hh", [P, H, DH])
            hmu = sb("hmu", [P, H])
            hmu2 = sb("hmu2", [P, H])
            hc = sb("hc", [P, H, DH])
            hsq = sb("hsq", [P, H, DH])
            hvar = sb("hvar", [P, H])
            hlv = sb("hlv", [P, H])
            hrs = sb("hrs", [P, H])
            hn = sb("hn", [P, H, DH])
            hw = sb("hw", [P, D])
            x3 = sb("x3", [P, D])
            zn = sb("zn", [P, D])
            zT = sb("zT", [P, KC, T])
            nmx = sb("nmx", [P, 1])
            er = sb("er", [P, E])
            top = sb("top", [P, 8])
            er2 = sb("er2", [P, E])
            sel = sb("sel", [P, E])
            selb = sb("selb", [P, E], BF16)
            selacc = sb("selacc", [P, E], BF16)
            s8 = sb("s8", [P, 1])
            r8 = sb("r8", [P, 1])
            wsel = sb("wsel", [P, E])
            slot1 = sb("slot1", [P, E])
            trash = sb("trash", [P, 1])
            tok_f = sb("tok_f", [P, 1])
            kept = sb("kept", [P, E])
            key = sb("key", [P, E])
            key2 = sb("key2", [P, E])
            key3 = sb("key3", [P, E])
            keys = sb("keys", [P, 8])
            miss = sb("miss", [P, 8])
            slots = sb("slots", [P, 8], U32)
            junk = sb("junk", [P, 8, E])
            pos = sb("pos", [P, E])
            pair = sb("pair", [P, 8, 2], U32)
            cntf = sb("cntf", [P, E])
            zero = sb("zero", [P, 2 * D])

            x1_go = sem("x1_go")
            x1_ready = sem("x1_ready")
            wa_loaded = sem("wa_loaded")
            wg_loaded = sem("wg_loaded")
            small_loaded = sem("small_loaded")
            const_ready = sem("const_ready")
            tabs_ready = sem("tabs_ready")
            act_step = sem("act_step")
            dve_step = sem("dve_step")
            pool_step = sem("pool_step")
            x_loaded = sem("x_loaded")
            ctx_loaded = sem("ctx_loaded")
            x_free = sem("x_free")
            ct_free = sem("ct_free")
            st0 = sem("st0")
            st1 = sem("st1")
            st2 = sem("st2")
            st3 = sem("st3")
            rs0 = sem("rs0")
            rs1 = sem("rs1")
            rs2 = sem("rs2")
            rs3 = sem("rs3")
            kn_ready = sem("kn_ready")
            kT_ps = sem("kT_ps")
            cT_ps = sem("cT_ps")
            e_ready = sem("e_ready")
            g_ready = sem("g_ready")
            c_ready = sem("c_ready")
            vT_ready = sem("vT_ready")
            ctx_used = sem("ctx_used")
            y_ready = sem("y_ready")
            yT_ps = sem("yT_ps")
            xn_ready = sem("xn_ready")
            xnT_ps = sem("xnT_ps")
            xnT_ready = sem("xnT_ready")
            q_ps = sem("q_ps")
            k_ps = sem("k_ps")
            v_ps = sem("v_ps")
            q_ready = sem("q_ready")
            k_ready = sem("k_ready")
            v_ready = sem("v_ready")
            s_ps = sem("s_ps")
            nm_ready = sem("nm_ready")
            p_ready = sem("p_ready")
            pT_ps_dve = sem("pT_ps_dve")
            pT_ps_act = sem("pT_ps_act")
            pT_ready_dve = sem("pT_ready_dve")
            pT_ready_act = sem("pT_ready_act")
            o_ps = sem("o_ps")
            on_ready = sem("on_ready")
            oT_ps = sem("oT_ps")
            oT_ready = sem("oT_ready")
            att_ps = sem("att_ps")
            cd_ctx_free = sem("cd_ctx_free")
            cd_ctx_ready = sem("cd_ctx_ready")
            qn_ready = sem("qn_ready")
            qT_ps = sem("qT_ps")
            qT_ready = sem("qT_ready")
            g_ps = sem("g_ps")
            lf_parts = sem("lf_parts")
            m_ready = sem("m_ready")
            fm_ready = sem("fm_ready")
            efm_ready = sem("efm_ready")
            nT_ps = sem("nT_ps")
            bd_ready = sem("bd_ready")
            l_ps = sem("l_ps")
            d_ready = sem("d_ready")
            qk_ps = sem("qk_ps")
            cm_ready = sem("cm_ready")
            hu_ps = sem("hu_ps")
            hc_ready = sem("hc_ready")
            hsq_ready = sem("hsq_ready")
            hvar_ready = sem("hvar_ready")
            hrs_ready = sem("hrs_ready")
            hn_ready = sem("hn_ready")
            x3_ready = sem("x3_ready")
            x3_go = sem("x3_go")
            x3_stored = sem("x3_stored")
            zn_ready = sem("zn_ready")
            zT_ps = sem("zT_ps")
            zT_ready = sem("zT_ready")
            zn_stored = sem("zn_stored")
            scratch_set = sem("scratch_set")
            pairs_ready = sem("pairs_ready")
            pairs_stored = sem("pairs_stored")
            pairs_free = sem("pairs_free")
            cnt_ps = sem("cnt_ps")
            rl_ps = sem("rl_ps")
            nmx_ready = sem("nmx_ready")
            er_ready = sem("er_ready")
            sel_ready = sem("sel_ready")
            pos_ps = sem("pos_ps")
            wts_scaled = sem("wts_scaled")
            masks_ready = sem("masks_ready")
            zeros_ready = sem("zeros_ready")
            tab_parts = sem("tab_parts")
            scale_parts = sem("scale_parts")
            srs_ready = sem("srs_ready")

            blank = pr[:, :, :, :].rearrange("p a b t -> p (a b t)")[:, 0:2 * SLOTS // P].bitcast(U32)
            wraw = dm[:, :, :, :].rearrange("p a b t -> p (a b t)")
            block = ctx.enter_context(nc.Block())

            @block.sync
            def _(sp):
                sp.dma_start(wch[:, :], w.rearrange("(k p) -> p k", p=P), allow_slow_non_contiguous=True).then_inc(small_loaded, 16)
                sp.dma_start(uch[:, :], u.rearrange("(k p) -> p k", p=P), allow_slow_non_contiguous=True).then_inc(small_loaded, 16)
                sp.dma_start(hs_[:, 0, :], w_std.partition_broadcast(P)).then_inc(small_loaded, 16)
                sp.dma_start(hs_[:, 1, :], w_rec.partition_broadcast(P)).then_inc(small_loaded, 16)
                sp.dma_start(xt[:, :], x[0]).then_inc(x_loaded, 16)
                sp.dma_start(ct[:, :], ctx_in[0]).then_inc(ctx_loaded, 16)
                wa_v = Wa.rearrange("(k p) n -> p k n", p=P)
                q_end, k_end, v_end, ql_end = H * DS, 2 * H * DS, 2 * H * DS + D, 2 * H * DS + D + H * R
                for k in range(KC):
                    for j, (c0, l0) in enumerate([(0, v_end), (q_end, ql_end)]):
                        sp.dma_start(wqk[:, k, j, :, 0:DS],
                                     wa_v[:, k, c0:c0 + H * DS].rearrange("p (h d) -> p h d", h=H)).then_inc(wa_loaded, 16)
                        sp.dma_start(wraw[:, (2 * k + j) * H * R:(2 * k + j + 1) * H * R],
                                     wa_v[:, k, l0:l0 + H * R]).then_inc(wa_loaded, 16)
                sp.dma_start(wv[:, :, :], wa_v[:, :, k_end:v_end]).then_inc(wa_loaded, 16)
                sp.dma_start(wp[:, :, :], Wp.rearrange("(k p) n -> p k n", p=P)).then_inc(wa_loaded, 16)
                sp.wait_ge(zeros_ready, 1)
                sp.sem_inc(zeros_ready, -1)
                for t_ in (acc_d, z_d):
                    sp.dma_start(t_[TOK:TOK + GROUP, :].rearrange("(p a) d -> p (a d)", p=P), zero[:, :])\
                      .then_inc(scratch_set, 16)
                sp.dma_start(slot_d[0:SLOTS, :].rearrange("(p s) c -> p (s c)", p=P), blank)\
                  .then_inc(scratch_set, 16)
                sp.wait_ge(masks_ready, 1)
                sp.sem_inc(masks_ready, -1)
                for a, (W_, c0) in enumerate([(Wi, 0), (Wf, 32)]):
                    v_ = W_.rearrange("(j k p) n -> p j k n", j=3, p=P)
                    for k in range(KC):
                        sp.dma_start(wg[:, 0, k, c0:c0 + H], v_[:, 0, k, :]).then_inc(wg_loaded, 16)
                        sp.dma_start(wg[:, 1, k, c0:c0 + H], v_[:, 1, k, :]).then_inc(wg_loaded, 16)
                        sp.dma_start(cm[:, a, 0, k * H:(k + 1) * H], v_[:, 2, k, :]).then_inc(wg_loaded, 16)
                sp.dma_start(gbias[0:H, :], bi.rearrange("(h a) -> h a", a=1)).then_inc(wg_loaded, 16)
                sp.dma_start(gbias[32:32 + H, :], bf.rearrange("(h a) -> h a", a=1)).then_inc(wg_loaded, 16)
                sp.dma_start(lnsc[:, :], ln_scale.partition_broadcast(P)).then_inc(wg_loaded, 16)
                sp.dma_start(gw[:, :, :], gate_w.rearrange("(k p) e -> p k e", p=P)).then_inc(wg_loaded, 16)

                def load_x(i):
                    sp.wait_ge(x_free, 1)
                    sp.sem_inc(x_free, -1)
                    sp.dma_start(xt[:, :], x[bass.ds(i, 1)].rearrange("a p d -> p (a d)")).then_inc(x_loaded, 16)

                def load_ctx(i):
                    sp.wait_ge(ct_free, 1)
                    sp.sem_inc(ct_free, -1)
                    sp.dma_start(ct[:, :], ctx_in[bass.ds(i, 1)].rearrange("a p d -> p (a d)")).then_inc(ctx_loaded, 16)

                def store(i):
                    sp.wait_ge(x3_go, 1)
                    sp.sem_inc(x3_go, -1)
                    sp.dma_start(acc_d[bass.ds(i * P, P), :], x3[:, :]).then_inc(x3_stored, 16)

                load_x(1)
                load_ctx(1)
                load_x(2)
                with sp.Fori(1, nb - 2) as i:
                    load_ctx(i + 1)
                    load_x(i + 2)
                    store(i - 1)
                load_ctx(nb - 1)
                sp.wait_ge(x_free, 1)
                sp.sem_inc(x_free, -1)
                store(nb - 3)
                sp.wait_ge(ct_free, 1)
                sp.sem_inc(ct_free, -1)
                store(nb - 2)
                store(nb - 1)

            @block.gpsimd
            def _(pool):
                pool.memset(wg[:, :, :, :], 0.0).then_inc(masks_ready, 1)
                pool.memset(ident[:, :], 0.0)
                pool.memset(onesf[:, :], 1.0)
                pool.memset(onesb[:, :], 1.0)
                pool.memset(zerob[:, :, :], 0.0)
                pool.memset(eps5[:, :], 1e-5)
                pool.memset(eps6[:, :], 1e-6)
                pool.memset(nshift[:, :], -K_SHIFT)
                pool.memset(selacc[:, :], 0.0)
                pool.memset(ar[:, :], 0.0)
                pool.memset(ind[:, :, :], 0.0)
                pool.memset(bd[:, :, :, :], 0.0).then_inc(pool_step, 1)
                pool.wait_ge(pool_step, 1)
                pool.sem_inc(pool_step, -1)
                pool.memset(ar[0:H, :], 1.0)
                pool.affine_select(out=ident[:, :], in_=ident[:, :], compare_op=ALU.not_equal, fill=1.0, base=0,
                                   pattern=[[-1, P]], channel_multiplier=1)
                pool.affine_select(out=identb[:, :], in_=zerob[:, 0, :], compare_op=ALU.not_equal, fill=1.0, base=0,
                                   pattern=[[-1, P]], channel_multiplier=1)
                pool.affine_select(out=ustrict[:, :], in_=zerob[:, 0, :], compare_op=ALU.is_ge, fill=1.0, base=0,
                                   pattern=[[-1, P]], channel_multiplier=1)
                pool.affine_select(out=mask_ts[:, :, :], in_=zerob[:, :, :], compare_op=ALU.is_ge, fill=NEG, base=0,
                                   pattern=[[0, 4], [-1, P]], channel_multiplier=1)
                pool.affine_select(out=mask_st[:, :, :], in_=zerob[:, :, :], compare_op=ALU.is_ge, fill=NEG, base=0,
                                   pattern=[[0, 4], [1, P]], channel_multiplier=-1)
                pool.affine_select(out=ind[:, :, :], in_=ind[:, :, :], compare_op=ALU.not_equal, fill=1.0, base=0,
                                   pattern=[[-1, 4], [-4, 4]], channel_multiplier=1).then_inc(pool_step, 1)
                pool.wait_ge(pool_step, 1)
                pool.sem_inc(pool_step, -1)
                pool.affine_select(out=bd[32:32 + H, :, :, :], in_=bd[32:32 + H, :, :, :],
                                   compare_op=ALU.not_equal, fill=1.0, base=0,
                                   pattern=[[-1, 4], [-4, 4], [0, T]], channel_multiplier=1).then_inc(pool_step, 1)
                pool.wait_ge(pool_step, 1)
                pool.sem_inc(pool_step, -1)
                pool.iota(steps[:, :], pattern=[[1, T]], base=0, channel_multiplier=0,
                          allow_small_or_imprecise_dtypes=True).then_inc(pool_step, 1)
                pool.wait_ge(pool_step, 1)
                pool.sem_inc(pool_step, -1)
                pool.memset(zero[:, :], 0.0)
                pool.memset(blank, 0).then_inc(pool_step, 1)
                pool.wait_ge(pool_step, 1)
                pool.sem_inc(pool_step, -1)
                pool.iota(slot1[:, :], pattern=[[CAP // P, E]], base=1, channel_multiplier=0,
                          allow_small_or_imprecise_dtypes=True)
                pool.iota(trash[:, :], pattern=[[1, 1]], base=SLOTS + 1, channel_multiplier=1,
                          allow_small_or_imprecise_dtypes=True)
                pool.iota(tok_f[:, :], pattern=[[1, 1]], base=0, channel_multiplier=1,
                          allow_small_or_imprecise_dtypes=True)
                pool.iota(blank.bitcast(mybir.dt.int32).rearrange("p (a s c) -> p a s c", s=2, c=2)[:, :, :, 0],
                          pattern=[[0, COLS // 2], [P, 2]], base=TOK, channel_multiplier=1).then_inc(pool_step, 1)
                pool.wait_ge(pool_step, 1)
                pool.sem_inc(pool_step, -1)
                pool.sem_inc(zeros_ready, 1)
                pool.sem_inc(x3_stored, 16)
                pool.sem_inc(zn_stored, 16)
                pool.sem_inc(pairs_free, 1)
                pool.sem_inc(cd_ctx_free, 1)
                pool.sem_inc(const_ready, 3)

                def weigh_keys():
                    pool.wait_ge(e_ready, 1)
                    pool.sem_inc(e_ready, -1)
                    pool.tensor_tensor(gg[:, :, :], gam[:, :, :], ex[:, :, :], ALU.mult).then_inc(g_ready, 1)
                    pool.tensor_tensor(cc[:, :, :], zc[:, :, :], ex[:, :, :], ALU.mult).then_inc(c_ready, 1)

                def hold_ctx():
                    pool.wait_ge(ctx_used, 1)
                    pool.sem_inc(ctx_used, -1)
                    pool.tensor_copy(vTk[:, :, :], vT[:, :, :])
                    pool.tensor_copy(ctk[:, :], ct[:, :]).then_inc(pool_step, 1)
                    pool.wait_ge(pool_step, 1)
                    pool.sem_inc(pool_step, -1)
                    pool.sem_inc(ct_free, 1)

                def spread_ctx():
                    pool.wait_ge(cd_ctx_free, 1)
                    pool.sem_inc(cd_ctx_free, -1)
                    pool.tensor_copy(kT2[:, :, :], vTk[:, :, :])
                    pool.tensor_copy(vaug[:, :, 0:DH], ctk[:, :].rearrange("p (h d) -> p h d", h=H)).then_inc(pool_step, 1)
                    pool.wait_ge(pool_step, 1)
                    pool.sem_inc(pool_step, -1)
                    pool.memset(vaug[:, :, DH:DH + 1], 1.0).then_inc(cd_ctx_ready, 1)

                def minus_running_max():
                    pool.wait_ge(m_ready, 1)
                    pool.sem_inc(m_ready, -1)
                    for r in range(4):
                        pool.tensor_tensor(bd[0:H, r, :, :], ind[:, r, :].unsqueeze(2).to_broadcast([H, 4, T]),
                                           ncmx[:, :].unsqueeze(1).to_broadcast([H, 4, T]), ALU.mult).then_inc(bd_ready, 1)

                def second_residual():
                    pool.wait_ge(hn_ready, 1)
                    pool.sem_inc(hn_ready, -1)
                    pool.tensor_tensor(hw[:, :], hn[:, :, :].rearrange("p h d -> p (h d)"), lnsc[:, :], ALU.mult).then_inc(pool_step, 1)
                    pool.wait_ge(pool_step, 1)
                    pool.sem_inc(pool_step, -1)
                    pool.wait_ge(x3_stored, 16)
                    pool.sem_inc(x3_stored, -16)
                    pool.tensor_tensor(x3[:, :], x2[:, :], hw[:, :], ALU.add).then_inc(x3_ready, 1)

                def store_pairs():
                    pool.wait_ge(pairs_ready, 1)
                    pool.sem_inc(pairs_ready, -1)
                    for k in range(8):
                        pool.indirect_dma_start(out=slot_d[:, :], out_offset=bass.IndirectOffsetOnAxis(ap=slots[:, k:k + 1], axis=0),
                                                in_=pair[:, k, :], in_offset=None).then_inc(pairs_stored, 16)

                pool.wait_ge(tabs_ready, 1)
                pool.sem_inc(tabs_ready, -1)
                def pairs_done(n):
                    pool.wait_ge(pairs_stored, n * (16 * 8))
                    pool.sem_inc(pairs_free, 1)

                pool.wait_ge(scratch_set, 48)
                pool.sem_inc(scratch_set, -48)
                def step(ab, cd, pairs, ahead):
                    if ab:
                        hold_ctx()
                    if cd:
                        minus_running_max()
                    if ahead:
                        weigh_keys()
                    if pairs is not None:
                        store_pairs()
                    if ab:
                        spread_ctx()
                    if cd:
                        second_residual()
                    if pairs is not None:
                        pairs_done(pairs)

                weigh_keys()
                step(True, False, None, True)
                step(True, True, None, True)
                with pool.Fori(2, nb - 1) as i:
                    step(True, True, i - 1, True)
                step(True, True, nb - 2, False)
                step(False, True, nb - 1, False)
                store_pairs()
                pairs_done(nb)
                pool.wait_ge(x3_stored, 16)
                pool.sem_inc(x3_stored, -16)

            @block.scalar
            def _(act):
                act.preload_act_table_set("natural_log_exp_and_others")
                act.wait_ge(const_ready, 1)
                act.sem_inc(const_ready, -1)
                act.wait_ge(tab_parts, 1)
                act.sem_inc(tab_parts, -1)
                act.activation(decay[:, :], wneg[:, :], ACT.Exp)
                for k in range(KC):
                    act.activation(gam[:, k, :], steps[:, :], ACT.Exp, scale=nwpos[:, k:k + 1])
                    a = act.activation(zc[:, k, :], zc[:, k, :], ACT.Exp)
                a.then_inc(scale_parts, 1)
                act.wait_ge(tab_parts, 1)
                act.sem_inc(tab_parts, -1)
                act.activation(srl[:, 0:2, :], hs_[:, 0:2, :], ACT.Ln).then_inc(act_step, 1)
                act.wait_ge(act_step, 1)
                act.sem_inc(act_step, -1)
                act.activation(srl[:, 2:4, :], srl[:, 0:2, :], ACT.Exp, scale=0.5).then_inc(srs_ready, 1)

                def rstd_of(n, eps):
                    act.wait_ge((st0, st1, st2, st3)[n], 1)
                    act.sem_inc((st0, st1, st2, st3)[n], -1)
                    act.activation(lnv[n][:, :], mv[n][:, 1:2], ACT.Ln, bias=eps[:, :]).then_inc(act_step, 1)
                    act.wait_ge(act_step, 1)
                    act.sem_inc(act_step, -1)
                    act.activation(rstd[n][:, :], lnv[n][:, :], ACT.Exp, scale=-0.5).then_inc((rs0, rs1, rs2, rs3)[n], 1)

                def exp_k():
                    act.wait_ge(kT_ps, 1)
                    act.sem_inc(kT_ps, -1)
                    act.activation(ex[:, :, :].rearrange("p k t -> p (k t)"), ps[:, 3, :], ACT.Exp,
                                   bias=nshift[:, :]).then_inc(e_ready, 1)

                def vT_copy():
                    act.wait_ge(cT_ps, 1)
                    act.sem_inc(cT_ps, -1)
                    act.activation(vT[:, :, :].rearrange("p k t -> p (k t)"), ps[:, 0, :], ACT.Copy).then_inc(vT_ready, 1)

                def xnT_copy():
                    act.wait_ge(xnT_ps, 1)
                    act.sem_inc(xnT_ps, -1)
                    act.activation(xnT[:, :, :].rearrange("p k t -> p (k t)"), ps[:, 3, :], ACT.Copy).then_inc(xnT_ready, 1)

                def k_copy():
                    act.wait_ge(k_ps, 1)
                    act.sem_inc(k_ps, -1)
                    act.activation(ks[:, :, :].rearrange("p k t -> p (k t)"), ps[:, 1, :], ACT.Copy).then_inc(k_ready, 1)

                def v_copy():
                    act.wait_ge(v_ps, 1)
                    act.sem_inc(v_ps, -1)
                    act.activation(vs[:, :], ps[:, 2, :], ACT.Copy).then_inc(v_ready, 1)

                def exps(r):
                    act.wait_ge(nm_ready, 1)
                    act.sem_inc(nm_ready, -1)
                    bank = (3, 0, 1, 3)[r]
                    for c in range(4):
                        a = act.activation(pr[:, r, c, :], ps[:, bank, c * T:(c + 1) * T], ACT.Exp,
                                           bias=nm[:, r, c:c + 1], accum_out=rsum[:, r, c:c + 1])
                    a.then_inc(p_ready, 1)

                def pT_copy(r):
                    act.wait_ge(pT_ps_act, 1)
                    act.sem_inc(pT_ps_act, -1)
                    bank = (2, 0, 1, 3)[r]
                    act.activation(pT[:, r, :, :].rearrange("p c t -> p (c t)"), ps[:, bank, :], ACT.Copy)\
                       .then_inc(pT_ready_act, 1)

                def oT_copy():
                    act.wait_ge(oT_ps, 1)
                    act.sem_inc(oT_ps, -1)
                    act.activation(oT[:, :, :].rearrange("p k t -> p (k t)"), ps[:, 0, :], ACT.Copy).then_inc(oT_ready, 1)

                def qT_copy():
                    act.wait_ge(qT_ps, 1)
                    act.sem_inc(qT_ps, -1)
                    act.activation(qT[:, :, :].rearrange("p k t -> p (k t)"), ps[:, 4, :], ACT.Copy).then_inc(qT_ready, 1)

                def log_gates():
                    act.wait_ge(g_ps, 1)
                    act.sem_inc(g_ps, -1)
                    act.activation(ig[:, :], ps[0:H, 4, 0:T], ACT.Identity, bias=gbias[0:H, :])
                    act.activation(fg[:, :], ps[32:32 + H, 4, 0:T], ACT.Identity, bias=gbias[32:32 + H, :]).then_inc(act_step, 1)
                    act.wait_ge(act_step, 1)
                    act.sem_inc(act_step, -1)
                    act.activation(fa[:, :], fg[:, :], ACT.Abs).then_inc(act_step, 1)
                    act.wait_ge(act_step, 1)
                    act.sem_inc(act_step, -1)
                    act.activation(fe[:, :], fa[:, :], ACT.Exp, scale=-1.0).then_inc(act_step, 1)
                    act.wait_ge(act_step, 1)
                    act.sem_inc(act_step, -1)
                    act.activation(fl[:, :], fe[:, :], ACT.Ln, bias=1.0).then_inc(lf_parts, 1)

                def efm_part():
                    act.wait_ge(fm_ready, 1)
                    act.sem_inc(fm_ready, -1)
                    act.activation(efm[:, :], fm[:, :], ACT.Exp, scale=-1.0).then_inc(efm_ready, 1)

                def exp_log_d(rs):
                    for r in rs:
                        act.wait_ge(l_ps, 1)
                        act.sem_inc(l_ps, -1)
                        act.activation(dm[:, r, :, :].rearrange("p c t -> p (c t)"), ps[:, (4, 6)[r % 2], :],
                                       ACT.Exp).then_inc(d_ready, 1)

                def squares():
                    act.wait_ge(hc_ready, 1)
                    act.sem_inc(hc_ready, -1)
                    act.activation(hsq[:, :, :], hc[:, :, :], ACT.Square).then_inc(hsq_ready, 1)

                def head_rstd():
                    act.wait_ge(hvar_ready, 1)
                    act.sem_inc(hvar_ready, -1)
                    act.activation(hlv[:, :], hvar[:, :], ACT.Ln, scale=1.0 / DH, bias=eps6[:, :]).then_inc(act_step, 1)
                    act.wait_ge(act_step, 1)
                    act.sem_inc(act_step, -1)
                    act.activation(hrs[:, :], hlv[:, :], ACT.Exp, scale=-0.5).then_inc(hrs_ready, 1)

                def zT_copy(i):
                    act.wait_ge(zT_ps, 1)
                    act.sem_inc(zT_ps, -1)
                    act.activation(zT[:, :, :].rearrange("p k t -> p (k t)"), ps[:, 6, :], ACT.Copy).then_inc(zT_ready, 1)
                    act.dma_start(z_d[bass.ds(i * P, P), :], zn[:, :]).then_inc(zn_stored, 16)

                def router_exp():
                    act.wait_ge(nmx_ready, 1)
                    act.sem_inc(nmx_ready, -1)
                    act.activation(er[:, :], ps[:, 7, 0:E], ACT.Exp, bias=nmx[:, :]).then_inc(er_ready, 1)

                def x1_copy():
                    act.wait_ge(x1_go, 1)
                    act.sem_inc(x1_go, -1)
                    act.activation(x1[:, :], x1n[:, :], ACT.Copy).then_inc(x1_ready, 1)

                def step(ab, cd, before, ahead):
                    if cd:
                        rstd_of(2, eps5)
                        qT_copy()
                    if ab:
                        x1_copy()
                    if cd:
                        log_gates()
                    if ahead:
                        rstd_of(0, eps5)
                    if ab:
                        k_copy()
                    if ahead:
                        exp_k()
                        vT_copy()
                    if cd:
                        efm_part()
                        exp_log_d((0, 1))
                    if ab:
                        v_copy()
                    if cd:
                        exp_log_d((2, 3))
                    if ab:
                        exps(0)
                        exps(1)
                        exps(2)
                    if cd:
                        squares()
                    if ab:
                        pT_copy(1)
                    if cd:
                        head_rstd()
                    if ab:
                        exps(3)
                        pT_copy(3)
                    if ahead:
                        rstd_of(1, eps5)
                    if cd:
                        rstd_of(3, eps5)
                    if ahead:
                        xnT_copy()
                    if cd:
                        zT_copy(before)
                    if ab:
                        oT_copy()
                    if cd:
                        router_exp()

                rstd_of(0, eps5)
                exp_k()
                vT_copy()
                rstd_of(1, eps5)
                xnT_copy()
                step(True, False, None, True)
                step(True, True, 0, True)
                with act.Fori(2, nb - 1) as i:
                    step(True, True, i - 1, True)
                step(True, True, nb - 2, False)
                step(False, True, nb - 1, False)

            @block.tensor
            def _(pe):
                pe.wait_ge(const_ready, 1)
                pe.sem_inc(const_ready, -1)

                def turn(bank, src, signal):
                    for c in range(4):
                        m = pe.transpose(ps[:, bank, c * P:(c + 1) * P], src(c), ident[:, :])
                    m.then_inc(signal, 1)

                def k_turn():
                    pe.wait_ge(kn_ready, 1)
                    pe.sem_inc(kn_ready, -1)
                    turn(3, lambda c: kn[:, c * P:(c + 1) * P], kT_ps)

                def ctx_turn():
                    pe.wait_ge(ctx_loaded, 16)
                    pe.sem_inc(ctx_loaded, -16)
                    turn(0, lambda c: ct[:, c * P:(c + 1) * P], cT_ps)

                def y_turn():
                    pe.wait_ge(y_ready, 1)
                    pe.sem_inc(y_ready, -1)
                    turn(7, lambda c: yy[:, c, :], yT_ps)

                def xn_turn():
                    pe.wait_ge(xn_ready, 1)
                    pe.sem_inc(xn_ready, -1)
                    turn(3, lambda c: xn[:, c * P:(c + 1) * P], xnT_ps)

                def head_product(j, signal):
                    for c in range(4):
                        for k in range(KC):
                            m = pe.matmul(ps[:, j, c * T:(c + 1) * T],
                                          wqk[:, k, j, 4 * c:4 * c + 4, :].rearrange("p h d -> p (h d)"),
                                          xnT[:, k, :], start=(k == 0), stop=(k == KC - 1))
                    m.then_inc(signal, 1)

                def q():
                    pe.wait_ge(xnT_ready, 1)
                    pe.sem_inc(xnT_ready, -1)
                    head_product(0, q_ps)

                def k():
                    head_product(1, k_ps)
                    pe.wait_ge(q_ready, 1)
                    pe.sem_inc(q_ready, -1)

                def v():
                    for k in range(KC):
                        m = pe.matmul(ps[:, 2, :], xnT[:, k, :], wv[:, k, :], start=(k == 0), stop=(k == KC - 1))
                    m.then_inc(v_ps, 1)

                def scores(r):
                    bank = (3, 0, 1, 3)[r]
                    pe.matmul(ps[:, bank, :], identb[:, :], mask_ts[:, :, :].rearrange("p a t -> p (a t)"),
                              start=True, stop=False, skip_group_check=True)
                    for c in range(4):
                        m = pe.matmul(ps[:, bank, c * T:(c + 1) * T], qs[32 * r:32 * r + 32, c, :],
                                      ks[32 * r:32 * r + 32, c, :], start=False, stop=True, skip_group_check=True)
                    m.then_inc(s_ps, 1)

                def p_turn(r):
                    pe.wait_ge(p_ready, 1)
                    pe.sem_inc(p_ready, -1)
                    bank = (2, 0, 1, 3)[r]
                    turn(bank, lambda c: pr[:, r, c, :], (pT_ps_dve, pT_ps_act)[r % 2])

                def weighted_v(rs):
                    for r in rs:
                        pe.wait_ge((pT_ready_dve, pT_ready_act)[r % 2], 1)
                        pe.sem_inc((pT_ready_dve, pT_ready_act)[r % 2], -1)
                        for c in range(4):
                            h = 4 * c + r
                            m = pe.matmul(ps[:, 2, h * DH:(h + 1) * DH], pT[:, r, c, :], vs[:, h * DH:(h + 1) * DH],
                                          start=True, stop=True)
                    return m

                def o_turn():
                    pe.wait_ge(on_ready, 1)
                    pe.sem_inc(on_ready, -1)
                    turn(0, lambda c: on[:, c * P:(c + 1) * P], oT_ps)

                def project():
                    pe.wait_ge(oT_ready, 1)
                    pe.sem_inc(oT_ready, -1)
                    for k in range(KC):
                        m = pe.matmul(ps[:, 1, :], oT[:, k, :], wp[:, k, :], start=(k == 0), stop=(k == KC - 1))
                    m.then_inc(att_ps, 1)

                def query_turn():
                    pe.wait_ge(qn_ready, 1)
                    pe.sem_inc(qn_ready, -1)
                    turn(4, lambda c: qn[:, c * P:(c + 1) * P], qT_ps)

                def gates():
                    pe.wait_ge(cd_ctx_ready, 1)
                    pe.sem_inc(cd_ctx_ready, -1)
                    pe.wait_ge(qT_ready, 1)
                    pe.sem_inc(qT_ready, -1)
                    for j in range(2):
                        for k in range(KC):
                            m = pe.matmul(ps[0:48, 4, 0:T], wg[:, j, k, :], (qT, kT2)[j][:, k, :],
                                          start=(j == 0 and k == 0), stop=(j == 1 and k == KC - 1))
                    m.then_inc(g_ps, 1)

                def qk(r):
                    for c in range(4):
                        m = pe.matmul(ps[:, (5, 7)[r % 2], c * T:(c + 1) * T], kT2[32 * r:32 * r + 32, c, :],
                                      qT[32 * r:32 * r + 32, c, :], start=True, stop=True)
                    m.then_inc(qk_ps, 1)

                def log_d(r):
                    lb = (4, 6)[r % 2]
                    pe.wait_ge(bd_ready, 1)
                    pe.sem_inc(bd_ready, -1)
                    pe.matmul(ps[:, lb, :], identb[:, :], mask_st[:, :, :].rearrange("p a t -> p (a t)"),
                              start=True, stop=False, skip_group_check=True)
                    pe.matmul(ps[:, lb, :], ar[:, :], bd[:, r, :, :].rearrange("h c t -> h (c t)"),
                              start=False, stop=True, skip_group_check=True).then_inc(l_ps, 1)

                def head_sums():
                    pe.wait_ge(efm_ready, 1)
                    pe.sem_inc(efm_ready, -1)
                    pe.transpose(ps[:, 6, 0:H], efm[:, :], ident[0:H, 0:H]).then_inc(nT_ps, 1)
                    for h in range(H):
                        r, c = h % 4, h // 4
                        o = (h % 8) * (DH + 1)
                        m = pe.matmul(ps[:, 4 + h // 8, o:o + DH + 1], cm[:, r, c, :], vaug[:, h, :],
                                      start=True, stop=True)
                    m.then_inc(hu_ps, 1)

                def z_turn():
                    pe.wait_ge(zn_ready, 1)
                    pe.sem_inc(zn_ready, -1)
                    turn(6, lambda c: zn[:, c * P:(c + 1) * P], zT_ps)

                def router():
                    pe.wait_ge(zT_ready, 1)
                    pe.sem_inc(zT_ready, -1)
                    for k in range(KC):
                        m = pe.matmul(ps[:, 7, 0:E], zT[:, k, :], gw[:, k, :], start=(k == 0), stop=(k == KC - 1))
                    m.then_inc(rl_ps, 1)

                def places():
                    pe.wait_ge(sel_ready, 1)
                    pe.sem_inc(sel_ready, -1)
                    pe.matmul(ps[:, 7, 64:64 + E], ustrict[:, :], selb[:, :], start=True, stop=False)
                    pe.matmul(ps[:, 7, 64:64 + E], onesb[:, :], selacc[:, :], start=False, stop=True).then_inc(pos_ps, 1)

                def step(ab, cd, ahead):
                    if cd:
                        query_turn()
                        gates()
                        qk(0)
                        qk(1)
                    if ab:
                        k()
                    if ahead:
                        k_turn()
                        ctx_turn()
                    if cd:
                        log_d(0)
                        log_d(1)
                    if ab:
                        v()
                    if cd:
                        for r in (2, 3):
                            pe.wait_ge(cm_ready, 1)
                            pe.sem_inc(cm_ready, -1)
                            qk(r)
                            log_d(r)
                    if ab:
                        pe.wait_ge(k_ready, 1)
                        pe.sem_inc(k_ready, -1)
                        pe.wait_ge(v_ready, 1)
                        pe.sem_inc(v_ready, -1)
                        scores(0)
                        scores(1)
                    if cd:
                        for n in range(2):
                            pe.wait_ge(cm_ready, 1)
                            pe.sem_inc(cm_ready, -1)
                        head_sums()
                    if ab:
                        scores(2)
                        p_turn(0)
                        scores(3)
                        p_turn(1)
                        p_turn(2)
                    if ahead:
                        y_turn()
                    if ab:
                        weighted_v((0, 1))
                        p_turn(3)
                        weighted_v((2, 3)).then_inc(o_ps, 1)
                    if ahead:
                        xn_turn()
                    if cd:
                        z_turn()
                    if ab:
                        o_turn()
                    if cd:
                        router()
                    if ab:
                        project()
                    if ahead:
                        q()
                    if cd:
                        places()

                k_turn()
                ctx_turn()
                y_turn()
                xn_turn()
                pe.wait_ge(wts_scaled, 1)
                pe.sem_inc(wts_scaled, -1)
                q()
                step(True, False, True)
                step(True, True, True)
                with pe.Fori(2, nb - 1):
                    step(True, True, True)
                step(True, True, False)
                step(False, True, False)
                pe.wait_ge(sel_ready, 1)
                pe.sem_inc(sel_ready, -1)
                pe.matmul(ps[:, 7, 0:E], onesb[:, :], selacc[:, :], start=True, stop=True).then_inc(cnt_ps, 1)

            @block.vector
            def _(dve):
                dve.wait_ge(const_ready, 1)
                dve.sem_inc(const_ready, -1)
                dve.wait_ge(small_loaded, 64)
                dve.sem_inc(small_loaded, -64)
                dve.tensor_scalar(wpos[:, :], wch[:, :], 0.0, None, ALU.max).then_inc(dve_step, 1)
                dve.wait_ge(dve_step, 1)
                dve.sem_inc(dve_step, -1)
                dve.tensor_scalar(nwpos[:, :], wch[:, :], 0.0, -1.0, ALU.max, ALU.mult)
                dve.tensor_scalar(wneg[:, :], wch[:, :], 0.0, None, ALU.min).then_inc(dve_step, 1)
                dve.wait_ge(dve_step, 1)
                dve.sem_inc(dve_step, -1)
                dve.tensor_tensor(uw[:, :], uch[:, :], wpos[:, :], ALU.add).then_inc(dve_step, 1)
                dve.wait_ge(dve_step, 1)
                dve.sem_inc(dve_step, -1)
                for k in range(KC):
                    dve.tensor_scalar(zc[:, k, :], steps[:, :], nwpos[:, k:k + 1], uw[:, k:k + 1], ALU.mult, ALU.add).then_inc(dve_step, 1)
                    dve.wait_ge(dve_step, 1)
                    dve.sem_inc(dve_step, -1)
                dve.tensor_scalar(zc[:, :, :], zc[:, :, :], U_CAP, None, ALU.min).then_inc(dve_step, 1)
                dve.wait_ge(dve_step, 1)
                dve.sem_inc(dve_step, -1)
                dve.sem_inc(tab_parts, 1)
                dve.tensor_scalar(hs_[:, 2, :], hs_[:, 1, :], THRESH, None, ALU.is_gt).then_inc(dve_step, 1)
                dve.wait_ge(dve_step, 1)
                dve.sem_inc(dve_step, -1)
                dve.tensor_scalar(hs_[:, 0:2, :], hs_[:, 0:2, :], 1e-8, None, ALU.max).then_inc(dve_step, 1)
                dve.wait_ge(dve_step, 1)
                dve.sem_inc(dve_step, -1)
                dve.sem_inc(tab_parts, 1)
                dve.wait_ge(scale_parts, 1)
                dve.sem_inc(scale_parts, -1)
                for k in range(KC):
                    dve.tensor_scalar(dtab[:, k, :], onesf[:, :], decay[:, k:k + 1], None, ALU.mult).then_inc(dve_step, 1)
                    dve.wait_ge(dve_step, 1)
                    dve.sem_inc(dve_step, -1)
                dve.memset(zc[:, :, 0:1], 1.0).then_inc(dve_step, 1)
                dve.wait_ge(dve_step, 1)
                dve.sem_inc(dve_step, -1)
                dve.memset(dtab[:, :, 0:1], 0.0).then_inc(dve_step, 1)
                dve.wait_ge(dve_step, 1)
                dve.sem_inc(dve_step, -1)
                dve.sem_inc(tabs_ready, 1)

                def stats(n, src):
                    dve.bn_stats(st[n][:, :], src).then_inc(dve_step, 1)
                    dve.wait_ge(dve_step, 1)
                    dve.sem_inc(dve_step, -1)
                    dve.bn_aggr(mv[n][:, :], st[n][:, :]).then_inc((st0, st1, st2, st3)[n], 1)

                def norm(n, src, dst, signal):
                    dve.wait_ge((rs0, rs1, rs2, rs3)[n], 1)
                    dve.sem_inc((rs0, rs1, rs2, rs3)[n], -1)
                    dve.tensor_scalar(dst, src, mv[n][:, 0:1], rstd[n][:, 0:1], ALU.subtract, ALU.mult).then_inc(signal, 1)

                def flat(t):
                    return t[:, :, :].rearrange("p k t -> p (k t)")

                def key_stats():
                    dve.wait_ge(x_loaded, 16)
                    dve.sem_inc(x_loaded, -16)
                    stats(0, xt[:, :])

                def key_norm():
                    norm(0, xt[:, :], kn[:, :], kn_ready)

                key_stats()
                key_norm()
                dve.wait_ge(srs_ready, 1)
                dve.sem_inc(srs_ready, -1)
                dve.tensor_copy(sst[:, :], srl[:, 2, :]).then_inc(dve_step, 1)
                dve.wait_ge(dve_step, 1)
                dve.sem_inc(dve_step, -1)
                dve.tensor_copy(srl[:, 0, :], srl[:, 3, :]).then_inc(dve_step, 1)
                dve.wait_ge(dve_step, 1)
                dve.sem_inc(dve_step, -1)
                dve.tensor_tensor(srl[:, 1, :], srl[:, 3, :], hs_[:, 2, :], ALU.mult).then_inc(dve_step, 1)
                dve.wait_ge(dve_step, 1)
                dve.sem_inc(dve_step, -1)
                dve.tensor_tensor(srl[:, 0, :], srl[:, 0, :], srl[:, 1, :], ALU.subtract).then_inc(dve_step, 1)
                dve.wait_ge(dve_step, 1)
                dve.sem_inc(dve_step, -1)
                dve.wait_ge(wa_loaded, 16 * (4 * KC + 2))
                dve.sem_inc(wa_loaded, -(16 * (4 * KC + 2)))
                for k in range(KC):
                    low = [wraw[:, (2 * k + j) * H * R:(2 * k + j + 1) * H * R].rearrange("p (h d) -> p h d", h=H)
                           for j in range(2)]
                    m_ = srl[:, 1, :].unsqueeze(2).to_broadcast([P, H, R])
                    n_ = srl[:, 0, :].unsqueeze(2).to_broadcast([P, H, R])
                    tail = [[cm[:, j, n, :].rearrange("p (h d) -> p h d", h=H) for n in (2, 3)] for j in range(2)]
                    for j in range(2):
                        dve.tensor_tensor(wqk[:, k, j, :, 0:DS], wqk[:, k, j, :, 0:DS],
                                          sst[:, :].unsqueeze(2).to_broadcast([P, H, DS]), ALU.mult)
                        dve.tensor_tensor(tail[j][0], low[1 - j], m_, ALU.mult)
                        a = dve.tensor_tensor(tail[j][1], low[j], n_, ALU.mult)
                    a.then_inc(dve_step, 1)
                    dve.wait_ge(dve_step, 1)
                    dve.sem_inc(dve_step, -1)
                    for j in range(2):
                        a = dve.tensor_tensor(wqk[:, k, j, :, DS:DH], tail[j][0], tail[j][1], ALU.add)
                    a.then_inc(dve_step, 1)
                    dve.wait_ge(dve_step, 1)
                    dve.sem_inc(dve_step, -1)
                    dve.tensor_scalar(wqk[:, k, 0, :, :], wqk[:, k, 0, :, :], QSCALE, None, ALU.mult).then_inc(dve_step, 1)
                    dve.wait_ge(dve_step, 1)
                    dve.sem_inc(dve_step, -1)
                dve.wait_ge(wg_loaded, 16 * (6 * KC + 4))
                dve.sem_inc(wg_loaded, -(16 * (6 * KC + 4)))
                for a, c0 in enumerate((0, 32)):
                    dve.tensor_tensor(wg[:, 1, :, c0:c0 + H], wg[:, 1, :, c0:c0 + H],
                                      cm[:, a, 0, 0:KC * H].rearrange("p (k n) -> p k n", k=KC), ALU.add).then_inc(dve_step, 1)
                    dve.wait_ge(dve_step, 1)
                    dve.sem_inc(dve_step, -1)
                dve.sem_inc(wts_scaled, 1)

                def wkv_terms():
                    dve.wait_ge(vT_ready, 1)
                    dve.sem_inc(vT_ready, -1)
                    dve.wait_ge(g_ready, 1)
                    dve.sem_inc(g_ready, -1)
                    dve.tensor_tensor(gv[:, :, :], gg[:, :, :], vT[:, :, :], ALU.mult).then_inc(dve_step, 1)
                    dve.wait_ge(dve_step, 1)
                    dve.sem_inc(dve_step, -1)
                    dve.wait_ge(c_ready, 1)
                    dve.sem_inc(c_ready, -1)
                    dve.tensor_tensor(cv[:, :, :], cc[:, :, :], vT[:, :, :], ALU.mult).then_inc(ctx_used, 1)

                def wkv_scans():
                    dve.tensor_tensor_scan(flat(sq_), flat(dtab), flat(gg), 0.0, ALU.mult, ALU.add)
                    dve.tensor_tensor_scan(flat(sp_), flat(dtab), flat(gv), 0.0, ALU.mult, ALU.add).then_inc(dve_step, 1)
                    dve.wait_ge(dve_step, 1)
                    dve.sem_inc(dve_step, -1)
                    dve.tensor_tensor(cc[:, :, 1:T], cc[:, :, 1:T], sq_[:, :, 0:T - 1], ALU.add)
                    dve.tensor_tensor(cv[:, :, 1:T], cv[:, :, 1:T], sp_[:, :, 0:T - 1], ALU.add).then_inc(dve_step, 1)
                    dve.wait_ge(dve_step, 1)
                    dve.sem_inc(dve_step, -1)

                def wkv_ratio():
                    dve.reciprocal(rden[:, :, :], cc[:, :, :]).then_inc(dve_step, 1)
                    dve.wait_ge(dve_step, 1)
                    dve.sem_inc(dve_step, -1)
                    dve.tensor_tensor(yy[:, :, :], cv[:, :, :], rden[:, :, :], ALU.mult).then_inc(y_ready, 1)

                def first_residual():
                    dve.wait_ge(yT_ps, 1)
                    dve.sem_inc(yT_ps, -1)
                    dve.tensor_tensor(x1n[:, :], xt[:, :], ps[:, 7, :], ALU.add).then_inc(dve_step, 1)
                    dve.wait_ge(dve_step, 1)
                    dve.sem_inc(dve_step, -1)
                    dve.sem_inc(x_free, 1)
                    stats(1, x1n[:, :])

                def q_copy():
                    dve.wait_ge(q_ps, 1)
                    dve.sem_inc(q_ps, -1)
                    dve.tensor_copy(flat(qs), ps[:, 0, :]).then_inc(q_ready, 1)

                def row_max(r):
                    dve.wait_ge(s_ps, 1)
                    dve.sem_inc(s_ps, -1)
                    bank = (3, 0, 1, 3)[r]
                    dve.tensor_reduce(nm[:, r, :], ps[:, bank, :].rearrange("p (c t) -> p c t", c=4), AX.X, ALU.max,
                                      negate=True).then_inc(nm_ready, 1)

                def pT_copy(r):
                    dve.wait_ge(pT_ps_dve, 1)
                    dve.sem_inc(pT_ps_dve, -1)
                    bank = (2, 0, 1, 3)[r]
                    dve.tensor_copy(pT[:, r, :, :].rearrange("p c t -> p (c t)"), ps[:, bank, :]).then_inc(pT_ready_dve, 1)

                def divide_by_row_sums():
                    dve.wait_ge(o_ps, 1)
                    dve.sem_inc(o_ps, -1)
                    dve.reciprocal(rinv[:, :, :], rsum[:, :, :]).then_inc(dve_step, 1)
                    dve.wait_ge(dve_step, 1)
                    dve.sem_inc(dve_step, -1)
                    dve.tensor_tensor(on[:, :].rearrange("p (c r d) -> p r c d", c=4, r=4),
                                      ps[:, 2, :].rearrange("p (c r d) -> p r c d", c=4, r=4),
                                      rinv[:, :, :].unsqueeze(3).to_broadcast([P, 4, 4, DH]), ALU.mult).then_inc(on_ready, 1)

                def add_attention():
                    dve.wait_ge(x1_ready, 1)
                    dve.sem_inc(x1_ready, -1)
                    dve.wait_ge(att_ps, 1)
                    dve.sem_inc(att_ps, -1)
                    dve.tensor_tensor(x2[:, :], x1[:, :], ps[:, 1, :], ALU.add).then_inc(dve_step, 1)
                    dve.wait_ge(dve_step, 1)
                    dve.sem_inc(dve_step, -1)

                def gate_sums():
                    dve.wait_ge(lf_parts, 1)
                    dve.sem_inc(lf_parts, -1)
                    dve.scalar_tensor_tensor(lf[:, :], fg[:, :], 0.0, fl[:, :], ALU.min, ALU.subtract).then_inc(dve_step, 1)
                    dve.wait_ge(dve_step, 1)
                    dve.sem_inc(dve_step, -1)
                    dve.tensor_tensor_scan(cum[:, :], onesf[0:H, :], lf[:, :], 0.0, ALU.mult, ALU.add).then_inc(dve_step, 1)
                    dve.wait_ge(dve_step, 1)
                    dve.sem_inc(dve_step, -1)
                    dve.tensor_tensor(ar[32:32 + H, :], ig[:, :], cum[:, :], ALU.subtract).then_inc(dve_step, 1)
                    dve.wait_ge(dve_step, 1)
                    dve.sem_inc(dve_step, -1)
                    dve.tensor_tensor_scan(cmx[:, :], onesf[32:32 + H, :], ar[32:32 + H, :], -3.0e38, ALU.mult, ALU.max).then_inc(dve_step, 1)
                    dve.wait_ge(dve_step, 1)
                    dve.sem_inc(dve_step, -1)
                    dve.tensor_scalar(ncmx[:, :], cmx[:, :], -1.0, None, ALU.mult).then_inc(m_ready, 1)
                    dve.tensor_tensor(fm[:, :], cum[:, :], cmx[:, :], ALU.add).then_inc(dve_step, 1)
                    dve.wait_ge(dve_step, 1)
                    dve.sem_inc(dve_step, -1)
                    dve.tensor_scalar(fm[:, :], fm[:, :], -86.0, None, ALU.max).then_inc(fm_ready, 1)

                def decayed_scores(rs):
                    for r in rs:
                        dve.wait_ge(d_ready, 1)
                        dve.sem_inc(d_ready, -1)
                        dve.wait_ge(qk_ps, 1)
                        dve.sem_inc(qk_ps, -1)
                        dve.scalar_tensor_tensor(cm[:, r, :, :].rearrange("p c t -> p (c t)"), ps[:, (5, 7)[r % 2], :], QSCALE,
                                                 dm[:, r, :, :].rearrange("p c t -> p (c t)"), ALU.mult, ALU.mult)\
                           .then_inc(cm_ready, 1)

                def wide(t, n):
                    return t[:, :].unsqueeze(2).to_broadcast([P, H, n])

                def normalize_heads():
                    dve.wait_ge(nT_ps, 1)
                    dve.sem_inc(nT_ps, -1)
                    dve.tensor_copy(enT[:, :], ps[:, 6, 0:H]).then_inc(dve_step, 1)
                    dve.wait_ge(dve_step, 1)
                    dve.sem_inc(dve_step, -1)
                    dve.wait_ge(hu_ps, 1)
                    dve.sem_inc(hu_ps, -1)
                    dve.sem_inc(cd_ctx_free, 1)
                    raw = ps[:, 4:6, 0:8 * (DH + 1)].rearrange("p b (h e) -> p b h e", e=DH + 1)
                    half = [t[:, :].rearrange("p (b h) -> p b h", b=2) for t in (nrm, nrm2, enT)]
                    dve.scalar_tensor_tensor(half[0], raw[:, :, :, DH], -1.0, half[2], ALU.mult, ALU.max).then_inc(dve_step, 1)
                    dve.wait_ge(dve_step, 1)
                    dve.sem_inc(dve_step, -1)
                    dve.tensor_tensor(half[1], half[0], raw[:, :, :, DH], ALU.max).then_inc(dve_step, 1)
                    dve.wait_ge(dve_step, 1)
                    dve.sem_inc(dve_step, -1)
                    dve.tensor_scalar(nrm[:, :], nrm2[:, :], 1e-6, None, ALU.add).then_inc(dve_step, 1)
                    dve.wait_ge(dve_step, 1)
                    dve.sem_inc(dve_step, -1)
                    dve.reciprocal(rn[:, :], nrm[:, :]).then_inc(dve_step, 1)
                    dve.wait_ge(dve_step, 1)
                    dve.sem_inc(dve_step, -1)
                    dve.tensor_tensor(hh[:, :, :].rearrange("p (b h) d -> p b h d", b=2), raw[:, :, :, 0:DH],
                                      rn[:, :].rearrange("p (b h) -> p b h", b=2).unsqueeze(3).to_broadcast([P, 2, 8, DH]),
                                      ALU.mult).then_inc(dve_step, 1)
                    dve.wait_ge(dve_step, 1)
                    dve.sem_inc(dve_step, -1)

                def head_mean():
                    dve.tensor_reduce(hmu[:, :], hh[:, :, :], AX.X, ALU.add).then_inc(dve_step, 1)
                    dve.wait_ge(dve_step, 1)
                    dve.sem_inc(dve_step, -1)
                    dve.tensor_scalar(hmu2[:, :], hmu[:, :], 1.0 / DH, None, ALU.mult).then_inc(dve_step, 1)
                    dve.wait_ge(dve_step, 1)
                    dve.sem_inc(dve_step, -1)
                    dve.tensor_tensor(hc[:, :, :], hh[:, :, :], wide(hmu2, DH), ALU.subtract).then_inc(hc_ready, 1)

                def head_var():
                    dve.wait_ge(hsq_ready, 1)
                    dve.sem_inc(hsq_ready, -1)
                    dve.tensor_reduce(hvar[:, :], hsq[:, :, :], AX.X, ALU.add).then_inc(hvar_ready, 1)

                def head_norm():
                    dve.wait_ge(hrs_ready, 1)
                    dve.sem_inc(hrs_ready, -1)
                    dve.tensor_tensor(hn[:, :, :], hc[:, :, :], wide(hrs, DH), ALU.mult).then_inc(hn_ready, 1)

                def third_stats():
                    dve.wait_ge(x3_ready, 1)
                    dve.sem_inc(x3_ready, -1)
                    dve.sem_inc(x3_go, 1)
                    stats(3, x3[:, :])

                def third_norm():
                    dve.wait_ge(zn_stored, 16)
                    dve.sem_inc(zn_stored, -16)
                    norm(3, x3[:, :], zn[:, :], zn_ready)

                def router_max():
                    dve.wait_ge(rl_ps, 1)
                    dve.sem_inc(rl_ps, -1)
                    dve.tensor_reduce(nmx[:, :], ps[:, 7, 0:E], AX.X, ALU.max, negate=True).then_inc(nmx_ready, 1)

                def choose():
                    dve.wait_ge(er_ready, 1)
                    dve.sem_inc(er_ready, -1)
                    dve.max(top[:, :], er[:, :]).then_inc(dve_step, 1)
                    dve.wait_ge(dve_step, 1)
                    dve.sem_inc(dve_step, -1)
                    dve.match_replace(er2[:, :], top[:, :], er[:, :], -1.0).then_inc(dve_step, 1)
                    dve.wait_ge(dve_step, 1)
                    dve.sem_inc(dve_step, -1)
                    dve.tensor_scalar(sel[:, :], er2[:, :], 0.0, None, ALU.is_lt)
                    dve.tensor_scalar(selb[:, :], er2[:, :], 0.0, None, ALU.is_lt).then_inc(sel_ready, 1)

                def take_places():
                    dve.wait_ge(pos_ps, 1)
                    dve.sem_inc(pos_ps, -1)
                    dve.tensor_copy(pos[:, :], ps[:, 7, 64:64 + E])
                    dve.tensor_tensor(selacc[:, :], selacc[:, :], selb[:, :], ALU.add)

                def make_pairs():
                    dve.tensor_reduce(s8[:, :], top[:, :], AX.X, ALU.add).then_inc(dve_step, 1)
                    dve.wait_ge(dve_step, 1)
                    dve.sem_inc(dve_step, -1)
                    dve.reciprocal(r8[:, :], s8[:, :]).then_inc(dve_step, 1)
                    dve.wait_ge(dve_step, 1)
                    dve.sem_inc(dve_step, -1)
                    dve.tensor_scalar(wsel[:, :], er[:, :], r8[:, :], 1.0 / WSC, ALU.mult, ALU.mult).then_inc(dve_step, 1)
                    dve.wait_ge(dve_step, 1)
                    dve.sem_inc(dve_step, -1)
                    dve.scalar_tensor_tensor(kept[:, :], pos[:, :], float(CAP), sel[:, :], ALU.is_lt, ALU.mult)
                    dve.tensor_scalar(key3[:, :], pos[:, :], 0.5 - P / 2, 1.0 / P, ALU.add, ALU.mult).then_inc(dve_step, 1)
                    dve.wait_ge(dve_step, 1)
                    dve.sem_inc(dve_step, -1)
                    dve.scalar_tensor_tensor(key2[:, :], pos[:, :], float(COLS), slot1[:, :], ALU.mult, ALU.add)
                    dve.tensor_scalar(key3[:, :], key3[:, :], ROUND, None, ALU.add).then_inc(dve_step, 1)
                    dve.wait_ge(dve_step, 1)
                    dve.sem_inc(dve_step, -1)
                    dve.tensor_scalar(key3[:, :], key3[:, :], ROUND, 1.0 - P * COLS, ALU.subtract, ALU.mult).then_inc(dve_step, 1)
                    dve.wait_ge(dve_step, 1)
                    dve.sem_inc(dve_step, -1)
                    dve.tensor_tensor(key[:, :], key2[:, :], key3[:, :], ALU.add).then_inc(dve_step, 1)
                    dve.wait_ge(dve_step, 1)
                    dve.sem_inc(dve_step, -1)
                    dve.tensor_tensor(key2[:, :], key[:, :], kept[:, :], ALU.mult).then_inc(dve_step, 1)
                    dve.wait_ge(dve_step, 1)
                    dve.sem_inc(dve_step, -1)
                    dve.max(keys[:, :], key2[:, :]).then_inc(dve_step, 1)
                    dve.wait_ge(dve_step, 1)
                    dve.sem_inc(dve_step, -1)
                    dve.tensor_scalar(miss[:, :], keys[:, :], 0.0, trash[:, :], ALU.is_equal, ALU.mult).then_inc(dve_step, 1)
                    dve.wait_ge(dve_step, 1)
                    dve.sem_inc(dve_step, -1)
                    dve.wait_ge(pairs_free, 1)
                    dve.sem_inc(pairs_free, -1)
                    dve.scalar_tensor_tensor(slots[:, :], miss[:, :], -1.0, keys[:, :], ALU.add, ALU.add)
                    dve.tensor_copy(pair[:, :, 0], tok_f[:, :].to_broadcast([P, 8]))
                    for k in range(8):
                        a = dve.scalar_tensor_tensor(junk[:, k, :], key2[:, :], keys[:, k:k + 1], wsel[:, :], ALU.is_equal,
                                                     ALU.mult, accum_out=pair[:, k, 1:2].bitcast(F32))
                    a.then_inc(dve_step, 1)
                    dve.wait_ge(dve_step, 1)
                    dve.sem_inc(dve_step, -1)
                    dve.tensor_scalar(tok_f[:, :], tok_f[:, :], float(T), None, ALU.add).then_inc(pairs_ready, 1)

                def step(ab, cd, pairs, ahead):
                    if cd:
                        stats(2, x2[:, :])
                    if pairs:
                        take_places()
                    if cd:
                        norm(2, x2[:, :], qn[:, :], qn_ready)
                    if ab:
                        q_copy()
                    if ahead:
                        key_stats()
                    if pairs:
                        make_pairs()
                    if ahead:
                        key_norm()
                    if cd:
                        gate_sums()
                        decayed_scores((0, 1))
                    if ahead:
                        wkv_terms()
                        wkv_scans()
                    if cd:
                        decayed_scores((2, 3))
                    if ab:
                        row_max(0)
                        row_max(1)
                    if ahead:
                        wkv_ratio()
                    if cd:
                        normalize_heads()
                    if ab:
                        row_max(2)
                    if cd:
                        head_mean()
                    if ab:
                        pT_copy(0)
                        row_max(3)
                    if cd:
                        head_var()
                        head_norm()
                    if ab:
                        pT_copy(2)
                    if ahead:
                        first_residual()
                    if cd:
                        third_stats()
                    if ahead:
                        norm(1, x1n[:, :], xn[:, :], xn_ready)
                    if cd:
                        third_norm()
                    if ab:
                        divide_by_row_sums()
                    if cd:
                        router_max()
                        choose()
                    if ab:
                        add_attention()
                    if ahead:
                        dve.sem_inc(x1_go, 1)

                wkv_terms()
                wkv_scans()
                wkv_ratio()
                first_residual()
                norm(1, x1n[:, :], xn[:, :], xn_ready)
                dve.sem_inc(x1_go, 1)
                step(True, False, False, True)
                step(True, True, False, True)
                with dve.Fori(2, nb - 1):
                    step(True, True, True, True)
                step(True, True, True, False)
                step(False, True, True, False)
                take_places()
                make_pairs()
                dve.sem_inc(sel_ready, 1)
                dve.wait_ge(cnt_ps, 1)
                dve.sem_inc(cnt_ps, -1)
                dve.tensor_scalar(cntf[:, :], ps[:, 7, 0:E], float(CAP), 1.0, ALU.min, ALU.max).then_inc(dve_step, 1)
                dve.wait_ge(dve_step, 1)
                dve.sem_inc(dve_step, -1)
                dve.tensor_copy(counts[:, :], cntf[:, :]).then_inc(dve_step, 1)
                dve.wait_ge(dve_step, 1)
                dve.sem_inc(dve_step, -1)
                dve.wait_ge(zn_stored, 16)
                dve.sem_inc(zn_stored, -16)
                dve.wait_ge(pairs_free, 1)
                dve.sem_inc(pairs_free, -1)

        with ExitStack() as ctx:
            def sb(name, shape, dt=F32):
                return ctx.enter_context(nc.sbuf_tensor(name, shape, dt))

            NGRP = CAP // GROUP
            USUAL = NGRP // 2 + 1
            ident = sb("ident2", [P, P])
            zero_i = sb("zero_i", [P, P])
            wst = sb("wst", [P, KC, 2 * INTER])
            wdst = sb("wdst", [P, 2, D])
            wh = sb("wh", [P, 2, KC, 2 * INTER], F16)
            wl = sb("wl", [P, 2, KC, 2 * INTER], F16)
            dh = sb("dh", [P, 2, 2, D], F16)
            dl = sb("dl", [P, 2, 2, D], F16)
            slot_t = sb("slot_t", [P, COLS, 2], U32)
            m_in = sb("m_in", [P, 2, 2], U32)
            m_a = sb("m_a", [P, 2, 2], U32)
            m_b = sb("m_b", [P, 2, 2], U32)
            m_add = sb("m_add", [P, 2, 2], U32)
            xg = sb("xg", [P, 2, D])
            xh = sb("xh", [P, KC, GROUP], F16)
            xl = sb("xl", [P, KC, GROUP], F16)
            s1 = sb("s1", [P, GROUP])
            s2 = sb("s2", [I2, GROUP])
            h1 = sb("h1", [P, GROUP])
            h2 = sb("h2", [I2, GROUP])
            hh1 = sb("hh1", [P, GROUP], F16)
            hx2 = sb("hx2", [P, GROUP], F16)
            hl1 = sb("hl1", [P, GROUP], F16)
            y = sb("y", [P, 2, D])
            w_loaded = sem("w_loaded")
            w_staged = sem("w_staged")
            hi_ready = sem("hi_ready")
            hi_down_ready = sem("hi_down_ready")
            slots_loaded = sem("slots_loaded")
            wh_ready0 = sem("wh_ready0")
            wh_ready1 = sem("wh_ready1")
            meta_ready = sem("meta_ready")
            rows_landed = sem("rows_landed")
            rows_ready = sem("rows_ready")
            rows_free = sem("rows_free")
            rows_ps = sem("rows_ps")
            xh_ready = sem("xh_ready")
            xh_ready_pe = sem("xh_ready_pe")
            xl_ready = sem("xl_ready")
            gate2_ps = sem("gate2_ps")
            gate_ps = sem("gate_ps")
            up_ps = sem("up_ps")
            s2_ready = sem("s2_ready")
            s_ready = sem("s_ready")
            hh_ready = sem("hh_ready")
            hl_ready = sem("hl_ready")
            y_ps = sem("y_ps")
            wy_ready = sem("wy_ready")
            added = sem("added")
            copied = sem("copied")
            m_free = sem("m_free")
            id_ready = sem("id_ready")
            all_added = sem("all_added")
            wh_ready = (wh_ready0, wh_ready1)
            block2 = ctx.enter_context(nc.Block())

            def pairs_of_experts(eng, expert):
                with eng.Fori(0, ne // 2 - 1) as i:
                    for j in range(2):
                        expert(2 * i + j, j, True)
                for j in range(2):
                    expert(ne - 2 + j, j, j == 0)

            def other_groups(eng, e, group):
                n = eng.value_load(counts[0:1, bass.ds(e, 1)], min_val=1, max_val=CAP)
                with eng.Fori(1, USUAL) as g:
                    with eng.If(n > g * GROUP):
                        group(g)
                with eng.If(n > USUAL * GROUP):
                    with eng.Fori(USUAL, NGRP) as g:
                        with eng.If(n > g * GROUP):
                            group(g)

            @block2.sync
            def _(sp):
                def load(e):
                    for src, c1_, c2_ in ((w_gate, 0, 2 * P), (w_up, P, 2 * P + I2)):
                        v_ = src[bass.ds(e, 1)].rearrange("a (k p) n -> p (a k) n", p=P)
                        sp.dma_start(wst[:, :, c1_:c1_ + P], v_[:, :, 0:P]).then_inc(w_loaded, 16)
                        sp.dma_start(wst[:, :, c2_:c2_ + I2], v_[:, :, P:INTER]).then_inc(w_loaded, 16)
                    v_ = w_down[bass.ds(e, 1)].rearrange("a i d -> (a i) d")
                    sp.dma_start(wdst[:, 0, :], v_[0:P, :]).then_inc(w_loaded, 16)
                    sp.dma_start(wdst[0:I2, 1, :], v_[P:INTER, :]).then_inc(w_loaded, 16)

                sp.dma_start(slot_t[:, :, :], slot_d[0:SLOTS, :].rearrange("(p s) c -> p s c", p=P)).then_inc(slots_loaded, 16)
                load(0)
                with sp.Fori(1, ne) as e:
                    sp.wait_ge(w_staged, 1)
                    sp.sem_inc(w_staged, -1)
                    load(e)
                sp.wait_ge(w_staged, 1)
                sp.sem_inc(w_staged, -1)
                sp.wait_ge(all_added, 1)
                sp.sem_inc(all_added, -1)
                sp.dma_start(out.rearrange("b t d -> (b t) d"), acc_d[0:TOK, :]).then_inc(copied, 16)
                sp.wait_ge(copied, 16)

            @block2.gpsimd
            def _(pool):
                n_added = pool.alloc_register("n_added")
                n_rows = pool.alloc_register("n_rows")
                pool.reg_mov(n_added, 0)
                pool.reg_mov(n_rows, 0)

                def shift():
                    pool.tensor_copy(m_add[:, :, :], m_b[:, :, :]).then_inc(pool_step, 1)
                    pool.wait_ge(pool_step, 1)
                    pool.sem_inc(pool_step, -1)
                    pool.sem_inc(meta_ready, 1)
                    pool.tensor_copy(m_b[:, :, :], m_a[:, :, :]).then_inc(pool_step, 1)
                    pool.wait_ge(pool_step, 1)
                    pool.sem_inc(pool_step, -1)

                def add_rows():
                    pool.wait_ge(wy_ready, 1)
                    pool.sem_inc(wy_ready, -1)
                    pool.reg_add(n_added, n_added, 32)
                    for h in range(2):
                        pool.indirect_dma_start(out=acc_d[:, :], out_offset=bass.IndirectOffsetOnAxis(ap=m_add[:, h, 0:1], axis=0),
                                                in_=y[:, h, :], in_offset=None, compute_op=ALU.add).then_inc(added, 16)

                def group(col):
                    pool.wait_ge(rows_free, 1)
                    pool.sem_inc(rows_free, -1)
                    pool.tensor_copy(m_in[:, :, :], slot_t[:, bass.ds(col, 2), :]).then_inc(pool_step, 1)
                    pool.wait_ge(pool_step, 1)
                    pool.sem_inc(pool_step, -1)
                    added_ = pool.snap(n_added, min_val=32, max_val=32 * (E * NGRP + 3))
                    pool.reg_add(n_rows, n_rows, 32)
                    landed = pool.snap(n_rows, min_val=32, max_val=32 * E * NGRP)
                    for h in range(2):
                        pool.indirect_dma_start(out=xg[:, h, :], out_offset=None, in_=z_d[:, :],
                                                in_offset=bass.IndirectOffsetOnAxis(ap=m_in[:, h, 0:1], axis=0)).then_inc(rows_landed, 16)
                    pool.wait_ge(added, added_)
                    pool.sem_inc(m_free, 1)
                    pool.wait_ge(m_free, 1)
                    pool.sem_inc(m_free, -1)
                    shift()
                    pool.tensor_copy(m_a[:, :, :], m_in[:, :, :]).then_inc(pool_step, 1)
                    pool.wait_ge(pool_step, 1)
                    pool.sem_inc(pool_step, -1)
                    pool.wait_ge(rows_landed, landed)
                    pool.sem_inc(rows_ready, 1)
                    add_rows()

                def expert(e, j, more):
                    group(e * (CAP // P))
                    other_groups(pool, e, lambda g: group(e * (CAP // P) + g * 2))

                pool.memset(zero_i[:, :], 0.0)
                for t_ in (hh1, hx2, hl1):
                    pool.memset(t_[:, :], 0.0)
                pool.memset(dh[:, 1, :, :], 0.0)
                pool.memset(dl[:, 1, :, :], 0.0)
                pool.memset(y[:, :, :], 0.0)
                for t_ in (m_a, m_b, m_add):
                    pool.memset(t_[:, :, :], 0).then_inc(pool_step, 1)
                    pool.wait_ge(pool_step, 1)
                    pool.sem_inc(pool_step, -1)
                    pool.iota(t_[:, :, 0].bitcast(mybir.dt.int32), pattern=[[P, 2]], base=TOK, channel_multiplier=1).then_inc(pool_step, 1)
                    pool.wait_ge(pool_step, 1)
                    pool.sem_inc(pool_step, -1)
                pool.affine_select(out=ident[:, :], in_=zero_i[:, :], compare_op=ALU.not_equal, fill=1.0, base=0,
                                   pattern=[[-1, P]], channel_multiplier=1).then_inc(pool_step, 1)
                pool.wait_ge(pool_step, 1)
                pool.sem_inc(pool_step, -1)
                pool.sem_inc(id_ready, 1)
                pool.sem_inc(rows_free, 1)
                pool.sem_inc(wy_ready, 1)
                pool.wait_ge(slots_loaded, 16)
                pool.sem_inc(slots_loaded, -16)
                add_rows()
                pool.sem_inc(wy_ready, 1)
                pairs_of_experts(pool, expert)
                for last in range(2):
                    added_ = pool.snap(n_added, min_val=32, max_val=32 * (E * NGRP + 3))
                    pool.wait_ge(added, added_)
                    pool.sem_inc(m_free, 1)
                    pool.wait_ge(m_free, 1)
                    pool.sem_inc(m_free, -1)
                    shift()
                    add_rows()
                added_ = pool.snap(n_added, min_val=32, max_val=32 * (E * NGRP + 3))
                pool.wait_ge(added, added_)
                pool.sem_inc(all_added, 1)

            @block2.tensor
            def _(pe):
                def turn():
                    pe.wait_ge(rows_ready, 1)
                    pe.sem_inc(rows_ready, -1)
                    for h in range(2):
                        for k in range(KC):
                            m = pe.transpose(ps[:, h, k * P:(k + 1) * P], xg[:, h, k * P:(k + 1) * P], ident[:, :])
                    m.then_inc(rows_ps, 1)

                def down(j):
                    pe.wait_ge(hh_ready, 2)
                    pe.sem_inc(hh_ready, -2)
                    for h in range(2):
                        o, t = ps[:, 5 + h, :], slice(h * P, h * P + P)
                        pe.matmul(o, hh1[:, t], dh[:, j, 0, :], start=True, stop=False)
                        pe.matmul(o, hh1[:, t], dl[:, j, 0, :], start=False, stop=False)
                        pe.matmul(o, hx2[0:I2, t], dl[0:I2, j, 1, :], start=False, stop=False)
                    pe.wait_ge(hl_ready, 2)
                    pe.sem_inc(hl_ready, -2)
                    for h in range(2):
                        o, t = ps[:, 5 + h, :], slice(h * P, h * P + P)
                        pe.matmul(o, hl1[:, t], dh[:, j, 0, :], start=False, stop=False)
                        pe.matmul(o, hx2[:, t], dh[:, j, 1, :], start=False, stop=True).then_inc(y_ps, 1)

                def gate_up(j):
                    pe.wait_ge(xh_ready_pe, 1)
                    pe.sem_inc(xh_ready_pe, -1)
                    for c0, dst, signal in ((2 * P, 3, gate2_ps), (0, 2, gate_ps), (P, 4, up_ps)):
                        for k in range(KC):
                            pe.matmul(ps[:, dst, 0:GROUP], wh[:, j, k, c0:c0 + P], xh[:, k, :], start=(k == 0), stop=False)
                            pe.matmul(ps[:, dst, 0:GROUP], wl[:, j, k, c0:c0 + P], xh[:, k, :], start=False, stop=False)
                        if dst == 3:
                            pe.wait_ge(xl_ready, 1)
                            pe.sem_inc(xl_ready, -1)
                        for k in range(KC):
                            m = pe.matmul(ps[:, dst, 0:GROUP], wh[:, j, k, c0:c0 + P], xl[:, k, :], start=False,
                                          stop=(k == KC - 1))
                        m.then_inc(signal, 1)

                def expert(e, j, more):
                    turn()
                    down(1 - j)
                    pe.wait_ge(wh_ready[j], 1)
                    pe.sem_inc(wh_ready[j], -1)
                    gate_up(j)

                    def group(g):
                        turn()
                        down(j)
                        gate_up(j)
                    other_groups(pe, e, group)

                pe.wait_ge(id_ready, 1)
                pe.sem_inc(id_ready, -1)
                pe.sem_inc(hh_ready, 2)
                pe.sem_inc(hl_ready, 2)
                pairs_of_experts(pe, expert)
                down(1)

            @block2.scalar
            def _(act):
                def split_gate_up(j):
                    act.wait_ge(w_loaded, 96)
                    act.sem_inc(w_loaded, -96)
                    act.activation(wh[:, j, :, :], wst[:, :, :], ACT.Copy, scale=WSC).then_inc(hi_ready, 1)

                def split_down(j):
                    act.activation(dh[:, j, 0, :], wdst[:, 0, :], ACT.Copy, scale=WSC)
                    act.activation(dh[I2:2 * I2, j, 1, :], wdst[0:I2, 1, :], ACT.Copy, scale=WSC)
                    act.activation(dh[0:I2, j, 1, :], wdst[0:I2, 1, :], ACT.Copy, scale=WSC).then_inc(hi_down_ready, 1)

                def weigh():
                    act.wait_ge(meta_ready, 1)
                    act.sem_inc(meta_ready, -1)
                    for h in range(2):
                        act.wait_ge(y_ps, 1)
                        act.sem_inc(y_ps, -1)
                        a = act.activation(y[:, h, :], ps[:, 5 + h, :], ACT.Copy, scale=m_add[:, h, 1:2].bitcast(F32))
                    a.then_inc(wy_ready, 1)

                def group(g=0, split=None):
                    act.wait_ge(rows_ps, 1)
                    act.sem_inc(rows_ps, -1)
                    act.sem_inc(rows_free, 1)
                    for h in range(2):
                        a = act.activation(xh[:, :, h * P:(h + 1) * P], ps[:, h, :].rearrange("p (k t) -> p k t", k=KC), ACT.Copy)
                    a.then_inc(xh_ready, 1)
                    if split is not None:
                        split_gate_up(split)
                    weigh()
                    if split is not None:
                        split_down(split)
                    act.wait_ge(gate2_ps, 1)
                    act.sem_inc(gate2_ps, -1)
                    act.activation(s2[:, :], ps[0:I2, 3, 0:GROUP], ACT.Silu, scale=1.0 / WSC).then_inc(s2_ready, 1)
                    act.wait_ge(gate_ps, 1)
                    act.sem_inc(gate_ps, -1)
                    act.activation(s1[:, :], ps[:, 2, 0:GROUP], ACT.Silu, scale=1.0 / WSC).then_inc(s_ready, 1)

                def expert(e, j, more):
                    group(split=(1 - j if more else None))
                    other_groups(act, e, group)

                split_gate_up(0)
                split_down(0)
                act.wait_ge(meta_ready, 1)
                act.sem_inc(meta_ready, -1)
                pairs_of_experts(act, expert)
                weigh()

            @block2.vector
            def _(dve):

                def split_low(j):
                    dve.wait_ge(hi_ready, 1)
                    dve.sem_inc(hi_ready, -1)
                    dve.scalar_tensor_tensor(wl[:, j, :, :], wst[:, :, :], WSC, wh[:, j, :, :], ALU.mult, ALU.subtract)
                    dve.wait_ge(hi_down_ready, 1)
                    dve.sem_inc(hi_down_ready, -1)
                    dve.scalar_tensor_tensor(dl[:, j, 0, :], wdst[:, 0, :], WSC, dh[:, j, 0, :], ALU.mult, ALU.subtract)
                    dve.scalar_tensor_tensor(dl[0:I2, j, 1, :], wdst[0:I2, 1, :], WSC, dh[0:I2, j, 1, :],
                                             ALU.mult, ALU.subtract).then_inc(dve_step, 1)
                    dve.wait_ge(dve_step, 1)
                    dve.sem_inc(dve_step, -1)
                    dve.sem_inc(wh_ready[j], 1)
                    dve.sem_inc(w_staged, 1)

                def gated(up, s, hi, full, low):
                    dve.scalar_tensor_tensor(hi, up, 1.0 / WSC, s, ALU.mult, ALU.mult).then_inc(hh_ready, 1)
                    dve.scalar_tensor_tensor(full, up, 1.0 / WSC, s, ALU.mult, ALU.mult).then_inc(dve_step, 1)
                    dve.wait_ge(dve_step, 1)
                    dve.sem_inc(dve_step, -1)
                    dve.tensor_tensor(low, full, hi, ALU.subtract).then_inc(hl_ready, 1)

                def group(g=0, split=None):
                    dve.wait_ge(xh_ready, 1)
                    dve.sem_inc(xh_ready, -1)
                    dve.sem_inc(xh_ready_pe, 1)
                    for h in range(2):
                        a = dve.tensor_tensor(xl[:, :, h * P:(h + 1) * P], ps[:, h, :].rearrange("p (k t) -> p k t", k=KC),
                                              xh[:, :, h * P:(h + 1) * P], ALU.subtract)
                    a.then_inc(xl_ready, 1)
                    if split is not None:
                        split_low(split)
                    dve.wait_ge(s2_ready, 1)
                    dve.sem_inc(s2_ready, -1)
                    gated(ps[I2:2 * I2, 3, 0:GROUP], s2[:, :], hx2[0:I2, :], h2[:, :], hx2[I2:2 * I2, :])
                    dve.wait_ge(s_ready, 1)
                    dve.sem_inc(s_ready, -1)
                    dve.wait_ge(up_ps, 1)
                    dve.sem_inc(up_ps, -1)
                    gated(ps[:, 4, 0:GROUP], s1[:, :], hh1[:, :], h1[:, :], hl1[:, :])

                def expert(e, j, more):
                    group(split=(1 - j if more else None))
                    other_groups(dve, e, group)

                split_low(0)
                pairs_of_experts(dve, expert)


_INS = ['x', 'ctx_2048', 'L0_xattn_w', 'L0_xattn_u', 'L0_ffn_Wa', 'L0_ffn_Wp', 'L0_ffn_w_std', 'L0_ffn_w_rec',
        'L1_xattn_Wi', 'L1_xattn_bi', 'L1_xattn_Wf', 'L1_xattn_bf', 'L1_xattn_ln_scale', 'L1_ffn_gate_w',
        'L1_ffn_w_gate', 'L1_ffn_w_up', 'L1_ffn_w_down']


def kernel(**inputs):
    import numpy as _np
    import concourse.bacc as _bacc
    from concourse import mybir as _mybir
    from concourse.bass_utils import run_bass_kernel_spmd as _run

    nc = _bacc.Bacc("TRN2", target_bir_lowering=False, num_devices=1)
    arrays, args = {}, []
    for name in _INS:
        a = _np.ascontiguousarray(inputs[name])
        arrays[f"in_{name}_dram"] = a
        args.append(nc.dram_tensor(f"in_{name}_dram", a.shape, _mybir.dt.from_np(a.dtype), kind="ExternalInput").ap())
    out = nc.dram_tensor("out_0_dram", (32, 128, 512), _mybir.dt.float32, kind="ExternalOutput").ap()
    build(nc, *args, out)
    r = _run(nc, [arrays], core_ids=[0])
    return r.results[0]["out_0_dram"]
```
